# Optimizing a Trainium2 kernel written in Bass

```python
import numpy as np
import jax
import jax.numpy as jnp

def _softmax(x, axis=-1):
    return jax.nn.softmax(x, axis=axis)

def _gelu(x):
    return jax.nn.gelu(x, approximate=True)

def _silu(x):
    return jax.nn.silu(x)

def _sigmoid(x):
    return jax.nn.sigmoid(x)

def _layernorm(x, axis=-1, eps=1e-05):
    m = jnp.mean(x, axis=axis, keepdims=True)
    v = jnp.var(x, axis=axis, keepdims=True)
    return (x - m) / jnp.sqrt(v + eps)

def _scatter_add(tgt, idx, src, axis=0):
    return tgt.at[idx].add(src)

def _segment_sum(src, seg, n):
    return jax.ops.segment_sum(src, seg, n)
kernel_name = 'mk_decoder_preln_d2_seqx_r4_149636'

def setup_inputs(seed: int=0):
    np.random.seed(seed)
    _w = jnp.asarray

    def _rec_inputs():
        import jax
        import jax.numpy as jnp
        _rk = jax.random.key(seed)
        x = -0.0002928 + 1 * jax.random.normal(jax.random.fold_in(_rk, 1), (4, 512, 256), jnp.float32)
        _lenS = 512 - jax.random.randint(jax.random.fold_in(_rk, 7), (4,), 0, max(1, 512 // 4) + 1, jnp.int32)
        _lenS2 = 1024 - jax.random.randint(jax.random.fold_in(_rk, 8), (4,), 0, max(1, 1024 // 4) + 1, jnp.int32)
        _ctx_1024P = jax.random.normal(jax.random.fold_in(_rk, 11), (4, 16, 256), jnp.float32)
        _ctx_1024c = jax.random.dirichlet(jax.random.fold_in(_rk, 511), 0.3 * jnp.ones((16,), jnp.float32), (4, 1024))
        _ctx_1024t = jnp.einsum('bsk,bkd->bsd', _ctx_1024c, _ctx_1024P)
        _ctx_1024t = _ctx_1024t * jax.lax.rsqrt(jnp.mean(jnp.square(_ctx_1024t)) + 1e-12) * 0.953939
        ctx_1024 = -1.39393e-06 + 0.999914 * (_ctx_1024t + 0.3 * jax.random.normal(jax.random.fold_in(_rk, 611), (4, 1024, 256), jnp.float32))
        _validS = jnp.arange(512)[None, :] < _lenS[:, None]
        _validS2 = jnp.arange(1024)[None, :] < _lenS2[:, None]
        _causal = jnp.tril(jnp.ones((512, 512), dtype=bool))
        mask_1x1xSxS2_ik0 = jnp.where(jnp.broadcast_to(_validS2[0:1, None, None, :], (1, 1, 512, 1024)), 0, 1).astype(jnp.int32)
        return (x, ctx_1024, mask_1x1xSxS2_ik0)
    x, ctx_1024, mask_1x1xSxS2_ik0 = _rec_inputs()

    def _L0_attn_setup():
        import jax, jax.numpy as jnp
        import numpy as np
        import math
        B, L, H, D, HID = (2, 256, 16, 64, 256)

        def _rope_tables(seq_len, dim):
            inv_freq = 1.0 / 10000.0 ** (jnp.arange(0, dim, 2, dtype=jnp.float32) / dim)
            t = jnp.arange(seq_len, dtype=jnp.float32)
            freqs = jnp.outer(t, inv_freq)
            emb = jnp.concatenate([freqs, freqs], -1)
            return (jnp.cos(emb), jnp.sin(emb))

        def _rotate_half(x):
            x1, x2 = jnp.split(x, 2, axis=-1)
            return jnp.concatenate([-x2, x1], axis=-1)

        def _apply_rope(x, cos, sin):
            return x * cos + _rotate_half(x) * sin

        def _forward(x, w_qkv, w_o, log_p, log_a, w1, b1, w2, b2):
            Bx, Lx, _ = x.shape
            qkv = jnp.dot(x, w_qkv).reshape(Bx, Lx, 3, H, D)
            qkv = jnp.transpose(qkv, (2, 0, 3, 1, 4))
            q, k, v = (qkv[0], qkv[1], qkv[2])
            cos, sin = _rope_tables(Lx, D)
            cos, sin = (cos[None, None], sin[None, None])
            q = _apply_rope(q, cos, sin)
            k = _apply_rope(k, cos, sin)
            scale = 1.0 / math.sqrt(D)
            scores = jnp.einsum('bhid,bhjd->bhij', q, k) * scale
            pos = jnp.arange(Lx, dtype=jnp.float32)
            dist = jnp.abs(pos[None, :] - pos[:, None])
            p = jax.nn.softplus(log_p)
            a = jax.nn.softplus(log_a)
            kerple = -p * jnp.log1p(a * dist[None])
            attn_t = jnp.transpose(scores, (0, 2, 3, 1))
            kerple_t = jnp.broadcast_to(jnp.transpose(kerple, (1, 2, 0))[None], attn_t.shape)
            combined = jnp.concatenate([attn_t, kerple_t], axis=-1)
            hdn = jax.nn.gelu(jnp.dot(combined, w1) + b1, approximate=False)
            refined = jnp.dot(hdn, w2) + b2
            refined = jnp.transpose(refined, (0, 3, 1, 2))
            scores = scores + kerple[None] + refined
            causal = jnp.tril(jnp.ones((Lx, Lx), dtype=bool))
            scores = jnp.where(causal[None, None], scores, -jnp.inf)
            weights = jax.nn.softmax(scores, axis=-1)
            out = jnp.einsum('bhij,bhjd->bhid', weights, v)
            out = jnp.transpose(out, (0, 2, 1, 3)).reshape(Bx, Lx, H * D)
            return jnp.dot(out, w_o)
        key = jax.random.key(seed)
        ks = jax.random.split(key, 8)
        s = 0.02
        return {'x': jax.random.normal(ks[0], (B, L, HID), jnp.float32), 'w_qkv': jax.random.normal(ks[1], (HID, 3 * H * D), jnp.float32) * s, 'w_o': jax.random.normal(ks[2], (H * D, HID), jnp.float32) * s, 'log_p': jax.random.normal(ks[3], (H, 1, 1), jnp.float32) * 0.02, 'log_a': jax.random.normal(ks[4], (H, 1, 1), jnp.float32) * 0.02, 'w1': jax.random.normal(ks[5], (2 * H, 2 * H), jnp.float32) * s, 'b1': jnp.zeros((2 * H,), jnp.float32), 'w2': jax.random.normal(ks[6], (2 * H, H), jnp.float32) * s, 'b2': jnp.zeros((H,), jnp.float32)}
    _L0_attn_all = _L0_attn_setup()
    _L0_attn_in = {k: v for k, v in _L0_attn_all.items() if k in ('w_qkv', 'w_o', 'log_p', 'log_a', 'w1', 'b1', 'w2', 'b2')}
    del _L0_attn_all

    def _L0_xattn_setup():
        import jax, jax.numpy as jnp
        import numpy as np
        DIM = 256
        NUM_HEADS = 16
        HEAD_DIM = DIM // NUM_HEADS
        SCALE = HEAD_DIM ** (-0.5)
        key = jax.random.key(seed)
        ks = jax.random.split(key, 8)
        B, QL, KL = (2, 512, 512)
        s = DIM ** (-0.5)
        return {'q': jax.random.normal(ks[0], (B, QL, DIM), jnp.float32), 'k': jax.random.normal(ks[1], (B, KL, DIM), jnp.float32), 'v': jax.random.normal(ks[2], (B, KL, DIM), jnp.float32), 'Wq': jax.random.normal(ks[3], (DIM, DIM), jnp.float32) * s, 'Wk': jax.random.normal(ks[4], (DIM, DIM), jnp.float32) * s, 'Wv': jax.random.normal(ks[5], (DIM, DIM), jnp.float32) * s, 'Wo': jax.random.normal(ks[6], (DIM, DIM), jnp.float32) * s, 'bo': jax.random.normal(ks[7], (DIM,), jnp.float32) * 0.02}
    _L0_xattn_all = _L0_xattn_setup()
    _L0_xattn_in = {k: v for k, v in _L0_xattn_all.items() if k in ('Wq', 'Wk', 'Wv', 'Wo', 'bo')}
    del _L0_xattn_all

    def _L0_ffn_setup():
        import jax, jax.numpy as jnp
        import numpy as np
        B, T, D = (4, 512, 256)
        H, DH, E, SEL = (8, 64, 5, 2)

        def _topk_mask(logits, k):
            _, idx = jax.lax.top_k(logits, k)
            return jnp.sum(jax.nn.one_hot(idx, logits.shape[-1], dtype=logits.dtype), axis=-2)
        key = jax.random.key(seed)
        ks = jax.random.split(key, 7)
        s = 0.02
        x = jax.random.normal(ks[0], (B, T, D), dtype=jnp.float32)
        Wq = jax.random.normal(ks[1], (D, H * DH), dtype=jnp.float32) * s
        Wk = jax.random.normal(ks[2], (D, H * DH), dtype=jnp.float32) * s
        Ws = jax.random.normal(ks[3], (D, H * E), dtype=jnp.float32) * s
        Wd = jax.random.normal(ks[4], (D, H * E), dtype=jnp.float32) * s
        Wv = jax.random.normal(ks[5], (E, D, DH), dtype=jnp.float32) * s
        Wo = jax.random.normal(ks[6], (E, DH, D), dtype=jnp.float32) * s
        return {'x': x, 'Wq': Wq, 'Wk': Wk, 'Ws': Ws, 'Wd': Wd, 'Wv': Wv, 'Wo': Wo}
    _L0_ffn_all = _L0_ffn_setup()
    _L0_ffn_in = {k: v for k, v in _L0_ffn_all.items() if k in ('Wq', 'Wk', 'Ws', 'Wd', 'Wv', 'Wo')}
    del _L0_ffn_all

    def _L1_attn_setup():
        import jax, jax.numpy as jnp
        import numpy as np
        D_MODEL = 256
        NUM_HEADS = 16
        HEAD_DIM = D_MODEL // NUM_HEADS
        ROPE_THETA = 10000.0

        def apply_rope(x):
            S, d_k = (x.shape[-2], x.shape[-1])
            inv_freq = ROPE_THETA ** (jnp.arange(0, d_k, 2, dtype=jnp.float32) / d_k)
            ang = jnp.arange(S, dtype=jnp.float32)[:, None] / inv_freq[None, :]
            cos, sin = (jnp.cos(ang), jnp.sin(ang))
            xp = x.reshape(x.shape[:-1] + (d_k // 2, 2))
            x0, x1 = (xp[..., 0], xp[..., 1])
            out = jnp.stack([x0 * cos - x1 * sin, x0 * sin + x1 * cos], axis=-1)
            return out.reshape(x.shape)
        key = jax.random.key(seed)
        k1, k2, k3 = jax.random.split(key, 3)
        B, S = (2, 512)
        std = 2.0 / (D_MODEL + 3 * D_MODEL)
        std_o = 2.0 / (D_MODEL + D_MODEL)
        return {'x': jax.random.normal(k1, (B, S, D_MODEL), dtype=jnp.float32), 'W_qkv': jax.random.normal(k2, (3 * D_MODEL, D_MODEL), dtype=jnp.float32) * std, 'W_o': jax.random.normal(k3, (D_MODEL, D_MODEL), dtype=jnp.float32) * std_o}
    _L1_attn_all = _L1_attn_setup()
    _L1_attn_in = {k: v for k, v in _L1_attn_all.items() if k in ('W_qkv', 'W_o')}
    del _L1_attn_all

    def _L1_xattn_setup():
        import jax, jax.numpy as jnp
        import numpy as np
        D_MODEL = 256
        H = 16
        D_K = D_MODEL // H
        B, S = (4, 512)
        key = jax.random.key(seed)
        ks = jax.random.split(key, 12)
        std = 1.0 / np.sqrt(D_MODEL)
        inp = {'q': jax.random.normal(ks[0], (B, S, D_MODEL), dtype=jnp.float32), 'k': jax.random.normal(ks[1], (B, S, D_MODEL), dtype=jnp.float32), 'v': jax.random.normal(ks[2], (B, S, D_MODEL), dtype=jnp.float32), 'mask': jnp.tril(jnp.ones((S, S), dtype=jnp.int32))[None, None], 'w_q': jax.random.normal(ks[3], (D_MODEL, D_MODEL), dtype=jnp.float32) * std, 'b_q': jax.random.normal(ks[4], (D_MODEL,), dtype=jnp.float32) * std, 'w_k': jax.random.normal(ks[5], (D_MODEL, D_MODEL), dtype=jnp.float32) * std, 'b_k': jax.random.normal(ks[6], (D_MODEL,), dtype=jnp.float32) * std, 'w_v': jax.random.normal(ks[7], (D_MODEL, D_MODEL), dtype=jnp.float32) * std, 'b_v': jax.random.normal(ks[8], (D_MODEL,), dtype=jnp.float32) * std, 'w_o': jax.random.normal(ks[9], (D_MODEL, D_MODEL), dtype=jnp.float32) * std, 'b_o': jax.random.normal(ks[10], (D_MODEL,), dtype=jnp.float32) * std}
        return inp
    _L1_xattn_all = _L1_xattn_setup()
    _L1_xattn_in = {k: v for k, v in _L1_xattn_all.items() if k in ('w_q', 'b_q', 'w_k', 'b_k', 'w_v', 'b_v', 'w_o', 'b_o')}
    del _L1_xattn_all

    def _L1_ffn_setup():
        import jax, jax.numpy as jnp
        import numpy as np
        E = 32
        H = 256
        I = 128
        G = 8
        TKG = 4
        TOPK = 8
        NSH = 2
        SCALE = 2.5
        key = jax.random.key(seed)
        ks = jax.random.split(key, 10)
        s = 0.02
        return {'hidden_states': jax.random.normal(ks[0], (2, 256, H), jnp.float32), 'gate_w': jax.random.normal(ks[1], (E, H), jnp.float32) * s, 'gate_bias': jax.random.normal(ks[2], (E,), jnp.float32) * s, 'w_gate': jax.random.normal(ks[3], (E, I, H), jnp.float32) * s, 'w_up': jax.random.normal(ks[4], (E, I, H), jnp.float32) * s, 'w_down': jax.random.normal(ks[5], (E, H, I), jnp.float32) * s, 'sh_gate': jax.random.normal(ks[6], (I * NSH, H), jnp.float32) * s, 'sh_up': jax.random.normal(ks[7], (I * NSH, H), jnp.float32) * s, 'sh_down': jax.random.normal(ks[8], (H, I * NSH), jnp.float32) * s}
    _L1_ffn_all = _L1_ffn_setup()
    _L1_ffn_in = {k: v for k, v in _L1_ffn_all.items() if k in ('gate_w', 'gate_bias', 'w_gate', 'w_up', 'w_down', 'sh_gate', 'sh_up', 'sh_down')}
    del _L1_ffn_all
    return {'x': x, 'ctx_1024': ctx_1024, 'mask_1x1xSxS2_ik0': mask_1x1xSxS2_ik0, 'L0_attn_w_qkv': _L0_attn_in['w_qkv'], 'L0_attn_w_o': _L0_attn_in['w_o'], 'L0_attn_log_p': _L0_attn_in['log_p'], 'L0_attn_log_a': _L0_attn_in['log_a'], 'L0_attn_w1': _L0_attn_in['w1'], 'L0_attn_b1': _L0_attn_in['b1'], 'L0_attn_w2': _L0_attn_in['w2'], 'L0_attn_b2': _L0_attn_in['b2'], 'L0_xattn_Wq': _L0_xattn_in['Wq'], 'L0_xattn_Wk': _L0_xattn_in['Wk'], 'L0_xattn_Wv': _L0_xattn_in['Wv'], 'L0_xattn_Wo': _L0_xattn_in['Wo'], 'L0_xattn_bo': _L0_xattn_in['bo'], 'L0_ffn_Wq': _L0_ffn_in['Wq'], 'L0_ffn_Wk': _L0_ffn_in['Wk'], 'L0_ffn_Ws': _L0_ffn_in['Ws'], 'L0_ffn_Wd': _L0_ffn_in['Wd'], 'L0_ffn_Wv': _L0_ffn_in['Wv'], 'L0_ffn_Wo': _L0_ffn_in['Wo'], 'L1_attn_W_qkv': _L1_attn_in['W_qkv'], 'L1_attn_W_o': _L1_attn_in['W_o'], 'L1_xattn_w_q': _L1_xattn_in['w_q'], 'L1_xattn_b_q': _L1_xattn_in['b_q'], 'L1_xattn_w_k': _L1_xattn_in['w_k'], 'L1_xattn_b_k': _L1_xattn_in['b_k'], 'L1_xattn_w_v': _L1_xattn_in['w_v'], 'L1_xattn_b_v': _L1_xattn_in['b_v'], 'L1_xattn_w_o': _L1_xattn_in['w_o'], 'L1_xattn_b_o': _L1_xattn_in['b_o'], 'L1_ffn_gate_w': _L1_ffn_in['gate_w'], 'L1_ffn_gate_bias': _L1_ffn_in['gate_bias'], 'L1_ffn_w_gate': _L1_ffn_in['w_gate'], 'L1_ffn_w_up': _L1_ffn_in['w_up'], 'L1_ffn_w_down': _L1_ffn_in['w_down'], 'L1_ffn_sh_gate': _L1_ffn_in['sh_gate'], 'L1_ffn_sh_up': _L1_ffn_in['sh_up'], 'L1_ffn_sh_down': _L1_ffn_in['sh_down']}

def reference(x, ctx_1024, mask_1x1xSxS2_ik0, L0_attn_w_qkv, L0_attn_w_o, L0_attn_log_p, L0_attn_log_a, L0_attn_w1, L0_attn_b1, L0_attn_w2, L0_attn_b2, L0_xattn_Wq, L0_xattn_Wk, L0_xattn_Wv, L0_xattn_Wo, L0_xattn_bo, L0_ffn_Wq, L0_ffn_Wk, L0_ffn_Ws, L0_ffn_Wd, L0_ffn_Wv, L0_ffn_Wo, L1_attn_W_qkv, L1_attn_W_o, L1_xattn_w_q, L1_xattn_b_q, L1_xattn_w_k, L1_xattn_b_k, L1_xattn_w_v, L1_xattn_b_v, L1_xattn_w_o, L1_xattn_b_o, L1_ffn_gate_w, L1_ffn_gate_bias, L1_ffn_w_gate, L1_ffn_w_up, L1_ffn_w_down, L1_ffn_sh_gate, L1_ffn_sh_up, L1_ffn_sh_down):
    import jax
    import jax.numpy as jnp

    def _L0_attn_ref(x, w_qkv, w_o, log_p, log_a, w1, b1, w2, b2):
        import jax, jax.numpy as jnp
        import numpy as np
        import math
        B, L, H, D, HID = (2, 256, 16, 64, 256)

        def _rope_tables(seq_len, dim):
            inv_freq = 1.0 / 10000.0 ** (jnp.arange(0, dim, 2, dtype=jnp.float32) / dim)
            t = jnp.arange(seq_len, dtype=jnp.float32)
            freqs = jnp.outer(t, inv_freq)
            emb = jnp.concatenate([freqs, freqs], -1)
            return (jnp.cos(emb), jnp.sin(emb))

        def _rotate_half(x):
            x1, x2 = jnp.split(x, 2, axis=-1)
            return jnp.concatenate([-x2, x1], axis=-1)

        def _apply_rope(x, cos, sin):
            return x * cos + _rotate_half(x) * sin

        def _forward(x, w_qkv, w_o, log_p, log_a, w1, b1, w2, b2):
            Bx, Lx, _ = x.shape
            qkv = jnp.dot(x, w_qkv).reshape(Bx, Lx, 3, H, D)
            qkv = jnp.transpose(qkv, (2, 0, 3, 1, 4))
            q, k, v = (qkv[0], qkv[1], qkv[2])
            cos, sin = _rope_tables(Lx, D)
            cos, sin = (cos[None, None], sin[None, None])
            q = _apply_rope(q, cos, sin)
            k = _apply_rope(k, cos, sin)
            scale = 1.0 / math.sqrt(D)
            scores = jnp.einsum('bhid,bhjd->bhij', q, k) * scale
            pos = jnp.arange(Lx, dtype=jnp.float32)
            dist = jnp.abs(pos[None, :] - pos[:, None])
            p = jax.nn.softplus(log_p)
            a = jax.nn.softplus(log_a)
            kerple = -p * jnp.log1p(a * dist[None])
            attn_t = jnp.transpose(scores, (0, 2, 3, 1))
            kerple_t = jnp.broadcast_to(jnp.transpose(kerple, (1, 2, 0))[None], attn_t.shape)
            combined = jnp.concatenate([attn_t, kerple_t], axis=-1)
            hdn = jax.nn.gelu(jnp.dot(combined, w1) + b1, approximate=False)
            refined = jnp.dot(hdn, w2) + b2
            refined = jnp.transpose(refined, (0, 3, 1, 2))
            scores = scores + kerple[None] + refined
            causal = jnp.tril(jnp.ones((Lx, Lx), dtype=bool))
            scores = jnp.where(causal[None, None], scores, -jnp.inf)
            weights = jax.nn.softmax(scores, axis=-1)
            out = jnp.einsum('bhij,bhjd->bhid', weights, v)
            out = jnp.transpose(out, (0, 2, 1, 3)).reshape(Bx, Lx, H * D)
            return jnp.dot(out, w_o)
        return _forward(x, w_qkv, w_o, log_p, log_a, w1, b1, w2, b2)

    def _L0_xattn_ref(q, k, v, Wq, Wk, Wv, Wo, bo):
        import jax, jax.numpy as jnp
        import numpy as np
        DIM = 256
        NUM_HEADS = 16
        HEAD_DIM = DIM // NUM_HEADS
        SCALE = HEAD_DIM ** (-0.5)
        B, QL, _ = q.shape
        KL = k.shape[1]
        qh = (q @ Wq.T).reshape(B, QL, NUM_HEADS, HEAD_DIM)
        kh = (k @ Wk.T).reshape(B, KL, NUM_HEADS, HEAD_DIM)
        vh = (v @ Wv.T).reshape(B, KL, NUM_HEADS, HEAD_DIM)
        attn = jnp.einsum('bnhc,bmhc->bhnm', qh, kh) * SCALE
        attn = jax.nn.softmax(attn, axis=-1)
        out = jnp.einsum('bhnm,bmhc->bnhc', attn, vh).reshape(B, QL, DIM)
        return out @ Wo.T + bo

    def _L0_ffn_ref(x, Wq, Wk, Ws, Wd, Wv, Wo):
        import jax, jax.numpy as jnp
        import numpy as np
        B, T, D = (4, 512, 256)
        H, DH, E, SEL = (8, 64, 5, 2)

        def _topk_mask(logits, k):
            _, idx = jax.lax.top_k(logits, k)
            return jnp.sum(jax.nn.one_hot(idx, logits.shape[-1], dtype=logits.dtype), axis=-2)
        e, d, dh = Wv.shape
        h = Wq.shape[1] // dh
        b, t, _ = x.shape
        scale = dh ** (-0.5)
        q = (x @ Wq).reshape(b, t, h, dh).transpose(0, 2, 1, 3)
        k = (x @ Wk).reshape(b, t, h, dh).transpose(0, 2, 1, 3)
        gl_v = (x @ Ws).reshape(b, t, h, e)
        wv = _topk_mask(gl_v, SEL) * jax.nn.sigmoid(gl_v)
        xv = jnp.einsum('btd,edk->btek', x, Wv)
        v = jnp.einsum('bthe,btek->bhtk', wv, xv)
        scores = jnp.einsum('bhid,bhjd->bhij', q * scale, k)
        probs = jax.nn.softmax(scores, axis=-1)
        attn = jnp.einsum('bhij,bhjd->bihd', probs, v)
        gl_o = (x @ Wd).reshape(b, t, h, e)
        mask_o = _topk_mask(gl_o, SEL)
        out = jnp.einsum('bthe,bthk,ekd->btd', mask_o, attn, Wo)
        return out

    def _L1_attn_ref(x, W_qkv, W_o):
        import jax, jax.numpy as jnp
        import numpy as np
        D_MODEL = 256
        NUM_HEADS = 16
        HEAD_DIM = D_MODEL // NUM_HEADS
        ROPE_THETA = 10000.0

        def apply_rope(x):
            S, d_k = (x.shape[-2], x.shape[-1])
            inv_freq = ROPE_THETA ** (jnp.arange(0, d_k, 2, dtype=jnp.float32) / d_k)
            ang = jnp.arange(S, dtype=jnp.float32)[:, None] / inv_freq[None, :]
            cos, sin = (jnp.cos(ang), jnp.sin(ang))
            xp = x.reshape(x.shape[:-1] + (d_k // 2, 2))
            x0, x1 = (xp[..., 0], xp[..., 1])
            out = jnp.stack([x0 * cos - x1 * sin, x0 * sin + x1 * cos], axis=-1)
            return out.reshape(x.shape)
        B, S, d_model = x.shape
        H, d_k = (NUM_HEADS, HEAD_DIM)
        qkv = jnp.einsum('bsi,oi->bso', x, W_qkv)
        Q, K, V = jnp.split(qkv, 3, axis=-1)

        def to_heads(t):
            return t.reshape(B, S, H, d_k).transpose(0, 2, 1, 3)
        Q, K, V = (to_heads(Q), to_heads(K), to_heads(V))
        Q, K = (apply_rope(Q), apply_rope(K))
        scores = jnp.einsum('bhqd,bhkd->bhqk', Q, K) / jnp.sqrt(jnp.float32(d_k))
        causal = jnp.tril(jnp.ones((S, S), dtype=bool))
        scores = jnp.where(causal, scores, -jnp.inf)
        attn = jax.nn.softmax(scores, axis=-1)
        out = jnp.einsum('bhqk,bhkd->bhqd', attn, V)
        out = out.transpose(0, 2, 1, 3).reshape(B, S, d_model)
        return jnp.einsum('bsi,oi->bso', out, W_o)

    def _L1_xattn_ref(q, k, v, mask, w_q, b_q, w_k, b_k, w_v, b_v, w_o, b_o):
        import jax, jax.numpy as jnp
        import numpy as np
        D_MODEL = 256
        H = 16
        D_K = D_MODEL // H
        B, S = (4, 512)
        b, s, _ = q.shape
        query = q @ w_q.T + b_q
        key_ = k @ w_k.T + b_k
        value = v @ w_v.T + b_v
        query = query.reshape(b, s, H, D_K).transpose(0, 2, 1, 3)
        key_ = key_.reshape(b, -1, H, D_K).transpose(0, 2, 1, 3)
        value = value.reshape(b, -1, H, D_K).transpose(0, 2, 1, 3)
        scores = jnp.einsum('bhqd,bhkd->bhqk', query, key_) / jnp.sqrt(jnp.float32(D_K))
        scores = jnp.where(mask == 0, jnp.float32(-1000000000.0), scores)
        attn = jax.nn.softmax(scores, axis=-1)
        out = jnp.einsum('bhqk,bhkd->bhqd', attn, value)
        out = out.transpose(0, 2, 1, 3).reshape(b, s, D_MODEL)
        return out @ w_o.T + b_o

    def _L1_ffn_ref(hidden_states, gate_w, gate_bias, w_gate, w_up, w_down, sh_gate, sh_up, sh_down):
        import jax, jax.numpy as jnp
        import numpy as np
        E = 32
        H = 256
        I = 128
        G = 8
        TKG = 4
        TOPK = 8
        NSH = 2
        SCALE = 2.5
        B, S, Hd = hidden_states.shape
        h = hidden_states.reshape(-1, Hd)
        logits = h.astype(jnp.float32) @ gate_w.T
        scores = jax.nn.sigmoid(logits)
        sc = scores + gate_bias
        grp = sc.reshape(-1, G, E // G)
        group_scores = jax.lax.top_k(grp, 2)[0].sum(-1)
        gidx = jax.lax.top_k(group_scores, TKG)[1]
        gmask = jnp.sum(jax.nn.one_hot(gidx, G, dtype=sc.dtype), axis=1)
        smask = jnp.repeat(gmask, E // G, axis=1)
        masked = jnp.where(smask > 0, sc, jnp.zeros_like(sc))
        tki = jax.lax.top_k(masked, TOPK)[1]
        tkw = jnp.take_along_axis(scores, tki, axis=1)
        tkw = tkw / (tkw.sum(-1, keepdims=True) + 1e-20)
        tkw = tkw * SCALE
        combine = (jax.nn.one_hot(tki, E, dtype=tkw.dtype) * tkw[..., None]).sum(1)
        g = jax.nn.silu(jnp.einsum('th,eih->tei', h, w_gate))
        u = jnp.einsum('th,eih->tei', h, w_up)
        routed = jnp.einsum('tei,ehi->th', g * u * combine[:, :, None], w_down)
        sg = jax.nn.silu(h @ sh_gate.T)
        shared = sg * (h @ sh_up.T) @ sh_down.T
        return (routed + shared).reshape(B, S, Hd)
    x = x + _L0_attn_ref(_layernorm(x, axis=-1), L0_attn_w_qkv, L0_attn_w_o, L0_attn_log_p, L0_attn_log_a, L0_attn_w1, L0_attn_b1, L0_attn_w2, L0_attn_b2)
    x = x + _L0_xattn_ref(_layernorm(x, axis=-1), ctx_1024, ctx_1024, L0_xattn_Wq, L0_xattn_Wk, L0_xattn_Wv, L0_xattn_Wo, L0_xattn_bo)
    x = x + _L0_ffn_ref(_layernorm(x, axis=-1), L0_ffn_Wq, L0_ffn_Wk, L0_ffn_Ws, L0_ffn_Wd, L0_ffn_Wv, L0_ffn_Wo)
    x = x + _L1_attn_ref(_layernorm(x, axis=-1), L1_attn_W_qkv, L1_attn_W_o)
    x = x + _L1_xattn_ref(_layernorm(x, axis=-1), ctx_1024, ctx_1024, mask_1x1xSxS2_ik0, L1_xattn_w_q, L1_xattn_b_q, L1_xattn_w_k, L1_xattn_b_k, L1_xattn_w_v, L1_xattn_b_v, L1_xattn_w_o, L1_xattn_b_o)
    x = x + _L1_ffn_ref(_layernorm(x, axis=-1), L1_ffn_gate_w, L1_ffn_gate_bias, L1_ffn_w_gate, L1_ffn_w_up, L1_ffn_w_down, L1_ffn_sh_gate, L1_ffn_sh_up, L1_ffn_sh_down)
    return x

_drawn_inputs = setup_inputs


def setup_inputs(seed=0):
    import zlib

    import numpy as np

    out = dict(_drawn_inputs(seed))
    spreads = {'L0_attn_b1': (0.0, 0.8), 'L0_attn_b2': (0.0, 0.8)}
    factors = {'L0_attn_log_p': 8.0,
     'L0_attn_log_a': 8.0,
     'L0_attn_w1': 8.0,
     'L0_attn_w2': 8.0,
     'L0_xattn_bo': 3.274,
     'L0_ffn_Wq': 8.0,
     'L0_ffn_Wk': 8.0,
     'L0_ffn_Ws': 3.087,
     'L1_attn_W_qkv': 8.0,
     'L1_attn_W_o': 8.0,
     'L1_xattn_b_q': 4.955,
     'L1_xattn_b_k': 8.0,
     'L1_ffn_gate_w': 7.712,
     'L1_ffn_gate_bias': 8.0,
     'L1_ffn_w_gate': 6.924,
     'L1_ffn_w_up': 6.817,
     'L1_ffn_w_down': 6.784,
     'L1_ffn_sh_gate': 4.3,
     'L1_ffn_sh_up': 4.245,
     'L1_ffn_sh_down': 4.245}
    for name, (base, spread) in spreads.items():
        noise = np.random.default_rng([zlib.crc32(name.encode()), seed]).standard_normal(out[name].shape)
        drawn = base * np.exp(spread * noise) if base else spread * noise
        out[name] = jnp.asarray(drawn.astype(out[name].dtype))
    for name, factor in factors.items():
        out[name] = (out[name] * factor).astype(out[name].dtype)
    return out
```

```python
import numpy as np
import concourse.bass as bass
from concourse import mybir
from contextlib import ExitStack

F32 = mybir.dt.float32
BF16 = mybir.dt.bfloat16
I32 = mybir.dt.int32
ALU = mybir.AluOpType
ACT = mybir.ActivationFunctionType
AX = mybir.AxisListType

P = 128
B, S, DM = 4, 512, 256
NI = S // P
KD = DM // P
CTX = 1024
BANK = 512
NEG = -1e30
MASKED = -float(2 ** 30)
STAGES = "ABCDEF"


def rope_half_tables():
    d = 64
    inv = (1.0 / 10000.0 ** (np.arange(0, d, 2, dtype=np.float32) / np.float32(d))).astype(np.float32)
    ang = np.outer(np.arange(S, dtype=np.float32), inv).astype(np.float32)
    ang = np.concatenate([ang, ang], -1).T
    cos, sin = np.cos(ang.astype(np.float64)), np.sin(ang.astype(np.float64))
    sin[: d // 2] = -sin[: d // 2]
    return np.tile(cos, (2, 1)).astype(np.float32), np.tile(sin, (2, 1)).astype(np.float32)


def rope_pair_tables():
    d = 16
    inv = (np.float32(10000.0) ** (np.arange(0, d, 2, dtype=np.float32) / np.float32(d))).astype(np.float32)
    ang = (np.arange(S, dtype=np.float32)[:, None] / inv[None, :]).astype(np.float32)
    ang = np.repeat(ang, 2, axis=1).T
    cos, sin = np.cos(ang.astype(np.float64)), np.sin(ang.astype(np.float64))
    sin[0::2] = -sin[0::2]
    return np.tile(cos, (8, 1)).astype(np.float32), np.tile(sin, (8, 1)).astype(np.float32)


class Chain:

    def __init__(self, eng, sem):
        self.eng, self.sem, self.n = eng, sem, 0

    def link(self, ins):
        self.n += 1
        ins.then_inc(self.sem, 1)
        self.eng.wait_ge(self.sem, self.n)


class Steps:

    def __init__(self, eng, bars, clears):
        self.eng, self.bars, self.clears, self.k = eng, bars, clears, 0

    def end(self):
        k = self.k % 3
        self.k += 1
        self.eng.drain().then_inc(self.bars[k], 1)
        self.eng.wait_ge(self.bars[k], 5)
        if self.clears:
            self.eng.sem_clear(self.bars[(k - 1) % 3])

    def end_round(self, sems=()):
        self.end()
        if self.clears:
            for s in sems:
                self.eng.sem_clear(s)
        self.end()
        while self.k % 3:
            self.end()


class Attn16:

    def __init__(self, name, nk, causal, masked, rope, cross):
        self.name, self.nk, self.causal, self.masked, self.rope, self.cross = name, nk, causal, masked, rope, cross
        self.nj = nk // P
        self.halves = nk // BANK
        self.tiles = [("q", t, 0) for t in range(2)] + [("k", t, f) for t in range(2) for f in range(self.halves)]
        if causal:
            self.s_tiles = [(i, 0, (i + 1) * P) for i in range(NI)]
            self.units = [[j] for j in range(self.nj)]
        else:
            self.s_tiles = [(i, f * BANK, BANK) for i in range(NI) for f in range(self.halves)]
            self.units = [[2 * u, 2 * u + 1] for u in range(self.nj // 2)]


NH = 16
HD = 16
NE, NSH = 32, 2
NRING = 6
CB = Attn16("B", CTX, False, False, False, True)
CD = Attn16("D", S, True, False, True, False)
CE = Attn16("E", CTX, False, True, False, True)
CFG = {"B": CB, "D": CD, "E": CE}
QPART = [0, 0, 1, 0, 1, 2]
KPART = [0, 1, 0, 2, 1, 0]
KR = 6 * HD
KST = KR + 3


def decoder(nc, io, out, rounds=B):
    ctx = ExitStack()
    with ctx:
        def sb(name, shape, dt=F32):
            return ctx.enter_context(nc.sbuf_tensor(name, shape, dt))

        def sem(name):
            s = ctx.enter_context(nc.semaphore(name))
            counting.append(s)
            return s

        counting = []

        x = sb("x", [P, NI, DM])
        xn = sb("xn", [P, NI, DM])
        xnT = sb("xnT", [P, KD, S])
        ctxT = sb("ctxT", [P, KD, CTX])
        ident = sb("ident", [P, P])
        identb = sb("identb", [P, P], BF16)
        caus = sb("caus", [P, P], BF16)
        causT = sb("causT", [P, P], BF16)
        selden = sb("selden", [P, P])
        mneg = sb("mneg", [P, NI, CTX], BF16)
        mnegT = sb("mnegT", [P, CTX // P, S], BF16)
        live = sb("live", [P, S])
        livec = sb("livec", [P, NI])
        half = sb("half", [P, NI])
        st6 = sb("st6", [P, NI, 6])
        mv = sb("mv", [P, NI, 2])
        rstd = sb("rstd", [P, NI])
        rt = sb("rt", [P, NI])
        cosD = sb("cosD", [P, S])
        sinD = sb("sinD", [P, S])
        boB = sb("boB", [P, DM])
        bvE = sb("bvE", [P, DM])
        boE = sb("boE", [P, DM])
        bqE = sb("bqE", [P, 2])
        bkE = sb("bkE", [P, 2])
        tri = sb("tri", [P, 8, 8])
        selE = sb("selE", [96, NE, P], BF16)
        gateW = sb("gateW", [P, KD, NE])
        gateB = sb("gateB", [P, NE])
        NWIN = 528
        biasA = sb("biasA", [P, NWIN])
        w1A = sb("w1A", [P, P])
        w2A = sb("w2A", [P, 64])
        b1A = sb("b1A", [P, 1])
        cosA = sb("cosA", [P, S])
        sinA = sb("sinA", [P, S])
        WCOLS = 3712
        wbuf = sb("wbuf", [P, 2, WCOLS])
        ps = ctx.enter_context(nc.psum_tensor("ps", [P, 8, BANK], F32))

        bars = [ctx.enter_context(nc.semaphore(f"phase{k}")) for k in range(3)]
        setup_loaded = ctx.enter_context(nc.semaphore("setup_loaded"))
        setup_dve = ctx.enter_context(nc.semaphore("setup_dve"))
        setup_pool_sem = ctx.enter_context(nc.semaphore("setup_pool"))
        setup_pe_sem = ctx.enter_context(nc.semaphore("setup_pe"))
        setup_act = ctx.enter_context(nc.semaphore("setup_act"))
        x_loaded = sem("x_loaded")
        x_stored = sem("x_stored")
        dve_chain = sem("dve_chain")
        pool_chain = sem("pool_chain")
        ln_var = sem("ln_var")
        ln_pow = sem("ln_pow")
        ln_xn = sem("ln_xn")
        ln_tr = sem("ln_tr")
        ln_T = sem("ln_T")
        w_loaded = {s: sem(f"w_loaded_{s}") for s in "BCDE"}
        sm = {}
        for c in CFG:
            if c in STAGES:
                for n in ("proj", "val", "split", "v_mm", "v_up", "v_zero", "part_out", "stack_in", "s_mm", "s_max",
                          "m_parts", "m_mm", "m_row", "st_mm", "exp", "pv", "o_up", "den_mm", "o_norm", "y_mm"):
                    sm[c, n] = sem(f"{n}_{c}")

        def scope(fn):
            with ExitStack() as inner:
                return fn(lambda name, shape, dt=F32: inner.enter_context(nc.sbuf_tensor(name, shape, dt)))

        def attn16_mem(sb2):
            m = {}
            m["QS"] = sb2("QS", [P, NH, S], BF16)
            m["KS"] = sb2("KS", [P, NH, CTX], BF16)
            m["VP"] = sb2("VP", [P, CTX // P, NH, 32])
            m["QP"] = sb2("QP", [P, 3, 2, S], BF16)
            m["KP"] = sb2("KP", [P, 3, 2, CTX], BF16)
            m["val"] = sb2("val", [P, 2, BANK])
            m["rope"] = sb2("rope", [P, BANK])
            m["rest"] = sb2("rest", [P, BANK])
            m["mx"] = sb2("mx", [P, 2, NI, 2])
            m["nm"] = sb2("nm", [P, NI])
            m["nr"] = sb2("nr", [P, NI])
            m["nmp"] = sb2("nmp", [P, 2, NI, 3], BF16)
            m["PT"] = sb2("PT", [P, 2, 2, BANK])
            m["OT"] = sb2("OT", [P, 4, S])
            m["rec"] = sb2("rec", [P, BANK])
            m["ON"] = sb2("ON", [P, 4, S])
            return m

        M16 = scope(attn16_mem)
        qd = nc.dram_tensor("qparts", (3, 2, P, S), BF16, kind="Internal").ap()
        kd = nc.dram_tensor("kparts", (3, 2, P, CTX), BF16, kind="Internal").ap()

        WIDTH = {"B": 2560, "D": 3584, "E": 2560, "C": 3616}
        ORDER = [s for s in "BCDE" if s in STAGES]
        slot_of = {s: n % 2 for n, s in enumerate(ORDER)}

        def W(stage, first, cols):
            return wbuf[:, slot_of[stage], first:first + cols]

        def ln_dve(dve, ch, n):
            for i in range(NI):
                last = nc.vector.bn_stats(out=st6[:, i, :], in_=x[:, i, :])
            ch.link(last)
            for i in range(NI):
                last = nc.vector.bn_aggr(out=mv[:, i, :], in_=st6[:, i, :])
            ch.link(last)
            nc.vector.tensor_scalar(mv[:, :, 1], mv[:, :, 1], 1e-5, None, ALU.add).then_inc(ln_var, 1)
            dve.wait_ge(ln_pow, n + 1)
            ch.link(nc.vector.tensor_tensor(rt[:, :], rstd[:, :], rstd[:, :], ALU.mult))
            ch.link(nc.vector.tensor_tensor(rt[:, :], rt[:, :], mv[:, :, 1], ALU.mult))
            ch.link(nc.vector.tensor_scalar(rt[:, :], rt[:, :], -0.5, 1.5, ALU.mult, ALU.add))
            ch.link(nc.vector.tensor_tensor(rstd[:, :], rstd[:, :], rt[:, :], ALU.mult))
            for i in range(NI):
                nc.vector.tensor_scalar(xn[:, i, :], x[:, i, :], mv[:, i, 0:1], rstd[:, i:i + 1],
                                        ALU.subtract, ALU.mult).then_inc(ln_xn, 1)

        def ln_pool(pool, n):
            pool.wait_ge(ln_var, n + 1)
            nc.gpsimd.tensor_tensor(rstd[:, :], mv[:, :, 1], half[:, :], ALU.pow).then_inc(ln_pow, 1)

        def ln_pe(pe, n):
            for i in range(NI):
                pe.wait_ge(ln_xn, NI * n + i + 1)
                for k in range(KD):
                    last = nc.tensor.transpose(ps[:, k, i * P:(i + 1) * P], xn[:, i, k * P:(k + 1) * P], ident[:, :])
            last.then_inc(ln_tr, 1)

        def ln_act(act, n):
            act.wait_ge(ln_tr, n + 1)
            for k in range(KD):
                last = nc.scalar.activation(xnT[:, k, :], ps[:, k, :], ACT.Copy)
            last.then_inc(ln_T, 1)

        def a16_sp(sp, c):
            m = M16
            g = lambda n: sm[c.name, n]
            nq = 2
            sp.wait_ge(g("split"), nq)
            sp.dma_start(qd.rearrange("a t p n -> p (a t) n"), m["QP"][:, :, :, :].rearrange("p a t n -> p (a t) n")).then_inc(g("part_out"), 16)
            sp.wait_ge(g("part_out"), 16)
            for r in range(6):
                src = qd[QPART[r]].rearrange("t (e d) n -> d (t e) n", d=HD)
                sp.dma_start(m["QS"][HD * r:HD * r + HD, :, :], src).then_inc(g("stack_in"), 16)
            sp.wait_ge(g("split"), len(c.tiles))
            for a in range(3):
                sp.dma_start(kd[a, :, :, 0:c.nk].rearrange("t p n -> p t n"), m["KP"][:, a, :, 0:c.nk]).then_inc(g("part_out"), 16)
            sp.wait_ge(g("part_out"), 64)
            for r in range(6):
                src = kd[KPART[r], :, :, 0:c.nk].rearrange("t (e d) n -> d (t e) n", d=HD)
                sp.dma_start(m["KS"][HD * r:HD * r + HD, :, 0:c.nk], src).then_inc(g("stack_in"), 16)

        def a16_pool(pool, ch, c):
            m = M16
            ch.link(nc.gpsimd.memset(m["VP"][:, :, :, :], 0.0))
            ch.link(nc.gpsimd.memset(m["VP"][:, :, :, HD:HD + 1], 1.0))
            nc.gpsimd.memset(m["KS"][KR:KST, :, 0:c.nk], 1.0).then_inc(sm[c.name, "v_zero"], 1)

        def a16_pe(pe, c, n):
            m = M16
            g = lambda s: sm[c.name, s]
            src = ctxT if c.cross else xnT
            nw = 4 if c.rope else 2
            wq, wk = 0, (2 if c.rope else 1) * KD * DM
            wv = nw * KD * DM
            wo = wv + KD * DM
            pe.wait_ge(w_loaded[c.name], 16)
            pe.wait_ge(ln_T, n + 1)
            step = 2 if c.rope else 1
            nb = 6 // step
            for e, (kind, t, f) in enumerate(c.tiles):
                if e >= nb:
                    pe.wait_ge(g("val"), e - nb + 1)
                for v in range(step):
                    base = (wq if kind == "q" else wk) + v * KD * DM
                    for k in range(KD):
                        rhs = xnT[:, k, :] if kind == "q" else src[:, k, f * BANK:(f + 1) * BANK]
                        last = nc.tensor.matmul(ps[:, (step * e + v) % 6, :], W(c.name, base + k * DM + t * P, P), rhs,
                                                start=(k == 0), stop=(k == KD - 1))
                last.then_inc(g("proj"), 1)
            for j in range(c.nj // 2):
                if j >= 2:
                    pe.wait_ge(g("v_up"), j - 1)
                for e in range(2):
                    jt = 2 * j + e
                    for k in range(KD):
                        last = nc.tensor.matmul(ps[:, 6 + j % 2, e * DM:(e + 1) * DM], src[:, k, jt * P:(jt + 1) * P],
                                                W(c.name, wv + k * DM, DM), start=(k == 0), stop=(k == KD - 1))
                last.then_inc(g("v_mm"), 1)
            pe.wait_ge(g("v_up"), c.nj // 2)
            pe.wait_ge(g("v_zero"), 1)
            pe.wait_ge(g("stack_in"), 12 * 16)
            ns, nu = len(c.s_tiles), len(c.units)

            def scores(h, tiles):
                for e in tiles:
                    s = h * ns + e
                    i, f, w = c.s_tiles[e]
                    if s >= 2:
                        pe.wait_ge(g("s_max"), s - 1)
                    o = ps[:, s % 2, 0:w]
                    plain = not (c.causal or c.masked)
                    last = nc.tensor.matmul(o, m["QS"][0:KR, h, i * P:(i + 1) * P], m["KS"][0:KR, h, f:f + w],
                                            start=True, stop=plain)
                    if c.causal:
                        last = nc.tensor.matmul(ps[:, s % 2, i * P:(i + 1) * P], identb[:, :], caus[:, :], start=False, stop=True)
                    if c.masked:
                        last = nc.tensor.matmul(o, identb[:, :], mneg[:, i, f:f + w], start=False, stop=True)
                    last.then_inc(g("s_mm"), 1)

            def max_row(h):
                pe.wait_ge(g("m_parts"), h + 1)
                if h:
                    pe.wait_ge(g("m_row"), h)
                for i in range(NI):
                    last = nc.tensor.matmul(ps[KR:KST, 7, i * P:(i + 1) * P], m["nmp"][:, h % 2, i, :], identb[:, :],
                                            start=True, stop=True)
                last.then_inc(g("m_mm"), 1)

            def scores_t(h, u):
                gu = h * nu + u
                if u == 0:
                    pe.wait_ge(g("m_row"), h + 1)
                if gu >= 2:
                    pe.wait_ge(g("exp"), gu - 1)
                for e, j in enumerate(c.units[u]):
                    q0 = j * P if c.causal else 0
                    o = ps[:, 2 + 2 * (gu % 2) + e, 0:S - q0]
                    plain = not (c.causal or c.masked)
                    last = nc.tensor.matmul(o, m["KS"][0:KST, h, j * P:(j + 1) * P], m["QS"][0:KST, h, q0:S],
                                            start=True, stop=plain)
                    if c.causal:
                        last = nc.tensor.matmul(o[:, 0:P], identb[:, :], causT[:, :], start=False, stop=True)
                    if c.masked:
                        last = nc.tensor.matmul(o, identb[:, :], mnegT[:, j, :], start=False, stop=True)
                last.then_inc(g("st_mm"), 1)

            def weighted(h, u):
                gu = h * nu + u
                pe.wait_ge(g("exp"), gu + 1)
                if h % 4 == 0 and u == 0 and h:
                    pe.wait_ge(g("o_up"), h // 4)
                for e, j in enumerate(c.units[u]):
                    q0 = j * P if c.causal else 0
                    r = 32 * (h % 4)
                    last = nc.tensor.matmul(ps[r:r + 32, 6, q0:S], m["VP"][:, j, h, :], m["PT"][:, gu % 2, e, 0:S - q0],
                                            start=(j == 0), stop=(j == c.nj - 1), tile_position=(0, r))
                last.then_inc(g("pv"), 1)

            scores(0, range(ns))
            scores(1, range(ns))
            max_row(0)
            before = None
            share = ns // nu
            for h in range(NH):
                for u in range(nu):
                    scores_t(h, u)
                    if u == 1 and h + 1 < NH:
                        max_row(h + 1)
                    if h + 2 < NH:
                        scores(h + 2, range(u * share, (u + 1) * share))
                    if before:
                        weighted(*before)
                    before = (h, u)
            weighted(*before)
            for q in range(4):
                pe.wait_ge(g("o_up"), q + 1)
                nc.tensor.matmul(ps[:, q, :], selden[:, :], m["OT"][:, q, :], start=True, stop=True).then_inc(g("den_mm"), 1)
            for i in range(NI):
                for q in range(4):
                    if i == 0:
                        pe.wait_ge(g("o_norm"), q + 1)
                    last = nc.tensor.matmul(ps[:, 4 + i, 0:DM], m["ON"][:, q, i * P:(i + 1) * P],
                                            W(c.name, wo + q * DM, DM), start=(q == 0), stop=(q == 3))
                last.then_inc(g("y_mm"), 1)

        def a16_act(act, c):
            m = M16
            g = lambda s: sm[c.name, s]
            step = 2 if c.rope else 1
            if not c.rope:
                for e, (kind, t, f) in enumerate(c.tiles):
                    act.wait_ge(g("proj"), e + 1)
                    if e >= 2:
                        act.wait_ge(g("split"), e - 1)
                    if c.masked:
                        bias = (bqE if kind == "q" else bkE)[:, t:t + 1]
                        nc.scalar.activation(m["val"][:, e % 2, :], ps[:, e % 6, :], ACT.Identity, bias=bias).then_inc(g("val"), 1)
                    else:
                        nc.scalar.activation(m["val"][:, e % 2, :], ps[:, e % 6, :], ACT.Copy).then_inc(g("val"), 1)
            act.wait_ge(g("v_zero"), 1)
            if not c.masked:
                for j in range(c.nj // 2):
                    act.wait_ge(g("v_mm"), j + 1)
                    nc.scalar.activation(m["VP"][:, 2 * j:2 * j + 2, :, 0:HD],
                                         ps[:, 6 + j % 2, :].rearrange("p (j h d) -> p j h d", j=2, d=HD), ACT.Copy).then_inc(g("v_up"), 1)
            nu = len(c.units)

            def row(h):
                act.wait_ge(g("m_mm"), h + 1)
                nc.scalar.activation(m["QS"][KR:KST, h, :], ps[KR:KST, 7, :], ACT.Copy).then_inc(g("m_row"), 1)

            row(0)
            for h in range(NH):
                for u in range(nu):
                    gu = h * nu + u
                    act.wait_ge(g("st_mm"), gu + 1)
                    if gu >= 2:
                        act.wait_ge(g("pv"), gu - 1)
                    n = len(c.units[u])
                    w = S - c.units[u][0] * P if c.causal else S
                    b0 = 2 + 2 * (gu % 2)
                    nc.scalar.activation(m["PT"][:, gu % 2, 0:n, 0:w], ps[:, b0:b0 + n, 0:w], ACT.Exp,
                                         scale=HD ** -0.5).then_inc(g("exp"), 1)
                    if u == 1 and h + 1 < NH:
                        row(h + 1)

        def a16_dve(dve, ch, c):
            m = M16
            g = lambda s: sm[c.name, s]

            def parts(dst, src, rest, last_sem):
                ch.link(nc.vector.tensor_copy(dst(0), src))
                ch.link(nc.vector.tensor_tensor(rest, src, dst(0), ALU.subtract))
                ch.link(nc.vector.tensor_copy(dst(1), rest))
                nc.vector.tensor_tensor(dst(2), rest, dst(1), ALU.subtract).then_inc(last_sem, 1)

            for e, (kind, t, f) in enumerate(c.tiles):
                if c.rope:
                    dve.wait_ge(g("proj"), e + 1)
                    b0 = (2 * e) % 6
                    if e >= 1:
                        dve.wait_ge(g("split"), e)
                    ch.link(nc.vector.tensor_tensor(m["rope"][:, :], ps[:, b0 + 1, :], sinD[:, :], ALU.mult))
                    ch.link(nc.vector.tensor_tensor(m["val"][:, e % 2, :], ps[:, b0, :], cosD[:, :], ALU.mult))
                    nc.vector.tensor_tensor(m["val"][:, e % 2, :], m["val"][:, e % 2, :], m["rope"][:, :], ALU.add).then_inc(g("val"), 1)
                dve.wait_ge(g("val"), e + 1)
                if c.masked and kind == "q":
                    ch.link(nc.vector.tensor_tensor(m["val"][:, e % 2, :], m["val"][:, e % 2, :], live[:, :], ALU.mult))
                if e >= 1:
                    dve.wait_ge(g("split"), e)
                dst = (lambda a: m["QP"][:, a, t, :]) if kind == "q" else (lambda a: m["KP"][:, a, t, f * BANK:(f + 1) * BANK])
                parts(dst, m["val"][:, e % 2, :], m["rest"][:, :], g("split"))
            if c.masked:
                dve.wait_ge(g("v_zero"), 1)
                for j in range(c.nj // 2):
                    dve.wait_ge(g("v_mm"), j + 1)
                    for e in range(2):
                        last = nc.vector.tensor_tensor(m["VP"][:, 2 * j + e, :, 0:HD],
                                                       ps[:, 6 + j % 2, e * DM:(e + 1) * DM].rearrange("p (h d) -> p h d", d=HD),
                                                       bvE[:, :].rearrange("p (h d) -> p h d", d=HD), ALU.add)
                    last.then_inc(g("v_up"), 1)
            ns, nu = len(c.s_tiles), len(c.units)

            def maxima(h):
                for e, (i, f, w) in enumerate(c.s_tiles):
                    s = h * ns + e
                    dve.wait_ge(g("s_mm"), s + 1)
                    nc.vector.tensor_reduce(m["mx"][:, h % 2, i, f // BANK:f // BANK + 1], ps[:, s % 2, 0:w], AX.X, ALU.max).then_inc(g("s_max"), 1)
                dve.wait_ge(g("s_max"), (h + 1) * ns)
                if c.halves == 2:
                    ch.link(nc.vector.tensor_tensor(m["nm"][:, :], m["mx"][:, h % 2, :, 0], m["mx"][:, h % 2, :, 1], ALU.max))
                    ch.link(nc.vector.tensor_scalar(m["nm"][:, :], m["nm"][:, :], -1.0, None, ALU.mult))
                else:
                    ch.link(nc.vector.tensor_scalar(m["nm"][:, :], m["mx"][:, h % 2, :, 0], -1.0, None, ALU.mult))
                if h >= 2:
                    dve.wait_ge(g("m_mm"), h - 1)
                parts(lambda a: m["nmp"][:, h % 2, :, a], m["nm"][:, :], m["nr"][:, :], g("m_parts"))
                dve.wait_ge(g("m_parts"), h + 1)

            maxima(0)
            maxima(1)
            for h in range(NH):
                if h + 2 < NH:
                    maxima(h + 2)
                if h % 4 == 3:
                    dve.wait_ge(g("pv"), (h + 1) * nu)
                    nc.vector.tensor_copy(m["OT"][:, h // 4, :], ps[:, 6, :]).then_inc(g("o_up"), 1)
            for q in range(4):
                dve.wait_ge(g("den_mm"), q + 1)
                if q:
                    dve.wait_ge(g("o_norm"), q)
                ch.link(nc.vector.reciprocal(m["rec"][:, :], ps[:, q, :]))
                nc.vector.tensor_tensor(m["ON"][:, q, :], m["OT"][:, q, :], m["rec"][:, :], ALU.mult).then_inc(g("o_norm"), 1)
            for i in range(NI):
                dve.wait_ge(g("y_mm"), i + 1)
                ch.link(nc.vector.tensor_tensor(x[:, i, :], x[:, i, :], ps[:, 4 + i, 0:DM], ALU.add))
                bo = {"B": boB, "E": boE}.get(c.name)
                if bo is not None:
                    ch.link(nc.vector.tensor_tensor(x[:, i, :], x[:, i, :], bo[:, :], ALU.add))
        EXTRA = {}
        SETUP_MORE = {}

        def named(prefix, *names):
            if prefix in STAGES:
                for n in names:
                    sm[prefix, n] = sem(f"{n}_{prefix}")


        def spread(ap, axis, shape):
            return ap.unsqueeze(axis).broadcast_to(shape)

        def top_mask(ch, v, groups, n, keep, c1, c2, mask):
            shape = [P, groups, n, n]
            other, own = spread(v, 2, shape), spread(v, 3, shape)
            earlier = spread(tri[:, 0:n, 0:n], 1, shape)
            ch.link(nc.vector.tensor_tensor(c1, other, own, ALU.is_gt))
            ch.link(nc.vector.tensor_tensor(c2, other, own, ALU.is_equal))
            ch.link(nc.vector.tensor_tensor(c2, c2, earlier, ALU.mult))
            ch.link(nc.vector.tensor_tensor(c1, c1, c2, ALU.add))
            ch.link(nc.vector.tensor_reduce(mask, c1, AX.X, ALU.add))
            ch.link(nc.vector.tensor_scalar(mask, mask, keep - 0.5, None, ALU.is_lt))

        CH, CW, CN = 8, 64, 5
        named("C", "gl_mm", "sig", "gl_free", "xv_mm", "xv_up", "qk_mm", "qk_up", "s_mm", "negm", "exp", "tr", "pt_up", "v_up", "pv",
              "o_up", "ob_mm", "attn", "ae", "aet_mm", "aet_up", "y_mm")

        def c_mem(sb2):
            m = {}
            m["qk"] = sb2("c_qk", [P, 8, S])
            m["gl"] = sb2("c_gl", [P, NI * 2 * CH, CN])
            m["msk"] = sb2("c_msk", [P, NI * 2 * CH, CN])
            m["c1"] = sb2("c_c1", [P, NI * 2 * CH, CN, CN])
            m["c2"] = sb2("c_c2", [P, NI * 2 * CH, CN, CN])
            m["sg"] = sb2("c_sg", [P, NI, 2 * CH * CN])
            m["xv"] = sb2("c_xv", [P, NI, CN * CW])
            m["V"] = sb2("c_V", [P, NI, CH * CW])
            m["tmp"] = sb2("c_tmp", [P, 2, CH * CW])
            m["Pr"] = sb2("c_P", [P, 2, S])
            m["PT"] = sb2("c_PT", [P, 2, NI, S])
            m["nm"] = sb2("c_nm", [P, CH * NI])
            m["den"] = sb2("c_den", [P, NI, CH])
            m["rden"] = sb2("c_rden", [P, NI, CH])
            m["OT"] = sb2("c_OT", [P, 2, S])
            m["at"] = sb2("c_at", [P, NI, CH * CW])
            m["ae"] = sb2("c_ae", [P, NI, CN * CW])
            m["aeT"] = sb2("c_aeT", [P, 3, S])
            return m

        MC = scope(c_mem)
        C_Q, C_K, C_G, C_X, C_O = 0, 1024, 2048, 2208, 2848
        KT_AE = [P, P, CN * CW - 2 * P]

        def c_pe(pe, _, n, st):
            m = MC
            g = lambda s: sm["C", s]
            pe.wait_ge(w_loaded["C"], 16)
            pe.wait_ge(ln_T, n + 1)
            for i in range(NI):
                for k in range(KD):
                    last = nc.tensor.matmul(ps[:, 0, i * 80:(i + 1) * 80], xnT[:, k, i * P:(i + 1) * P],
                                            W("C", C_G + 80 * k, 80), start=(k == 0), stop=(k == KD - 1))
            last.then_inc(g("gl_mm"), 1)
            for i in range(NI):
                for k in range(KD):
                    last = nc.tensor.matmul(ps[:, 1 + i, 0:320], xnT[:, k, i * P:(i + 1) * P],
                                            W("C", C_X + 320 * k, 320), start=(k == 0), stop=(k == KD - 1))
                last.then_inc(g("xv_mm"), 1)
            for e in range(8):
                if e >= 3:
                    pe.wait_ge(g("qk_up"), e - 2)
                base = (C_Q if e < 4 else C_K) + (e % 4) * P
                for k in range(KD):
                    last = nc.tensor.matmul(ps[:, 5 + e % 3, :], W("C", base + 512 * k, P), xnT[:, k, :],
                                            start=(k == 0), stop=(k == KD - 1))
                last.then_inc(g("qk_mm"), 1)
            pe.wait_ge(g("qk_up"), 8)
            pe.wait_ge(g("xv_up"), NI)
            pe.wait_ge(g("gl_free"), 1)

            def scores(s):
                h, i = divmod(s, NI)
                if s >= 2:
                    pe.wait_ge(g("exp"), s - 1)
                r = CW * (h % 2)
                nc.tensor.matmul(ps[:, s % 2, :], m["qk"][r:r + CW, h // 2, i * P:(i + 1) * P], m["qk"][r:r + CW, 4 + h // 2, :],
                                 start=True, stop=True).then_inc(g("s_mm"), 1)

            def turn(s):
                pe.wait_ge(g("exp"), s + 1)
                if s >= 2:
                    pe.wait_ge(g("pt_up"), s - 1)
                for j in range(NI):
                    last = nc.tensor.transpose(ps[:, 2 + s % 2, j * P:(j + 1) * P], m["Pr"][:, s % 2, j * P:(j + 1) * P], ident[:, :])
                last.then_inc(g("tr"), 1)

            def weighted(h):
                pe.wait_ge(g("pt_up"), NI * (h + 1))
                pe.wait_ge(g("v_up"), NI)
                if h % 2 == 0 and h >= 4:
                    pe.wait_ge(g("o_up"), h // 2 - 1)
                r = CW * (h % 2)
                for j in range(NI):
                    last = nc.tensor.matmul(ps[r:r + CW, 4 + (h // 2) % 2, :], m["V"][:, j, h * CW:(h + 1) * CW], m["PT"][:, h % 2, j, :],
                                            start=(j == 0), stop=(j == NI - 1), tile_position=(0, r))
                last.then_inc(g("pv"), 1)

            def back(q):
                pe.wait_ge(g("o_up"), q + 1)
                if q >= 2:
                    pe.wait_ge(g("attn"), q - 1)
                for i in range(NI):
                    last = nc.tensor.transpose(ps[:, 6 + q % 2, i * P:(i + 1) * P], m["OT"][:, q % 2, i * P:(i + 1) * P], ident[:, :])
                last.then_inc(g("ob_mm"), 1)

            scores(0)
            scores(1)
            for s in range(CH * NI):
                if s + 2 < CH * NI:
                    scores(s + 2)
                h, i = divmod(s, NI)
                if i == 1 and h:
                    weighted(h - 1)
                if i == 3 and h and h % 2 == 0:
                    back(h // 2 - 1)
                turn(s)
            weighted(CH - 1)
            back(CH // 2 - 1)
            for i in range(NI):
                pe.wait_ge(g("ae"), i + 1)
                if i:
                    pe.wait_ge(g("aet_up"), i)
                for t, rows in enumerate(KT_AE):
                    last = nc.tensor.transpose(ps[0:rows, t, i * P:(i + 1) * P], m["ae"][:, i, t * P:t * P + rows], ident[:, :])
                last.then_inc(g("aet_mm"), 1)
            for i in range(NI):
                pe.wait_ge(g("aet_up"), i + 1)
                for t, rows in enumerate(KT_AE):
                    last = nc.tensor.matmul(ps[:, 4 + i, 0:DM], m["aeT"][0:rows, t, i * P:(i + 1) * P],
                                            wbuf[0:rows, slot_of["C"], C_O + t * DM:C_O + (t + 1) * DM],
                                            start=(t == 0), stop=(t == 2))
                last.then_inc(g("y_mm"), 1)

        def c_act(act, _, n, st):
            m = MC
            g = lambda s: sm["C", s]
            act.wait_ge(g("gl_free"), 1)
            nc.scalar.activation(m["sg"][:, :, :], m["gl"][:, :, :].rearrange("p (i a) e -> p i (a e)", i=NI), ACT.Exp, scale=-1.0).then_inc(g("sig"), 1)
            for i in range(NI):
                act.wait_ge(g("xv_mm"), i + 1)
                nc.scalar.activation(m["xv"][:, i, :], ps[:, 1 + i, 0:320], ACT.Copy).then_inc(g("xv_up"), 1)
            for e in range(8):
                act.wait_ge(g("qk_mm"), e + 1)
                nc.scalar.activation(m["qk"][:, e, :], ps[:, 5 + e % 3, :], ACT.Copy).then_inc(g("qk_up"), 1)

            def up(s):
                h, i = divmod(s, NI)
                act.wait_ge(g("tr"), s + 1)
                if h >= 2:
                    act.wait_ge(g("pv"), h - 1)
                nc.scalar.activation(m["PT"][:, h % 2, :, i * P:(i + 1) * P],
                                     ps[:, 2 + s % 2, :].rearrange("p (j q) -> p j q", j=NI), ACT.Copy).then_inc(g("pt_up"), 1)

            for s in range(CH * NI):
                h, i = divmod(s, NI)
                act.wait_ge(g("negm"), s + 1)
                if s >= 2:
                    act.wait_ge(g("tr"), s - 1)
                nc.scalar.activation(m["Pr"][:, s % 2, :], ps[:, s % 2, :], ACT.Exp, bias=m["nm"][:, s:s + 1], scale=CW ** -0.5,
                                     accum_out=m["den"][:, i, h:h + 1]).then_inc(g("exp"), 1)
                if s:
                    up(s - 1)
            up(CH * NI - 1)
            for i in range(NI):
                act.wait_ge(g("aet_mm"), i + 1)
                for t, rows in enumerate(KT_AE):
                    last = nc.scalar.activation(m["aeT"][0:rows, t, i * P:(i + 1) * P], ps[0:rows, t, i * P:(i + 1) * P], ACT.Copy)
                last.then_inc(g("aet_up"), 1)

        def c_dve(dve, ch, n, st):
            m = MC
            g = lambda s: sm["C", s]
            dve.wait_ge(g("gl_mm"), 1)
            nc.vector.tensor_copy(m["gl"][:, :, :], ps[:, 0, 0:320].rearrange("p (a e) -> p a e", e=CN)).then_inc(g("gl_free"), 1)
            dve.wait_ge(g("gl_free"), 1)
            top_mask(ch, m["gl"][:, :, :], NI * 2 * CH, CN, 2, m["c1"][:, :, :, :], m["c2"][:, :, :, :], m["msk"][:, :, :])
            dve.wait_ge(g("sig"), 1)
            ch.link(nc.vector.tensor_scalar(m["sg"][:, :, :], m["sg"][:, :, :], 1.0, None, ALU.add))
            ch.link(nc.vector.reciprocal(m["sg"][:, :, :], m["sg"][:, :, :]))
            mk = m["msk"][:, :, :].rearrange("p (i a) e -> p i (a e)", i=NI)
            ch.link(nc.vector.tensor_tensor(m["sg"][:, :, :], m["sg"][:, :, :], mk, ALU.mult))

            def maximum(s):
                dve.wait_ge(g("s_mm"), s + 1)
                ch.link(nc.vector.tensor_reduce(m["nm"][:, s:s + 1], ps[:, s % 2, :], AX.X, ALU.max))
                nc.vector.tensor_scalar(m["nm"][:, s:s + 1], m["nm"][:, s:s + 1], -(CW ** -0.5), None, ALU.mult).then_inc(g("negm"), 1)

            def mix(i):
                shape = [P, CH, CW]
                dst = m["V"][:, i, :].rearrange("p (h k) -> p h k", h=CH)
                for e in range(CN):
                    gate = spread(m["sg"][:, i, 0:CH * CN].rearrange("p (h e) -> p h e", e=CN)[:, :, e], 2, shape)
                    val = spread(m["xv"][:, i, e * CW:(e + 1) * CW], 1, shape)
                    o = dst if e == 0 else m["tmp"][:, 0, :].rearrange("p (h k) -> p h k", h=CH)
                    ch.link(nc.vector.tensor_tensor(o, val, gate, ALU.mult))
                    if e:
                        add = nc.vector.tensor_tensor(dst, dst, o, ALU.add)
                        if e < CN - 1:
                            ch.link(add)
                add.then_inc(g("v_up"), 1)

            def pair(q):
                dve.wait_ge(g("pv"), 2 * q + 2)
                if q >= 2:
                    dve.wait_ge(g("ob_mm"), q - 1)
                nc.vector.tensor_copy(m["OT"][:, q % 2, :], ps[:, 4 + q % 2, :]).then_inc(g("o_up"), 1)
                ch.link(nc.vector.reciprocal(m["rden"][:, :, 2 * q:2 * q + 2], m["den"][:, :, 2 * q:2 * q + 2]))
                dve.wait_ge(g("ob_mm"), q + 1)
                for i in range(NI):
                    last = nc.vector.tensor_tensor(m["at"][:, i, q * P:(q + 1) * P].rearrange("p (h k) -> p h k", h=2),
                                                   ps[:, 6 + q % 2, i * P:(i + 1) * P].rearrange("p (h k) -> p h k", h=2),
                                                   spread(m["rden"][:, i, 2 * q:2 * q + 2], 2, [P, 2, CW]), ALU.mult)
                last.then_inc(g("attn"), 1)

            dve.wait_ge(g("xv_up"), NI)
            for s in range(CH * NI):
                h, i = divmod(s, NI)
                maximum(s)
                if s < NI:
                    mix(s)
                if i == 3 and h >= 2 and h % 2 == 0:
                    pair(h // 2 - 1)
            pair(CH // 2 - 1)
            dve.wait_ge(g("attn"), CH // 2)
            for i in range(NI):
                shape = [P, CH, CW]
                for e in range(CN):
                    k = (i * CN + e) % 2
                    pick = spread(m["msk"][:, :, :].rearrange("p (i a) e -> p i a e", i=NI)[:, i, CH:2 * CH, e], 2, shape)
                    ch.link(nc.vector.tensor_tensor(m["tmp"][:, k, :].rearrange("p (h k) -> p h k", h=CH),
                                                    m["at"][:, i, :].rearrange("p (h k) -> p h k", h=CH), pick, ALU.mult))
                    last = nc.vector.tensor_reduce(m["ae"][:, i, e * CW:(e + 1) * CW],
                                                   m["tmp"][:, k, :].rearrange("p (h k) -> p k h", h=CH), AX.X, ALU.add)
                last.then_inc(g("ae"), 1)
            for i in range(NI):
                dve.wait_ge(g("y_mm"), i + 1)
                ch.link(nc.vector.tensor_tensor(x[:, i, :], x[:, i, :], ps[:, 4 + i, 0:DM], ALU.add))

        EXTRA["C"] = dict(pe=c_pe, act=c_act, dve=c_dve, pool=lambda *a: None, sp=lambda *a: None)

        named("F", "lg_mm", "lg_exp", "comb", "ct_mm", "ct_up", "gu_mm", "silu", "gu", "down")

        if "F" in STAGES:
            w_in = [sem(f"w_in{k}_F") for k in range(NRING)]

        def f_mem(sb2):
            m = {}
            m["w"] = sb2("f_w", [P, NRING, 3 * DM])
            m["sc"] = sb2("f_sc", [P, NI, NE])
            m["sb"] = sb2("f_sb", [P, NI, NE])
            m["mb"] = sb2("f_mb", [P, NI, NE])
            m["rp"] = sb2("f_rp", [P, NI, NE])
            m["t8"] = sb2("f_t8", [P, NI, 8])
            m["m4"] = sb2("f_m4", [P, NI * 8, 4])
            m["c1"] = sb2("f_c1", [P, NI * 128])
            m["c2"] = sb2("f_c2", [P, NI * 128])
            m["gs"] = sb2("f_gs", [P, NI, 8])
            m["gm"] = sb2("f_gm", [P, NI, 8])
            m["sum"] = sb2("f_sum", [P, NI])
            m["rest"] = sb2("f_rest", [P, NI, NE])
            m["cp"] = sb2("f_cp", [P, NI, 3, NE], BF16)
            m["cT"] = sb2("f_cT", [96, S], BF16)
            m["si"] = sb2("f_si", [P, 2, S])
            m["gu"] = sb2("f_gu", [P, 2, S])
            m["tm"] = sb2("f_tm", [P, S])
            return m

        MF = scope(f_mem)

        def f_sp(sp, *_):
            for e in range(NE + NSH):
                if e >= NRING:
                    sp.wait_ge(sm["F", "down"], e - NRING + 1)
                sp.dma_start(MF["w"][:, e % NRING, :], io["wF"][e]).then_inc(w_in[e % NRING], 16)

        def f_pe(pe, _, n, st):
            m = MF
            g = lambda s: sm["F", s]
            pe.wait_ge(ln_T, n + 1)
            for i in range(NI):
                for k in range(KD):
                    last = nc.tensor.matmul(ps[:, 4, i * NE:(i + 1) * NE], xnT[:, k, i * P:(i + 1) * P], gateW[:, k, :],
                                            start=(k == 0), stop=(k == KD - 1))
            last.then_inc(g("lg_mm"), 1)

            def up(e):
                pe.wait_ge(w_in[e % NRING], 16 * (e // NRING + 1))
                if e >= 2:
                    pe.wait_ge(g("gu"), e - 1)
                for v in range(2):
                    for k in range(KD):
                        last = nc.tensor.matmul(ps[:, 2 * v + e % 2, :], m["w"][:, e % NRING, (2 * v + k) * P:(2 * v + k + 1) * P],
                                                xnT[:, k, :], start=(k == 0), stop=(k == KD - 1))
                if e == NSH:
                    pe.wait_ge(g("comb"), 1)
                    for i in range(NI):
                        last = nc.tensor.matmul(ps[0:96, 5, i * P:(i + 1) * P], m["cp"][:, i, :, :].rearrange("p a e -> p (a e)"),
                                                identb[:, :], start=True, stop=True)
                    last.then_inc(g("ct_mm"), 1)
                    pe.wait_ge(g("ct_up"), 1)
                if e >= NSH:
                    last = nc.tensor.matmul(ps[:, 4 + e % 2, :], selE[:, e - NSH, :], m["cT"][:, :], start=True, stop=True)
                last.then_inc(g("gu_mm"), 1)

            def down(e):
                pe.wait_ge(g("gu"), e + 1)
                for i in range(NI):
                    last = nc.tensor.matmul(ps[:, 6 + i // 2, (i % 2) * DM:(i % 2 + 1) * DM], m["gu"][:, e % 2, i * P:(i + 1) * P],
                                            m["w"][:, e % NRING, 2 * DM:3 * DM], start=(e == 0 and i % 2 == 0),
                                            stop=(e == NE + NSH - 1), skip_group_check=True)
                last.then_inc(g("down"), 1)

            up(0)
            for e in range(1, NE + NSH):
                up(e)
                down(e - 1)
            down(NE + NSH - 1)

        def f_act(act, _, n, st):
            m = MF
            g = lambda s: sm["F", s]
            act.wait_ge(g("lg_mm"), 1)
            nc.scalar.activation(m["sc"][:, :, :], ps[:, 4, 0:NI * NE].rearrange("p (i e) -> p i e", i=NI), ACT.Exp, scale=-1.0).then_inc(g("lg_exp"), 1)
            for e in range(NE + NSH):
                if e == NSH:
                    act.wait_ge(g("ct_mm"), 1)
                    nc.scalar.activation(m["cT"][:, :], ps[0:96, 5, :], ACT.Copy).then_inc(g("ct_up"), 1)
                act.wait_ge(g("gu_mm"), e + 1)
                if e >= 2:
                    act.wait_ge(g("gu"), e - 1)
                nc.scalar.activation(m["si"][:, e % 2, :], ps[:, e % 2, :], ACT.Silu).then_inc(g("silu"), 1)

        def f_dve(dve, ch, n, st):
            m = MF
            g = lambda s: sm["F", s]

            def gate():
                dve.wait_ge(g("lg_exp"), 1)
                f2 = lambda t: m[t][:, :, :]
                ch.link(nc.vector.tensor_scalar(f2("sc"), f2("sc"), 1.0, None, ALU.add))
                ch.link(nc.vector.reciprocal(f2("sc"), f2("sc")))
                ch.link(nc.vector.tensor_tensor(f2("sb"), f2("sc"), spread(gateB[:, :], 1, [P, NI, NE]), ALU.add))
                by4 = m["sb"][:, :, :].rearrange("p i (g e) -> p (i g) e", e=4)
                c = lambda t, k: m[t][:, 0:NI * 8 * k * k if k == 4 else NI * 64].rearrange("p (a e f) -> p a e f", e=k, f=k)
                top_mask(ch, by4, NI * 8, 4, 2, c("c1", 4), c("c2", 4), m["m4"][:, :, :])
                ch.link(nc.vector.tensor_tensor(m["m4"][:, :, :], m["m4"][:, :, :], by4, ALU.mult))
                ch.link(nc.vector.tensor_reduce(m["gs"][:, :, :].rearrange("p i g -> p (i g)"), m["m4"][:, :, :], AX.X, ALU.add))
                top_mask(ch, m["gs"][:, :, :], NI, 8, 4, c("c1", 8), c("c2", 8), m["gm"][:, :, :])
                ch.link(nc.vector.tensor_tensor(m["mb"][:, :, :].rearrange("p i (g e) -> p (i g) e", e=4), by4,
                                                spread(m["gm"][:, :, :].rearrange("p i g -> p (i g)"), 2, [P, NI * 8, 4]), ALU.mult))
                for i in range(NI):
                    last = nc.vector.max(m["t8"][:, i, :], m["mb"][:, i, :])
                ch.link(last)
                for i in range(NI):
                    last = nc.vector.match_replace(m["rp"][:, i, :], m["t8"][:, i, :], m["mb"][:, i, :], -1e30)
                ch.link(last)
                ch.link(nc.vector.tensor_tensor(f2("rp"), f2("rp"), f2("mb"), ALU.is_lt))
                ch.link(nc.vector.tensor_tensor(f2("mb"), f2("rp"), f2("sc"), ALU.mult))
                ch.link(nc.vector.tensor_reduce(m["sum"][:, :], f2("mb"), AX.X, ALU.add))
                ch.link(nc.vector.tensor_scalar(m["sum"][:, :], m["sum"][:, :], 1e-20, None, ALU.add))
                ch.link(nc.vector.reciprocal(m["sum"][:, :], m["sum"][:, :]))
                ch.link(nc.vector.tensor_tensor(f2("mb"), f2("mb"), spread(m["sum"][:, :], 2, [P, NI, NE]), ALU.mult))
                ch.link(nc.vector.tensor_scalar(f2("mb"), f2("mb"), 2.5, None, ALU.mult))
                ch.link(nc.vector.tensor_copy(m["cp"][:, :, 0, :], f2("mb")))
                ch.link(nc.vector.tensor_tensor(f2("rest"), f2("mb"), m["cp"][:, :, 0, :], ALU.subtract))
                ch.link(nc.vector.tensor_copy(m["cp"][:, :, 1, :], f2("rest")))
                nc.vector.tensor_tensor(m["cp"][:, :, 2, :], f2("rest"), m["cp"][:, :, 1, :], ALU.subtract).then_inc(g("comb"), 1)

            gate()
            for e in range(NE + NSH):
                dve.wait_ge(g("silu"), e + 1)
                if e >= 2:
                    dve.wait_ge(g("down"), e - 1)
                if e < NSH:
                    nc.vector.tensor_tensor(m["gu"][:, e % 2, :], m["si"][:, e % 2, :], ps[:, 2 + e % 2, :], ALU.mult).then_inc(g("gu"), 1)
                else:
                    ch.link(nc.vector.tensor_tensor(m["tm"][:, :], m["si"][:, e % 2, :], ps[:, 2 + e % 2, :], ALU.mult))
                    nc.vector.tensor_tensor(m["gu"][:, e % 2, :], m["tm"][:, :], ps[:, 4 + e % 2, :], ALU.mult).then_inc(g("gu"), 1)
                    dve.wait_ge(g("gu"), e + 1)
            dve.wait_ge(g("down"), NE + NSH)
            for i in range(NI):
                ch.link(nc.vector.tensor_tensor(x[:, i, :], x[:, i, :], ps[:, 6 + i // 2, (i % 2) * DM:(i % 2 + 1) * DM], ALU.add))

        EXTRA["F"] = dict(pe=f_pe, act=f_act, dve=f_dve, pool=lambda *a: None, sp=f_sp)

        AH, AW = 16, 64
        SA_R = [4, 2, 1, 1]
        CH_ROWS = 4
        NCHUNK = NI * 16 // CH_ROWS
        BACK = 399
        sk = nc.dram_tensor("scores_kerple", (2 * AH, S, S), F32, kind="Internal").ap()
        named("A", "w", "qk_mm", "qk_up", "e_mm", "e_up", "out0", "out1", "cmb0", "cmb1", "fin0", "fin1", "fin2", "fin3",
              "w1", "gelu", "w2", "mixed", "negm", "exp", "prob", "tr", "pt_up", "pv", "ot_up", "y_mm", "y_up")
        KT_A = AH * AW // P
        AC = 5 * AH * AW

        def a1_mem(sb2):
            m = dict(both)
            m["w"] = sb2("a_w", [P, KD, AC])
            m["qk"] = sb2("a_qk", [P, 16, S])
            m["Ss"] = sb2("a_Ss", [P, 2, 4, S])
            m["t"] = sb2("a_t", [P, S])
            return m

        def a2_mem(sb2):
            m = dict(both)
            m["cmb"] = sb2("a_cmb", [P, 2, 2, CH_ROWS, S])
            m["fin"] = sb2("a_fin", [P, 4, CH_ROWS, S])
            m["hid"] = xn[:, :, :].rearrange("p (e a) c -> p e (a c)", e=2)
            m["PT"] = sb2("a_PT", [P, NI, 16, P])
            m["OT"] = spare[:, KT_A * DM:KT_A * (DM + P)].rearrange("p (t c) -> p t c", t=KT_A)
            m["nm"] = sb2("a_nm", [P, 4, CH_ROWS])
            m["den"] = sb2("a_den", [P, 4, CH_ROWS])
            return m

        def a_mem(sb2):
            both.update(V=sb2("a_V", [P, NI, AH * AW]), wo=spare[:, 0:KT_A * DM].rearrange("p (t c) -> p t c", t=KT_A))
            return scope(a1_mem), scope(a2_mem)

        spare = wbuf[:, 1, :]
        both = {}
        M1, M2 = scope(a_mem)

        def chunk(n):
            i, c = divmod(n, 4)
            return i, c, (i + 1) * P

        A_UNITS = [(n, f, q) for n in range(NCHUNK) for q in range(0, CH_ROWS, SA_R[n // 4]) for f in range(2)]
        UNITS_TO = [sum(u[0] < n for u in A_UNITS) for n in range(NCHUNK + 1)]
        TURNS_TO = [sum(chunk(k)[0] + 1 for k in range(n)) for n in range(NCHUNK + 1)]

        def a_sp(sp, _, n, st):
            g = lambda s: sm["A", s]
            sp.dma_start(M1["w"][:, :, :], io["wA"].rearrange("(k p) c -> p k c", p=P)).then_inc(g("w"), 16)
            sp.dma_start(M1["wo"][:, :, :], io["woA"].rearrange("(k p) c -> p k c", p=P)).then_inc(g("w"), 16)
            for grp in range(16):
                hq, i = divmod(grp, NI)
                L = (i + 1) * P
                sp.wait_ge(g("e_up"), 8 + 4 * (grp + 1))
                sp.dma_start(sk[4 * hq:4 * hq + 4, i * P:(i + 1) * P, 0:L].rearrange("h p j -> p h j"),
                             M1["Ss"][:, grp % 2, :, 0:L]).then_inc(g(f"out{grp % 2}"), 16)
            for k in range(2):
                sp.wait_ge(g(f"out{k}"), 8 * 16)
            st.end()
            for c in range(NCHUNK):
                i, q, L = chunk(c)
                if c >= 2:
                    sp.wait_ge(g("w1"), UNITS_TO[c - 1])
                rows = sk[:, i * P:(i + 1) * P, 0:L].rearrange("r (f g q) j -> g r f q j", f=2, g=4)
                for u in range(4):
                    for f in range(2):
                        sp.dma_start(M2["cmb"][32 * u:32 * u + 32, c % 2, f, :, 0:L],
                                     rows[u, :, f, CH_ROWS * q:CH_ROWS * (q + 1), :]).then_inc(g(f"cmb{c % 2}"), 16)
                if c >= 4:
                    sp.wait_ge(g("tr"), TURNS_TO[c - 3])
                rows = sk[0:AH, i * P:(i + 1) * P, 0:L].rearrange("h (g q) j -> g h q j", g=8)
                for u in range(8):
                    sp.dma_start(M2["fin"][16 * u:16 * u + 16, c % 4, :, 0:L],
                                 rows[u, :, CH_ROWS * q:CH_ROWS * (q + 1), :]).then_inc(g(f"fin{c % 4}"), 16)

        def a_pe(pe, _, n, st):
            g = lambda s: sm["A", s]
            m = M1
            pe.wait_ge(g("w"), 32)
            pe.wait_ge(ln_T, n + 1)
            HW = AH * AW
            for e in range(16):
                if e >= 2:
                    pe.wait_ge(g("qk_up"), e - 1)
                t, kind = divmod(e, 2)
                for v in range(2):
                    col = (2 * kind + v) * HW + t * P
                    for k in range(KD):
                        last = nc.tensor.matmul(ps[:, 2 * (e % 2) + v, :], m["w"][:, k, col:col + P], xnT[:, k, :],
                                                start=(k == 0), stop=(k == KD - 1))
                last.then_inc(g("qk_mm"), 1)
            for e in range(8):
                i, f = divmod(e, 2)
                if e >= 4:
                    pe.wait_ge(g("e_up"), e - 3)
                for k in range(KD):
                    last = nc.tensor.matmul(ps[:, 4 + e % 4, :], xnT[:, k, i * P:(i + 1) * P],
                                            m["w"][:, k, 4 * HW + f * BANK:4 * HW + (f + 1) * BANK], start=(k == 0), stop=(k == KD - 1))
                last.then_inc(g("e_mm"), 1)
            for s in range(64):
                e = 8 + s
                grp, hh = divmod(s, 4)
                hq, i = divmod(grp, NI)
                h = 4 * hq + hh
                pe.wait_ge(g("e_up"), e - 3)
                if i == 0:
                    pe.wait_ge(g("qk_up"), 2 * (h // 2 + 1))
                r = AW * (h % 2)
                nc.tensor.matmul(ps[:, 4 + e % 4, 0:(i + 1) * P], m["qk"][r:r + AW, 2 * (h // 2), i * P:(i + 1) * P],
                                 m["qk"][r:r + AW, 2 * (h // 2) + 1, 0:(i + 1) * P], start=True, stop=True).then_inc(g("e_mm"), 1)
            st.end()
            m = M2

            def up(k):
                c, f, q = A_UNITS[k]
                i, _, L = chunk(c)
                if k == UNITS_TO[c]:
                    pe.wait_ge(g(f"cmb{c % 2}"), 16 * 8 * (c // 2 + 1))
                if k >= 2:
                    pe.wait_ge(g("gelu"), k - 1)
                R = SA_R[i]
                nc.tensor.matmul(ps[:, k % 2, 0:R * L].rearrange("p (r l) -> p r l", r=R), w1A[:, :], m["cmb"][:, c % 2, f, q:q + R, 0:L],
                                 start=True, stop=True).then_inc(g("w1"), 1)

            def down(k):
                c, f, q = A_UNITS[k]
                i, _, L = chunk(c)
                w = k // 2
                pe.wait_ge(g("gelu"), k + 1)
                if w >= 2:
                    pe.wait_ge(g("mixed"), w - 1)
                nc.tensor.matmul(ps[64 * f:64 * f + 64, 2 + w % 2, 0:SA_R[i] * L], w2A[:, :], m["hid"][:, k % 2, 0:SA_R[i] * L],
                                 start=True, stop=True, tile_position=(0, 64 * f)).then_inc(g("w2"), 1)

            def turn(c, j):
                t = TURNS_TO[c] + j
                if j == 0:
                    pe.wait_ge(g("prob"), c + 1)
                if t >= 2:
                    pe.wait_ge(g("pt_up"), t - 1)
                for q in range(CH_ROWS):
                    last = nc.tensor.transpose(ps[:, 4 + t % 2, q * P:(q + 1) * P], m["fin"][:, c % 4, q, j * P:(j + 1) * P], ident[:, :])
                last.then_inc(g("tr"), 1)

            def weighted(i):
                pe.wait_ge(g("pt_up"), TURNS_TO[4 * (i + 1)])
                if i:
                    pe.wait_ge(g("y_up"), i)
                for h in range(AH):
                    r, t = AW * (h % 2), h // 2
                    for j in range(i + 1):
                        rhs = m["PT"][:, j, :, :].rearrange("p q (g h) -> p h g q", h=AH)[:, h]
                        o = ps[r:r + AW, 6 + t // 4, (t % 4) * P:(t % 4 + 1) * P].rearrange("p (g q) -> p g q", g=8)
                        last = nc.tensor.matmul(o, m["V"][:, j, h * AW:(h + 1) * AW], rhs, start=(j == 0), stop=(j == i), tile_position=(0, r))
                last.then_inc(g("pv"), 1)

            def project(i):
                pe.wait_ge(g("ot_up"), i + 1)
                for t in range(KT_A):
                    last = nc.tensor.matmul(ps[:, 6, 0:DM], m["OT"][:, t, :], m["wo"][:, t, :], start=(t == 0), stop=(t == KT_A - 1))
                last.then_inc(g("y_mm"), 1)

            for s in range(NCHUNK + 3):
                c = s - 2
                if s < NCHUNK:
                    for k in range(UNITS_TO[s], UNITS_TO[s + 1]):
                        up(k)
                        if k > UNITS_TO[s]:
                            down(k - 1)
                if 0 <= c < NCHUNK:
                    turn(c, 0)
                if s < NCHUNK:
                    down(UNITS_TO[s + 1] - 1)
                if s % 4 == 2 and s >= 6:
                    project(s // 4 - 1)
                if 0 <= c < NCHUNK:
                    for j in range(1, chunk(c)[0] + 1):
                        turn(c, j)
                if s % 4 == 1 and s >= 5:
                    weighted(s // 4 - 1)

        def a_act(act, _, n, st):
            g = lambda s: sm["A", s]
            m = M1
            for e in range(8):
                i, f = divmod(e, 2)
                act.wait_ge(g("e_mm"), e + 1)
                nc.scalar.activation(m["V"][:, i, f * BANK:(f + 1) * BANK], ps[:, 4 + e % 4, :], ACT.Copy).then_inc(g("e_up"), 1)
            for s in range(64):
                grp, hh = divmod(s, 4)
                i = grp % NI
                e = 8 + s
                act.wait_ge(g("e_mm"), e + 1)
                if grp >= 2 and hh == 0:
                    act.wait_ge(g(f"out{grp % 2}"), 16 * (grp // 2))
                nc.scalar.activation(m["Ss"][:, grp % 2, hh, 0:(i + 1) * P], ps[:, 4 + e % 4, 0:(i + 1) * P], ACT.Copy,
                                     scale=AW ** -0.5).then_inc(g("e_up"), 1)
            st.end()
            m = M2
            for s in range(NCHUNK + 1):
                if s < NCHUNK:
                    for k in range(UNITS_TO[s], UNITS_TO[s + 1]):
                        i, _, L = chunk(s)
                        w = SA_R[i] * L
                        act.wait_ge(g("w1"), k + 1)
                        if k >= 2:
                            act.wait_ge(g("w2"), k - 1)
                        nc.scalar.activation(m["hid"][:, k % 2, 0:w], ps[:, k % 2, 0:w], ACT.Gelu, bias=b1A[:, 0:1]).then_inc(g("gelu"), 1)
                if s:
                    c = s - 1
                    L = chunk(c)[2]
                    act.wait_ge(g("negm"), c + 1)
                    for q in range(CH_ROWS):
                        row = m["fin"][:, c % 4, q, 0:L]
                        nc.scalar.activation(row, row, ACT.Exp, bias=m["nm"][:, c % 4, q:q + 1],
                                             accum_out=m["den"][:, c % 4, q:q + 1]).then_inc(g("exp"), 1)

        def a_dve(dve, ch, n, st):
            g = lambda s: sm["A", s]
            m = M1
            for e in range(16):
                dve.wait_ge(g("qk_mm"), e + 1)
                b0 = 2 * (e % 2)
                ch.link(nc.vector.tensor_tensor(m["t"][:, :], ps[:, b0 + 1, :], sinA[:, :], ALU.mult))
                ch.link(nc.vector.tensor_tensor(m["qk"][:, e, :], ps[:, b0, :], cosA[:, :], ALU.mult))
                nc.vector.tensor_tensor(m["qk"][:, e, :], m["qk"][:, e, :], m["t"][:, :], ALU.add).then_inc(g("qk_up"), 1)
                dve.wait_ge(g("qk_up"), e + 1)
            st.end()
            m = M2
            for s in range(NCHUNK + 3):
                if s < NCHUNK:
                    i, c4, L = chunk(s)
                    R = SA_R[i]
                    slot = s % 4
                    dve.wait_ge(g(f"fin{slot}"), 16 * 8 * (s // 4 + 1))
                    for w in range(UNITS_TO[s] // 2, UNITS_TO[s + 1] // 2):
                        q0 = A_UNITS[2 * w][2]
                        dve.wait_ge(g("w2"), 2 * w + 2)
                        rows = m["fin"][:, slot, q0:q0 + R, 0:L]
                        nc.vector.tensor_tensor(rows, rows, ps[:, 2 + w % 2, 0:R * L].rearrange("p (r l) -> p r l", r=R), ALU.add).then_inc(g("mixed"), 1)
                        dve.wait_ge(g("mixed"), w + 1)
                        for q in range(q0, q0 + R):
                            row = m["fin"][:, slot, q, 0:L]
                            t0 = BACK - i * P - (CH_ROWS * c4 + q)
                            last = nc.vector.tensor_tensor(row, row, biasA[:, t0:t0 + L], ALU.add)
                        ch.link(last)
                    ch.link(nc.vector.tensor_reduce(m["nm"][:, slot, :], m["fin"][:, slot, :, 0:L], AX.X, ALU.max))
                    nc.vector.tensor_scalar(m["nm"][:, slot, :], m["nm"][:, slot, :], -1.0, None, ALU.mult).then_inc(g("negm"), 1)
                if 1 <= s <= NCHUNK:
                    c = s - 1
                    slot, L = c % 4, chunk(c)[2]
                    dve.wait_ge(g("exp"), CH_ROWS * (c + 1))
                    ch.link(nc.vector.reciprocal(m["den"][:, slot, :], m["den"][:, slot, :]))
                    for q in range(CH_ROWS):
                        row = m["fin"][:, slot, q, 0:L]
                        last = nc.vector.tensor_scalar(row, row, m["den"][:, slot, q:q + 1], None, ALU.mult)
                    last.then_inc(g("prob"), 1)
                if 2 <= s < NCHUNK + 2:
                    c = s - 2
                    i, c4, L = chunk(c)
                    for j in range(i + 1):
                        t = TURNS_TO[c] + j
                        dve.wait_ge(g("tr"), t + 1)
                        nc.vector.tensor_copy(m["PT"][:, j, CH_ROWS * c4:CH_ROWS * (c4 + 1), :],
                                              ps[:, 4 + t % 2, :].rearrange("p (q c) -> p q c", q=CH_ROWS)).then_inc(g("pt_up"), 1)
                if s % 4 == 1 and s >= 5:
                    dve.wait_ge(g("pv"), s // 4)
                    if s > 5:
                        dve.wait_ge(g("y_mm"), s // 4 - 1)
                    for f in range(2):
                        last = nc.vector.tensor_copy(m["OT"][:, 4 * f:4 * f + 4, :], ps[:, 6 + f, :].rearrange("p (t q) -> p t q", t=4))
                    last.then_inc(g("ot_up"), 1)
                if s % 4 == 2 and s >= 6:
                    i = s // 4 - 1
                    dve.wait_ge(g("y_mm"), i + 1)
                    nc.vector.tensor_tensor(x[:, i, :], x[:, i, :], ps[:, 6, 0:DM], ALU.add).then_inc(g("y_up"), 1)

            dve.wait_ge(g("y_up"), NI)

        EXTRA["A"] = dict(pe=a_pe, act=a_act, dve=a_dve, pool=lambda pool, ch, n, st: st.end(), sp=a_sp)

        def ker_mem(sb2):
            m = dict(pad=sb2("k_pad", [P, 9400]))
            for t in ("lp", "la", "b2", "e", "r"):
                m[t] = sb2("k_" + t, [P, 2])
            m["dist"] = sb2("k_dist", [P, NWIN])
            m["ahead"] = sb2("k_ahead", [P, NWIN])
            m["kt"] = sb2("k_kt", [P, NWIN])
            return m

        MK = scope(ker_mem)
        kt_ready = ctx.enter_context(nc.semaphore("kt_ready"))
        kt_act = ctx.enter_context(nc.semaphore("kt_act"))
        kt_dve = ctx.enter_context(nc.semaphore("kt_dve"))
        kt_out = ctx.enter_context(nc.semaphore("kt_out"))
        N_SETUP = 21

        def more_sp(sp):
            sp.dma_start(gateW[:, :, :], io["gateW"].rearrange("(k p) e -> p k e", p=P)).then_inc(setup_loaded, 16)
            sp.dma_start(gateB[:, :], io["gateB"].partition_broadcast(P)).then_inc(setup_loaded, 16)
            for t, n in ((w1A, "w1A"), (w2A, "w2A"), (b1A, "b1A"), (cosA, "cosA"), (sinA, "sinA"), (MK["lp"][:, 0:1], "lp"),
                         (MK["lp"][:, 1:2], "la"), (MK["b2"][:, 0:1], "b2"), (MK["dist"], "dist"), (MK["ahead"], "ahead")):
                sp.dma_start(t if len(n) == 2 else t[:, :], io[n]).then_inc(setup_loaded, 16)
            if "A" in STAGES:
                sp.wait_ge(kt_ready, 1)
                for i in range(NI):
                    L = (i + 1) * P
                    rows = sk[AH:2 * AH, i * P:(i + 1) * P, 0:L].rearrange("h (g q) j -> g h q j", g=8)
                    for q in range(16):
                        t0 = BACK - i * P - q
                        sp.dma_start(rows[:, :, q, :], MK["kt"][:, t0:t0 + L]).then_inc(kt_out, 16)
                sp.wait_ge(kt_out, 16 * 64)

        def more_dve(dve):
            m = MK
            n = [0]

            def link(ins):
                n[0] += 1
                ins.then_inc(kt_dve, 1)
                dve.wait_ge(kt_dve, n[0])

            link(nc.vector.tensor_scalar(m["e"][:, :], m["lp"][:, :], -1.0, None, ALU.mult))
            link(nc.vector.tensor_tensor(m["e"][:, :], m["e"][:, :], m["lp"][:, :], ALU.min))
            dve.wait_ge(kt_act, 2)
            link(nc.vector.tensor_scalar(m["r"][:, :], m["lp"][:, :], 0.0, None, ALU.max))
            link(nc.vector.tensor_tensor(m["r"][:, :], m["r"][:, :], m["la"][:, :], ALU.add))
            link(nc.vector.tensor_scalar(m["e"][:, 0:1], m["r"][:, 0:1], -1.0, None, ALU.mult))
            dve.wait_ge(kt_act, 3)
            nc.vector.tensor_scalar(m["kt"][:, :], m["kt"][:, :], m["e"][:, 0:1], None, ALU.mult).then_inc(kt_ready, 1)
            dve.wait_ge(kt_ready, 1)
            nc.vector.scalar_tensor_tensor(out=biasA[:, :], in0=m["kt"][:, :], scalar=m["b2"][:, 0:1], in1=m["ahead"][:, :],
                                           op0=ALU.add, op1=ALU.add)

        def more_act(act):
            m = MK
            act.wait_ge(kt_dve, 2)
            nc.scalar.activation(m["la"][:, :], m["e"][:, :], ACT.Exp).then_inc(kt_act, 1)
            act.wait_ge(kt_act, 1)
            nc.scalar.activation(m["la"][:, :], m["la"][:, :], ACT.Ln, bias=1.0).then_inc(kt_act, 1)
            act.wait_ge(kt_dve, 4)
            nc.scalar.activation(m["kt"][:, :], m["dist"][:, :], ACT.Ln, bias=1.0, scale=m["r"][:, 1:2]).then_inc(kt_act, 1)

        def more_pool(pool):
            nc.gpsimd.memset(tri[:, :, :], 1.0).then_inc(setup_pool_sem, 1)
            nc.gpsimd.memset(selE[:, :, :], 0.0).then_inc(setup_pool_sem, 1)
            pool.wait_ge(setup_pool_sem, 10)
            nc.gpsimd.affine_select(out=tri[:, :, :], in_=tri[:, :, :], compare_op=ALU.is_ge, fill=0.0,
                                    base=-1, pattern=[[1, 8], [-1, 8]], channel_multiplier=0).then_inc(setup_pool_sem, 1)
            for a in range(3):
                nc.gpsimd.affine_select(out=selE[:, :, :], in_=selE[:, :, :], compare_op=ALU.not_equal, fill=1.0,
                                        base=-NE * a, pattern=[[-1, NE], [0, P]], channel_multiplier=1).then_inc(setup_pool_sem, 1)
                pool.wait_ge(setup_pool_sem, 12 + a)

        SETUP_MORE.update(sp=more_sp, pool=more_pool, dve=more_dve, act=more_act)

        def setup_mem(sb2):
            return dict(mi=sb2("mi", [P, NI, CTX], I32), mt=sb2("mt", [P, CTX // P, S], I32), dg=sb2("dg", [P, S]),
                        ones=sb2("ones", [P, P]), cf=sb2("cf", [P, 2, P]), mm=sb2("mm", [P, NI]))

        SU = scope(setup_mem)

        def setup_sp(sp):
            sp.dma_start(SU["mi"][:, :, :], io["mask"].rearrange("(i p) j -> p i j", p=P)).then_inc(setup_loaded, 16)
            sp.dma_start(SU["mt"][:, :, :], io["maskT"].rearrange("(j p) i -> p j i", p=P)).then_inc(setup_loaded, 16)
            for t, n in ((cosD, "cosD"), (sinD, "sinD"), (bqE, "bqE"), (bkE, "bkE")):
                sp.dma_start(t[:, :], io[n]).then_inc(setup_loaded, 16)
            for t, n in ((boB, "boB"), (bvE, "bvE"), (boE, "boE")):
                sp.dma_start(t[:, :], io[n].partition_broadcast(P)).then_inc(setup_loaded, 16)
            SETUP_MORE["sp"](sp)

        def setup_pool(pool):
            nc.gpsimd.memset(half[:, :], -0.5)
            for t in (ident, selden, SU["cf"][:, 0, :], SU["cf"][:, 1, :]):
                nc.gpsimd.memset(t[:, :] if t is ident or t is selden else t, 0.0).then_inc(setup_pool_sem, 1)
            pool.wait_ge(setup_pool_sem, 4)
            nc.gpsimd.affine_select(out=ident[:, :], in_=ident[:, :], compare_op=ALU.not_equal, fill=1.0,
                                    base=0, pattern=[[-1, P]], channel_multiplier=1).then_inc(setup_pool_sem, 1)
            sv = selden[:, :].rearrange("p (a b) -> p a b", a=4)
            nc.gpsimd.affine_select(out=sv, in_=sv, compare_op=ALU.not_equal, fill=1.0,
                                    base=-HD, pattern=[[-32, 4], [0, 32]], channel_multiplier=1).then_inc(setup_pool_sem, 1)
            nc.gpsimd.affine_select(out=SU["cf"][:, 0, :], in_=SU["cf"][:, 0, :], compare_op=ALU.is_ge, fill=NEG,
                                    base=0, pattern=[[-1, P]], channel_multiplier=1).then_inc(setup_pool_sem, 1)
            nc.gpsimd.affine_select(out=SU["cf"][:, 1, :], in_=SU["cf"][:, 1, :], compare_op=ALU.is_ge, fill=NEG,
                                    base=0, pattern=[[1, P]], channel_multiplier=-1).then_inc(setup_pool_sem, 1)
            SETUP_MORE["pool"](pool)

        def setup_vector(dve):
            nc.vector.memset(SU["ones"][:, :], 1.0)
            dve.wait_ge(setup_pool_sem, 8)
            nc.vector.tensor_copy(identb[:, :], ident[:, :])
            nc.vector.tensor_copy(caus[:, :], SU["cf"][:, 0, :])
            nc.vector.tensor_copy(causT[:, :], SU["cf"][:, 1, :])
            dve.wait_ge(setup_loaded, N_SETUP * 16)
            nc.vector.tensor_scalar(mneg[:, :, :], SU["mi"][:, :, :], 0.0, MASKED, ALU.is_equal, ALU.mult).then_inc(setup_dve, 1)
            nc.vector.tensor_scalar(mnegT[:, :, :], SU["mt"][:, :, :], 0.0, MASKED, ALU.is_equal, ALU.mult).then_inc(setup_dve, 1)
            dve.wait_ge(setup_dve, 2)
            nc.vector.tensor_reduce(SU["mm"][:, :], mneg[:, :, :], AX.X, ALU.max).then_inc(setup_dve, 1)
            dve.wait_ge(setup_dve, 3)
            nc.vector.tensor_scalar(livec[:, :], SU["mm"][:, :], -1.0, None, ALU.is_ge).then_inc(setup_dve, 1)
            dve.wait_ge(setup_dve, 4)
            for i in range(NI):
                nc.vector.tensor_scalar(SU["dg"][:, i * P:(i + 1) * P], ident[:, :], livec[:, i:i + 1], None, ALU.mult).then_inc(setup_dve, 1)
                nc.vector.tensor_scalar(mneg[:, i, :], mneg[:, i, :], livec[:, i:i + 1], None, ALU.mult)
            dve.wait_ge(setup_act, 1)
            for j in range(CTX // P):
                nc.vector.tensor_tensor(mnegT[:, j, :], mnegT[:, j, :], live[:, :], ALU.mult)
            SETUP_MORE["dve"](dve)

        def setup_pe(pe):
            pe.wait_ge(setup_dve, 4 + NI)
            nc.tensor.matmul(ps[:, 0, :], SU["ones"][:, :], SU["dg"][:, :], start=True, stop=True).then_inc(setup_pe_sem, 1)

        def setup_scalar(act):
            act.wait_ge(setup_pe_sem, 1)
            nc.scalar.activation(live[:, :], ps[:, 0, :], ACT.Copy).then_inc(setup_act, 1)
            SETUP_MORE["act"](act)

        block = ctx.enter_context(nc.Block())
        SETUP_PHASES = 3

        def load_weights(sp, s):
            sp.dma_start(W(s, 0, WIDTH[s]), io["w" + s]).then_inc(w_loaded[s], 16)

        @block.sync
        def _(sp):
            st = Steps(sp, bars, True)
            setup_sp(sp)
            for _ in range(SETUP_PHASES):
                st.end()
            with sp.Fori(0, rounds) as b:
                sp.dma_start(x[:, :, :], io["x"][bass.ds(b, 1), :, :].rearrange("o (t p) d -> p (o t) d", p=P)).then_inc(x_loaded, 16)
                if ORDER:
                    load_weights(sp, ORDER[0])
                sp.dma_start(ctxT[:, :, :], io["ctxT"][bass.ds(b, 1), :, :].rearrange("o (k p) j -> p (o k) j", p=P)).then_inc(x_loaded, 16)
                for n, s in enumerate(STAGES):
                    if s in ORDER and ORDER.index(s) + 1 < len(ORDER):
                        load_weights(sp, ORDER[ORDER.index(s) + 1])
                    if s in CFG:
                        a16_sp(sp, CFG[s])
                    else:
                        EXTRA[s]["sp"](sp, None, n, st)
                    st.end()
                sp.dma_start(out[bass.ds(b, 1), :, :].rearrange("o (t p) d -> p (o t) d", p=P), x[:, :, :]).then_inc(x_stored, 16)
                sp.wait_ge(x_stored, 16)
                st.end_round(counting)

        @block.gpsimd
        def _(pool):
            st = Steps(pool, bars, False)
            setup_pool(pool)
            for _ in range(SETUP_PHASES):
                st.end()
            with pool.Fori(0, rounds) as b:
                ch = Chain(pool, pool_chain)
                for n, s in enumerate(STAGES):
                    ln_pool(pool, n)
                    if s in CFG:
                        a16_pool(pool, ch, CFG[s])
                    else:
                        EXTRA[s]["pool"](pool, ch, n, st)
                    st.end()
                st.end_round()

        @block.scalar
        def _(act):
            st = Steps(act, bars, False)
            setup_scalar(act)
            for _ in range(SETUP_PHASES):
                st.end()
            with act.Fori(0, rounds) as b:
                for n, s in enumerate(STAGES):
                    ln_act(act, n)
                    if s in CFG:
                        a16_act(act, CFG[s])
                    else:
                        EXTRA[s]["act"](act, None, n, st)
                    st.end()
                st.end_round()

        @block.vector
        def _(dve):
            st = Steps(dve, bars, False)
            setup_vector(dve)
            for _ in range(SETUP_PHASES):
                st.end()
            with dve.Fori(0, rounds) as b:
                ch = Chain(dve, dve_chain)
                dve.wait_ge(x_loaded, 32)
                for n, s in enumerate(STAGES):
                    ln_dve(dve, ch, n)
                    if s in CFG:
                        a16_dve(dve, ch, CFG[s])
                    else:
                        EXTRA[s]["dve"](dve, ch, n, st)
                    st.end()
                st.end_round()

        @block.tensor
        def _(pe):
            st = Steps(pe, bars, False)
            setup_pe(pe)
            for _ in range(SETUP_PHASES):
                st.end()
            with pe.Fori(0, rounds) as b:
                for n, s in enumerate(STAGES):
                    ln_pe(pe, n)
                    if s in CFG:
                        a16_pe(pe, CFG[s], n)
                    else:
                        EXTRA[s]["pe"](pe, None, n, st)
                    st.end()
                st.end_round()


def lay_out_more(d, a, ktiles):
    import numpy as np

    wo = a["L0_ffn_Wo"].reshape(320, DM)
    wop = np.zeros((3 * P, DM), wo.dtype)
    wop[:320] = wo
    d["wC"] = np.concatenate([ktiles(w) for w in (a["L0_ffn_Wq"], a["L0_ffn_Wk"],
                                                  np.concatenate([a["L0_ffn_Ws"], a["L0_ffn_Wd"]], 1),
                                                  a["L0_ffn_Wv"].transpose(1, 0, 2).reshape(DM, 320), wop)], 1)
    gate = np.concatenate([a["L1_ffn_sh_gate"].reshape(2, P, DM), a["L1_ffn_w_gate"]])
    up = np.concatenate([a["L1_ffn_sh_up"].reshape(2, P, DM), a["L1_ffn_w_up"]])
    down = np.concatenate([a["L1_ffn_sh_down"].reshape(DM, 2, P).transpose(1, 0, 2), a["L1_ffn_w_down"]])

    def feature_rows(w):
        return w.transpose(0, 2, 1).reshape(-1, KD, P, P).transpose(0, 2, 1, 3).reshape(-1, P, DM)

    d["wF"] = np.concatenate([feature_rows(gate), feature_rows(up), down.transpose(0, 2, 1)], 2)
    d["gateW"] = a["L1_ffn_gate_w"].T
    d["gateB"] = a["L1_ffn_gate_bias"]

    H, D = 16, 64
    wq, wk, wv = (a["L0_attn_w_qkv"][:, n * H * D:(n + 1) * H * D] for n in range(3))
    rot = (np.arange(H * D) // D) * D + (np.arange(H * D) + D // 2) % D
    d["wA"] = np.concatenate([wq, wq[:, rot], wk, wk[:, rot], wv], 1)
    d["woA"] = a["L0_attn_w_o"]
    w1, w2 = np.zeros((4, 32, 4, 32), np.float32), np.zeros((4, 32, 4, 16), np.float32)
    for g in range(4):
        w1[g, :, g], w2[g, :, g] = a["L0_attn_w1"], a["L0_attn_w2"]
    d["w1A"], d["w2A"] = w1.reshape(P, P), w2.reshape(P, 64)
    d["b1A"] = np.tile(a["L0_attn_b1"], 4).reshape(P, 1)
    d["lp"], d["la"], d["b2"] = (np.tile(a["L0_attn_" + n].reshape(-1), 8).reshape(P, 1) for n in ("log_p", "log_a", "b2"))
    d["cosA"], d["sinA"] = rope_half_tables()
    off = 399 + 16 * (np.arange(P)[:, None] // 16) - np.arange(528)[None, :]
    d["dist"] = np.abs(off).astype(np.float32)
    d["ahead"] = np.where(off < 0, np.float32(NEG), np.float32(0))


def lay_out(i):
    import numpy as np

    def ktiles(w):
        k = w.shape[0] // P
        return w.reshape(k, P, w.shape[1]).transpose(1, 0, 2).reshape(P, -1)

    def padded_out(w):
        q = np.zeros((NH, 32, w.shape[1]), w.dtype)
        q[:, :HD, :] = w.reshape(NH, HD, -1)
        return ktiles(q.reshape(NH * 32, -1))

    a = {k: np.asarray(v) for k, v in i.items()}
    swap = np.arange(DM) ^ 1
    d = {}
    d["x"] = a["x"]
    d["ctxT"] = a["ctx_1024"].transpose(0, 2, 1)
    mask = a["mask_1x1xSxS2_ik0"][0, 0]
    d["mask"], d["maskT"] = mask, mask.T
    d["cosD"], d["sinD"] = rope_pair_tables()
    d["wB"] = np.concatenate([ktiles(a["L0_xattn_" + n].T) for n in ("Wq", "Wk", "Wv")] + [padded_out(a["L0_xattn_Wo"].T)], 1)
    d["boB"] = a["L0_xattn_bo"]
    wd = a["L1_attn_W_qkv"]
    q, k, v = wd[:DM], wd[DM:2 * DM], wd[2 * DM:]
    d["wD"] = np.concatenate([ktiles(w.T) for w in (q, q[swap], k, k[swap], v)] + [padded_out(a["L1_attn_W_o"].T)], 1)
    d["wE"] = np.concatenate([ktiles(a["L1_xattn_" + n].T) for n in ("w_q", "w_k", "w_v")] + [padded_out(a["L1_xattn_w_o"].T)], 1)
    d["bqE"] = a["L1_xattn_b_q"].reshape(2, P).T
    d["bkE"] = a["L1_xattn_b_k"].reshape(2, P).T
    d["bvE"], d["boE"] = a["L1_xattn_b_v"], a["L1_xattn_b_o"]
    lay_out_more(d, a, ktiles)
    return {n: np.ascontiguousarray(v) for n, v in d.items()}


def kernel(**inputs):
    import concourse.bacc as _bacc
    from concourse import mybir as _mybir
    from concourse.bass_utils import run_bass_kernel_spmd as _run

    nc = _bacc.Bacc("TRN2", target_bir_lowering=False, num_devices=1)
    arrays, io = {}, {}
    for name, a in lay_out(inputs).items():
        arrays[f"in_{name}"] = a
        io[name] = nc.dram_tensor(f"in_{name}", a.shape, _mybir.dt.from_np(a.dtype), kind="ExternalInput").ap()
    out = nc.dram_tensor("out_0", (B, S, DM), _mybir.dt.float32, kind="ExternalOutput").ap()
    decoder(nc, io, out, B)
    r = _run(nc, [arrays], core_ids=[0])
    return r.results[0]["out_0"]
```

```python
import numpy as np
import concourse.bass as bass
from concourse import mybir
from contextlib import ExitStack

F32 = mybir.dt.float32
BF16 = mybir.dt.bfloat16
I32 = mybir.dt.int32
ALU = mybir.AluOpType
ACT = mybir.ActivationFunctionType
AX = mybir.AxisListType

P = 128
B, S, DM = 4, 512, 256
NI = S // P
KD = DM // P
CTX = 1024
BANK = 512
NEG = -1e30
MASKED = -float(2 ** 30)
STAGES = "ABCDEF"


def rope_half_tables():
    d = 64
    inv = (1.0 / 10000.0 ** (np.arange(0, d, 2, dtype=np.float32) / np.float32(d))).astype(np.float32)
    ang = np.outer(np.arange(S, dtype=np.float32), inv).astype(np.float32)
    ang = np.concatenate([ang, ang], -1).T
    cos, sin = np.cos(ang.astype(np.float64)), np.sin(ang.astype(np.float64))
    sin[: d // 2] = -sin[: d // 2]
    return np.tile(cos, (2, 1)).astype(np.float32), np.tile(sin, (2, 1)).astype(np.float32)


def rope_pair_tables():
    d = 16
    inv = (np.float32(10000.0) ** (np.arange(0, d, 2, dtype=np.float32) / np.float32(d))).astype(np.float32)
    ang = (np.arange(S, dtype=np.float32)[:, None] / inv[None, :]).astype(np.float32)
    ang = np.repeat(ang, 2, axis=1).T
    cos, sin = np.cos(ang.astype(np.float64)), np.sin(ang.astype(np.float64))
    sin[0::2] = -sin[0::2]
    return np.tile(cos, (8, 1)).astype(np.float32), np.tile(sin, (8, 1)).astype(np.float32)


class Chain:

    def __init__(self, eng, sem):
        self.eng, self.sem, self.n = eng, sem, 0

    def link(self, ins):
        self.n += 1
        ins.then_inc(self.sem, 1)
        self.eng.wait_ge(self.sem, self.n)


class Steps:

    def __init__(self, eng, bars, clears):
        self.eng, self.bars, self.clears, self.k = eng, bars, clears, 0

    def end(self):
        k = self.k % 3
        self.k += 1
        self.eng.drain().then_inc(self.bars[k], 1)
        self.eng.wait_ge(self.bars[k], 5)
        if self.clears:
            self.eng.sem_clear(self.bars[(k - 1) % 3])

    def end_round(self, sems=()):
        self.end()
        if self.clears:
            for s in sems:
                self.eng.sem_clear(s)
        self.end()
        while self.k % 3:
            self.end()


class Attn16:

    def __init__(self, name, nk, causal, masked, rope, cross):
        self.name, self.nk, self.causal, self.masked, self.rope, self.cross = name, nk, causal, masked, rope, cross
        self.nj = nk // P
        self.halves = nk // BANK
        self.tiles = [("q", t, 0) for t in range(2)] + [("k", t, f) for t in range(2) for f in range(self.halves)]
        if causal:
            self.s_tiles = [(i, 0, (i + 1) * P) for i in range(NI)]
            self.units = [[j] for j in range(self.nj)]
        else:
            self.s_tiles = [(i, f * BANK, BANK) for i in range(NI) for f in range(self.halves)]
            self.units = [[2 * u, 2 * u + 1] for u in range(self.nj // 2)]


NH = 16
HD = 16
NE, NSH = 32, 2
NRING = 6
CB = Attn16("B", CTX, False, False, False, True)
CD = Attn16("D", S, True, False, True, False)
CE = Attn16("E", CTX, False, True, False, True)
CFG = {"B": CB, "D": CD, "E": CE}
QPART = [0, 0, 1, 0, 1, 2]
KPART = [0, 1, 0, 2, 1, 0]
KR = 6 * HD
KST = KR + 3
Y_BANKS = [0, 1, 4, 5]


def decoder(nc, io, out, rounds=B):
    ctx = ExitStack()
    with ctx:
        def sb(name, shape, dt=F32):
            return ctx.enter_context(nc.sbuf_tensor(name, shape, dt))

        def sem(name):
            s = ctx.enter_context(nc.semaphore(name))
            counting.append(s)
            return s

        counting = []

        x = sb("x", [P, NI, DM])
        xn = sb("xn", [P, NI, DM])
        xnT = sb("xnT", [P, KD, S])
        ctxT = sb("ctxT", [P, KD, CTX])
        ident = sb("ident", [P, P])
        identb = sb("identb", [P, P], BF16)
        caus = sb("caus", [P, P], BF16)
        causT = sb("causT", [P, P], BF16)
        selden = sb("selden", [P, P])
        mneg = sb("mneg", [P, NI, CTX], BF16)
        mnegT = sb("mnegT", [P, CTX // P, S], BF16)
        live = sb("live", [P, S])
        livec = sb("livec", [P, NI])
        half = sb("half", [P, NI])
        st6 = sb("st6", [P, NI, 6])
        mv = sb("mv", [P, NI, 2])
        rstd = sb("rstd", [P, NI])
        rt = sb("rt", [P, NI])
        cosD = sb("cosD", [P, S])
        sinD = sb("sinD", [P, S])
        boB = sb("boB", [P, DM])
        bvE = sb("bvE", [P, DM])
        boE = sb("boE", [P, DM])
        bqE = sb("bqE", [P, 2])
        bkE = sb("bkE", [P, 2])
        tri = sb("tri", [P, 8, 8])
        selE = sb("selE", [96, NE, P], BF16)
        gateW = sb("gateW", [P, KD, NE])
        gateB = sb("gateB", [P, NE])
        NWIN = 528
        biasA = sb("biasA", [P, NWIN])
        w1A = sb("w1A", [P, P])
        w2A = sb("w2A", [P, 64])
        b1A = sb("b1A", [P, 1])
        cosA = sb("cosA", [P, S])
        sinA = sb("sinA", [P, S])
        WCOLS = 3712
        wbuf = sb("wbuf", [P, 2, WCOLS])
        ps = ctx.enter_context(nc.psum_tensor("ps", [P, 8, BANK], F32))

        bars = [ctx.enter_context(nc.semaphore(f"phase{k}")) for k in range(3)]
        setup_loaded = ctx.enter_context(nc.semaphore("setup_loaded"))
        setup_dve = ctx.enter_context(nc.semaphore("setup_dve"))
        setup_pool_sem = ctx.enter_context(nc.semaphore("setup_pool"))
        setup_pe_sem = ctx.enter_context(nc.semaphore("setup_pe"))
        setup_act = ctx.enter_context(nc.semaphore("setup_act"))
        ctx_loaded = sem("ctx_loaded")
        x_stored = sem("x_stored")
        dve_chain = sem("dve_chain")
        pool_chain = sem("pool_chain")
        ln_var = sem("ln_var")
        ln_pow = sem("ln_pow")
        ln_xn = sem("ln_xn")
        ln_tr = sem("ln_tr")
        ln_T = sem("ln_T")
        w_loaded = {s: sem(f"w_loaded_{s}") for s in "BCDE"}
        sm = {}
        for c in CFG:
            if c in STAGES:
                for n in ("proj", "val", "split", "v_mm", "v_up", "v_zero", "part_out", "stack_in", "s_mm", "s_max",
                          "m_parts", "m_mm", "m_row", "st_mm", "exp", "pv", "o_up", "den_mm", "den_up", "recip", "o_norm", "y_mm"):
                    sm[c, n] = sm["B", n] if c == "D" and "B" in STAGES else sem(f"{n}_{c}")

        def scope(fn):
            with ExitStack() as inner:
                return fn(lambda name, shape, dt=F32: inner.enter_context(nc.sbuf_tensor(name, shape, dt)))

        def attn16_mem(sb2):
            m = {}
            m["QS"] = sb2("QS", [P, NH, S], BF16)
            m["KS"] = sb2("KS", [P, NH, CTX], BF16)
            m["VP"] = sb2("VP", [P, CTX // P, NH, 32])
            m["QP"] = sb2("QP", [P, 3, 2, S], BF16)
            m["KP"] = sb2("KP", [P, 3, 2, CTX], BF16)
            m["val"] = sb2("val", [P, 2, BANK])
            m["rope"] = sb2("rope", [P, BANK])
            m["rest"] = sb2("rest", [P, BANK])
            m["mx"] = sb2("mx", [P, 2, NI, 2])
            m["nm"] = sb2("nm", [P, NI])
            m["nr"] = sb2("nr", [P, NI])
            m["nmp"] = sb2("nmp", [P, 2, NI, 3], BF16)
            m["PT"] = sb2("PT", [P, 2, 2, BANK])
            m["OT"] = sb2("OT", [P, 4, S])
            m["rec"] = sb2("rec", [P, BANK])
            m["den"] = m["rope"]
            m["ON"] = sb2("ON", [P, 4, S])
            return m

        M16 = scope(attn16_mem)
        qd = nc.dram_tensor("qparts", (3, 2, P, S), BF16, kind="Internal").ap()
        kd = nc.dram_tensor("kparts", (3, 2, P, CTX), BF16, kind="Internal").ap()

        WIDTH = {"B": 2560, "D": 3584, "E": 2560, "C": 3616}
        ORDER = [s for s in "BCDE" if s in STAGES]
        slot_of = {s: n % 2 for n, s in enumerate(ORDER)}

        def W(stage, first, cols):
            return wbuf[:, slot_of[stage], first:first + cols]

        def ln_dve(dve, ch, n):
            for i in range(NI):
                last = nc.vector.bn_stats(out=st6[:, i, :], in_=x[:, i, :])
            ch.link(last)
            for i in range(NI):
                last = nc.vector.bn_aggr(out=mv[:, i, :], in_=st6[:, i, :])
            ch.link(last)
            nc.vector.tensor_scalar(mv[:, :, 1], mv[:, :, 1], 1e-5, None, ALU.add).then_inc(ln_var, 1)
            dve.wait_ge(ln_pow, n + 1)
            ch.link(nc.vector.tensor_tensor(rt[:, :], rstd[:, :], rstd[:, :], ALU.mult))
            ch.link(nc.vector.tensor_tensor(rt[:, :], rt[:, :], mv[:, :, 1], ALU.mult))
            ch.link(nc.vector.tensor_scalar(rt[:, :], rt[:, :], -0.5, 1.5, ALU.mult, ALU.add))
            ch.link(nc.vector.tensor_tensor(rstd[:, :], rstd[:, :], rt[:, :], ALU.mult))
            for i in range(NI):
                nc.vector.tensor_scalar(xn[:, i, :], x[:, i, :], mv[:, i, 0:1], rstd[:, i:i + 1],
                                        ALU.subtract, ALU.mult).then_inc(ln_xn, 1)

        def ln_pool(pool, n):
            pool.wait_ge(ln_var, n + 1)
            nc.gpsimd.tensor_tensor(rstd[:, :], mv[:, :, 1], half[:, :], ALU.pow).then_inc(ln_pow, 1)

        def ln_pe(pe, n):
            for i in range(NI):
                pe.wait_ge(ln_xn, NI * n + i + 1)
                for k in range(KD):
                    last = nc.tensor.transpose(ps[:, k, i * P:(i + 1) * P], xn[:, i, k * P:(k + 1) * P], ident[:, :])
            last.then_inc(ln_tr, 1)

        def ln_act(act, n):
            act.wait_ge(ln_tr, n + 1)
            for k in range(KD):
                last = nc.scalar.activation(xnT[:, k, :], ps[:, k, :], ACT.Copy)
            last.then_inc(ln_T, 1)

        def a16_sp(sp, c):
            m = M16
            g = lambda n: sm[c.name, n]
            nq = 2
            sp.wait_ge(g("split"), nq)
            sp.dma_start(qd.rearrange("a t p n -> p (a t) n"), m["QP"][:, :, :, :].rearrange("p a t n -> p (a t) n")).then_inc(g("part_out"), 16)
            sp.wait_ge(g("part_out"), 16)
            for r in range(6):
                src = qd[QPART[r]].rearrange("t (e d) n -> d (t e) n", d=HD)
                sp.dma_start(m["QS"][HD * r:HD * r + HD, :, :], src).then_inc(g("stack_in"), 16)
            sp.wait_ge(g("split"), len(c.tiles))
            for a in range(3):
                sp.dma_start(kd[a, :, :, 0:c.nk].rearrange("t p n -> p t n"), m["KP"][:, a, :, 0:c.nk]).then_inc(g("part_out"), 16)
            sp.wait_ge(g("part_out"), 64)
            for r in range(6):
                src = kd[KPART[r], :, :, 0:c.nk].rearrange("t (e d) n -> d (t e) n", d=HD)
                sp.dma_start(m["KS"][HD * r:HD * r + HD, :, 0:c.nk], src).then_inc(g("stack_in"), 16)

        def a16_pool(pool, ch, c):
            m = M16
            ch.link(nc.gpsimd.memset(m["VP"][:, :, :, :], 0.0))
            ch.link(nc.gpsimd.memset(m["VP"][:, :, :, HD:HD + 1], 1.0))
            nc.gpsimd.memset(m["KS"][KR:KST, :, 0:c.nk], 1.0).then_inc(sm[c.name, "v_zero"], 1)
            for q in range(3):
                pool.wait_ge(sm[c.name, "recip"], NI * (q + 1))
                nc.gpsimd.tensor_tensor(m["ON"][:, q, :], m["OT"][:, q, :], m["rec"][:, :], ALU.mult).then_inc(sm[c.name, "o_norm"], 1)

        def a16_pe(pe, c, n):
            m = M16
            g = lambda s: sm[c.name, s]
            src = ctxT if c.cross else xnT
            nw = 4 if c.rope else 2
            wq, wk = 0, (2 if c.rope else 1) * KD * DM
            wv = nw * KD * DM
            wo = wv + KD * DM
            pe.wait_ge(w_loaded[c.name], 16)
            if c.cross:
                pe.wait_ge(ctx_loaded, 16)
            pe.wait_ge(ln_T, n + 1)
            step = 2 if c.rope else 1
            nb = 6 // step
            for e, (kind, t, f) in enumerate(c.tiles):
                if e >= nb:
                    pe.wait_ge(g("val"), e - nb + 1)
                for v in range(step):
                    base = (wq if kind == "q" else wk) + v * KD * DM
                    for k in range(KD):
                        rhs = xnT[:, k, :] if kind == "q" else src[:, k, f * BANK:(f + 1) * BANK]
                        last = nc.tensor.matmul(ps[:, (step * e + v) % 6, :], W(c.name, base + k * DM + t * P, P), rhs,
                                                start=(k == 0), stop=(k == KD - 1))
                last.then_inc(g("proj"), 1)
            for j in range(c.nj // 2):
                if j >= 2:
                    pe.wait_ge(g("v_up"), j - 1)
                for e in range(2):
                    jt = 2 * j + e
                    for k in range(KD):
                        last = nc.tensor.matmul(ps[:, 6 + j % 2, e * DM:(e + 1) * DM], src[:, k, jt * P:(jt + 1) * P],
                                                W(c.name, wv + k * DM, DM), start=(k == 0), stop=(k == KD - 1))
                last.then_inc(g("v_mm"), 1)
            pe.wait_ge(g("v_up"), c.nj // 2)
            pe.wait_ge(g("v_zero"), 1)
            pe.wait_ge(g("stack_in"), 12 * 16)
            ns, nu = len(c.s_tiles), len(c.units)

            def scores(h, tiles):
                for e in tiles:
                    s = h * ns + e
                    i, f, w = c.s_tiles[e]
                    if s >= 2:
                        pe.wait_ge(g("s_max"), s - 1)
                    o = ps[:, s % 2, 0:w]
                    plain = not (c.causal or c.masked)
                    last = nc.tensor.matmul(o, m["QS"][0:KR, h, i * P:(i + 1) * P], m["KS"][0:KR, h, f:f + w],
                                            start=True, stop=plain)
                    if c.causal:
                        last = nc.tensor.matmul(ps[:, s % 2, i * P:(i + 1) * P], identb[:, :], caus[:, :], start=False, stop=True)
                    if c.masked:
                        last = nc.tensor.matmul(o, identb[:, :], mneg[:, i, f:f + w], start=False, stop=True)
                    last.then_inc(g("s_mm"), 1)

            def max_row(h):
                pe.wait_ge(g("m_parts"), h + 1)
                if h:
                    pe.wait_ge(g("m_row"), h)
                if h >= 6 and h % 4 == 2:
                    pe.wait_ge(g("den_up"), (h - 2) // 4)
                for i in range(NI):
                    last = nc.tensor.matmul(ps[KR:KST, 7, i * P:(i + 1) * P], m["nmp"][:, h % 2, i, :], identb[:, :],
                                            start=True, stop=True)
                last.then_inc(g("m_mm"), 1)

            def scores_t(h, u):
                gu = h * nu + u
                if u == 0:
                    pe.wait_ge(g("m_row"), h + 1)
                if gu >= 2:
                    pe.wait_ge(g("exp"), gu - 1)
                for e, j in enumerate(c.units[u]):
                    q0 = j * P if c.causal else 0
                    o = ps[:, 2 + 2 * (gu % 2) + e, 0:S - q0]
                    plain = not (c.causal or c.masked)
                    last = nc.tensor.matmul(o, m["KS"][0:KST, h, j * P:(j + 1) * P], m["QS"][0:KST, h, q0:S],
                                            start=True, stop=plain)
                    if c.causal:
                        last = nc.tensor.matmul(o[:, 0:P], identb[:, :], causT[:, :], start=False, stop=True)
                    if c.masked:
                        last = nc.tensor.matmul(o, identb[:, :], mnegT[:, j, :], start=False, stop=True)
                last.then_inc(g("st_mm"), 1)

            def weighted(h, u):
                gu = h * nu + u
                pe.wait_ge(g("exp"), gu + 1)
                if h % 4 == 0 and u == 0 and h:
                    pe.wait_ge(g("o_up"), h // 4)
                for e, j in enumerate(c.units[u]):
                    q0 = j * P if c.causal else 0
                    r = 32 * (h % 4)
                    last = nc.tensor.matmul(ps[r:r + 32, 6, q0:S], m["VP"][:, j, h, :], m["PT"][:, gu % 2, e, 0:S - q0],
                                            start=(j == 0), stop=(j == c.nj - 1), tile_position=(0, r))
                last.then_inc(g("pv"), 1)

            def denominators(q):
                pe.wait_ge(g("o_up"), q + 1)
                nc.tensor.matmul(ps[:, 7, :], selden[:, :], m["OT"][:, q, :], start=True, stop=True).then_inc(g("den_mm"), 1)

            scores(0, range(ns))
            scores(1, range(ns))
            max_row(0)
            before = None
            share = ns // nu
            for h in range(NH):
                for u in range(nu):
                    scores_t(h, u)
                    if u == 0 and h >= 5 and h % 4 == 1:
                        denominators(h // 4 - 1)
                    if u == 1 and h + 1 < NH:
                        max_row(h + 1)
                    if h + 2 < NH:
                        scores(h + 2, range(u * share, (u + 1) * share))
                    if before:
                        weighted(*before)
                    before = (h, u)
            weighted(*before)
            denominators(3)
            for i in range(NI):
                pe.wait_ge(g("o_norm"), 3)
                for q in range(3):
                    nc.tensor.matmul(ps[:, Y_BANKS[i], 0:DM], m["ON"][:, q, i * P:(i + 1) * P],
                                     W(c.name, wo + q * DM, DM), start=(q == 0), stop=False)
            for i in range(NI):
                pe.wait_ge(g("o_norm"), 3 + i + 1)
                nc.tensor.matmul(ps[:, Y_BANKS[i], 0:DM], m["ON"][:, 3, i * P:(i + 1) * P],
                                 W(c.name, wo + 3 * DM, DM), start=False, stop=True).then_inc(g("y_mm"), 1)

        def a16_act(act, c):
            m = M16
            g = lambda s: sm[c.name, s]
            step = 2 if c.rope else 1
            if not c.rope:
                for e, (kind, t, f) in enumerate(c.tiles):
                    act.wait_ge(g("proj"), e + 1)
                    if e >= 2:
                        act.wait_ge(g("split"), e - 1)
                    if c.masked:
                        bias = (bqE if kind == "q" else bkE)[:, t:t + 1]
                        nc.scalar.activation(m["val"][:, e % 2, :], ps[:, e % 6, :], ACT.Identity, bias=bias).then_inc(g("val"), 1)
                    else:
                        nc.scalar.activation(m["val"][:, e % 2, :], ps[:, e % 6, :], ACT.Copy).then_inc(g("val"), 1)
            act.wait_ge(g("v_zero"), 1)
            if not c.masked:
                for j in range(c.nj // 2):
                    act.wait_ge(g("v_mm"), j + 1)
                    nc.scalar.activation(m["VP"][:, 2 * j:2 * j + 2, :, 0:HD],
                                         ps[:, 6 + j % 2, :].rearrange("p (j h d) -> p j h d", j=2, d=HD), ACT.Copy).then_inc(g("v_up"), 1)
            nu = len(c.units)

            def row(h):
                act.wait_ge(g("m_mm"), h + 1)
                nc.scalar.activation(m["QS"][KR:KST, h, :], ps[KR:KST, 7, :], ACT.Copy).then_inc(g("m_row"), 1)

            def denominators(q):
                act.wait_ge(g("den_mm"), q + 1)
                if q:
                    act.wait_ge(g("recip"), NI * q)
                nc.scalar.activation(m["den"][:, :], ps[:, 7, :], ACT.Copy).then_inc(g("den_up"), 1)

            row(0)
            for h in range(NH):
                for u in range(nu):
                    gu = h * nu + u
                    act.wait_ge(g("st_mm"), gu + 1)
                    if gu >= 2:
                        act.wait_ge(g("pv"), gu - 1)
                    n = len(c.units[u])
                    w = S - c.units[u][0] * P if c.causal else S
                    b0 = 2 + 2 * (gu % 2)
                    nc.scalar.activation(m["PT"][:, gu % 2, 0:n, 0:w], ps[:, b0:b0 + n, 0:w], ACT.Exp,
                                         scale=HD ** -0.5).then_inc(g("exp"), 1)
                    if u == 0 and h >= 5 and h % 4 == 1:
                        denominators(h // 4 - 1)
                    if u == 1 and h + 1 < NH:
                        row(h + 1)
            denominators(3)

        def a16_dve(dve, ch, c):
            m = M16
            g = lambda s: sm[c.name, s]

            def parts(dst, src, rest, last_sem):
                ch.link(nc.vector.tensor_copy(dst(0), src))
                ch.link(nc.vector.tensor_tensor(rest, src, dst(0), ALU.subtract))
                ch.link(nc.vector.tensor_copy(dst(1), rest))
                nc.vector.tensor_tensor(dst(2), rest, dst(1), ALU.subtract).then_inc(last_sem, 1)

            for e, (kind, t, f) in enumerate(c.tiles):
                if c.rope:
                    dve.wait_ge(g("proj"), e + 1)
                    b0 = (2 * e) % 6
                    if e >= 1:
                        dve.wait_ge(g("split"), e)
                    ch.link(nc.vector.tensor_tensor(m["rope"][:, :], ps[:, b0 + 1, :], sinD[:, :], ALU.mult))
                    ch.link(nc.vector.tensor_tensor(m["val"][:, e % 2, :], ps[:, b0, :], cosD[:, :], ALU.mult))
                    nc.vector.tensor_tensor(m["val"][:, e % 2, :], m["val"][:, e % 2, :], m["rope"][:, :], ALU.add).then_inc(g("val"), 1)
                dve.wait_ge(g("val"), e + 1)
                if c.masked and kind == "q":
                    ch.link(nc.vector.tensor_tensor(m["val"][:, e % 2, :], m["val"][:, e % 2, :], live[:, :], ALU.mult))
                if e >= 1:
                    dve.wait_ge(g("split"), e)
                dst = (lambda a: m["QP"][:, a, t, :]) if kind == "q" else (lambda a: m["KP"][:, a, t, f * BANK:(f + 1) * BANK])
                parts(dst, m["val"][:, e % 2, :], m["rest"][:, :], g("split"))
            if c.masked:
                dve.wait_ge(g("v_zero"), 1)
                for j in range(c.nj // 2):
                    dve.wait_ge(g("v_mm"), j + 1)
                    for e in range(2):
                        last = nc.vector.tensor_tensor(m["VP"][:, 2 * j + e, :, 0:HD],
                                                       ps[:, 6 + j % 2, e * DM:(e + 1) * DM].rearrange("p (h d) -> p h d", d=HD),
                                                       bvE[:, :].rearrange("p (h d) -> p h d", d=HD), ALU.add)
                    last.then_inc(g("v_up"), 1)
            ns, nu = len(c.s_tiles), len(c.units)

            def recip(q, i):
                if i == 0:
                    dve.wait_ge(g("den_up"), q + 1)
                    if q:
                        dve.wait_ge(g("o_norm"), q)
                t = slice(i * P, (i + 1) * P)
                nc.vector.reciprocal(m["rec"][:, t], m["den"][:, t]).then_inc(g("recip"), 1)

            def maxima(h, q=None):
                for e, (i, f, w) in enumerate(c.s_tiles):
                    s = h * ns + e
                    dve.wait_ge(g("s_mm"), s + 1)
                    nc.vector.tensor_reduce(m["mx"][:, h % 2, i, f // BANK:f // BANK + 1], ps[:, s % 2, 0:w], AX.X, ALU.max).then_inc(g("s_max"), 1)
                    if q is not None and e < NI:
                        recip(q, e)
                dve.wait_ge(g("s_max"), (h + 1) * ns)
                if c.halves == 2:
                    ch.link(nc.vector.tensor_tensor(m["nm"][:, :], m["mx"][:, h % 2, :, 0], m["mx"][:, h % 2, :, 1], ALU.max))
                    ch.link(nc.vector.tensor_scalar(m["nm"][:, :], m["nm"][:, :], -1.0, None, ALU.mult))
                else:
                    ch.link(nc.vector.tensor_scalar(m["nm"][:, :], m["mx"][:, h % 2, :, 0], -1.0, None, ALU.mult))
                if h >= 2:
                    dve.wait_ge(g("m_mm"), h - 1)
                parts(lambda a: m["nmp"][:, h % 2, :, a], m["nm"][:, :], m["nr"][:, :], g("m_parts"))
                dve.wait_ge(g("m_parts"), h + 1)

            maxima(0)
            maxima(1)
            for h in range(NH):
                q = h // 4 - 1 if h % 4 == 2 and h > 4 else None
                if h + 2 < NH:
                    maxima(h + 2, q)
                elif q is not None:
                    for i in range(NI):
                        recip(q, i)
                if h % 4 == 3:
                    dve.wait_ge(g("pv"), (h + 1) * nu)
                    nc.vector.tensor_copy(m["OT"][:, h // 4, :], ps[:, 6, :]).then_inc(g("o_up"), 1)
            for i in range(NI):
                recip(3, i)
                dve.wait_ge(g("recip"), 3 * NI + i + 1)
                t = slice(i * P, (i + 1) * P)
                nc.vector.tensor_tensor(m["ON"][:, 3, t], m["OT"][:, 3, t], m["rec"][:, t], ALU.mult).then_inc(g("o_norm"), 1)
            for i in range(NI):
                dve.wait_ge(g("y_mm"), i + 1)
                ch.link(nc.vector.tensor_tensor(x[:, i, :], x[:, i, :], ps[:, Y_BANKS[i], 0:DM], ALU.add))
                bo = {"B": boB, "E": boE}.get(c.name)
                if bo is not None:
                    ch.link(nc.vector.tensor_tensor(x[:, i, :], x[:, i, :], bo[:, :], ALU.add))
        EXTRA = {}
        SETUP_MORE = {}

        def named(prefix, *names):
            if prefix in STAGES:
                for n in names:
                    sm[prefix, n] = sem(f"{n}_{prefix}")


        def spread(ap, axis, shape):
            return ap.unsqueeze(axis).broadcast_to(shape)

        def top_mask(ch, v, groups, n, keep, c1, c2, mask):
            shape = [P, groups, n, n]
            other, own = spread(v, 2, shape), spread(v, 3, shape)
            earlier = spread(tri[:, 0:n, 0:n], 1, shape)
            ch.link(nc.vector.tensor_tensor(c1, other, own, ALU.is_gt))
            ch.link(nc.vector.tensor_tensor(c2, other, own, ALU.is_equal))
            ch.link(nc.vector.tensor_tensor(c2, c2, earlier, ALU.mult))
            ch.link(nc.vector.tensor_tensor(c1, c1, c2, ALU.add))
            ch.link(nc.vector.tensor_reduce(mask, c1, AX.X, ALU.add))
            ch.link(nc.vector.tensor_scalar(mask, mask, keep - 0.5, None, ALU.is_lt))

        CH, CW, CN = 8, 64, 5
        named("C", "gated", "gl_mm", "sig", "gl_free", "xv_mm", "xv_up", "qk_mm", "qk_up", "s_mm", "negm", "exp", "tr", "pt_up", "v_up", "pv",
              "o_up", "ob_mm", "attn", "ae_pool", "ae_dve", "aet_mm", "aet_up", "y_mm")

        def c_mem(sb2):
            m = {}
            m["qk"] = sb2("c_qk", [P, 8, S])
            m["gl"] = sb2("c_gl", [P, NI * 2 * CH, CN])
            m["msk"] = sb2("c_msk", [P, NI * 2 * CH, CN])
            m["c1"] = sb2("c_c1", [P, NI * 2 * CH, CN, CN])
            m["c2"] = sb2("c_c2", [P, NI * 2 * CH, CN, CN])
            m["sg"] = sb2("c_sg", [P, NI, 2 * CH * CN])
            m["xv"] = sb2("c_xv", [P, NI, CN * CW])
            m["V"] = sb2("c_V", [P, NI, CH * CW])
            m["tmp"] = sb2("c_tmp", [P, 2, CH * CW])
            m["Pr"] = sb2("c_P", [P, 2, S])
            m["PT"] = sb2("c_PT", [P, 2, NI, S])
            m["nm"] = sb2("c_nm", [P, CH * NI])
            m["den"] = sb2("c_den", [P, NI, CH])
            m["rden"] = sb2("c_rden", [P, NI, CH])
            m["OT"] = sb2("c_OT", [P, 2, S])
            m["at"] = sb2("c_at", [P, NI, P])
            m["ae"] = sb2("c_ae", [P, NI, CN * CW])
            m["aeT"] = sb2("c_aeT", [P, 3, S])
            return m

        MC = scope(c_mem)
        C_Q, C_K, C_G, C_X, C_O = 0, 1024, 2048, 2208, 2848
        KT_AE = [P, P, CN * CW - 2 * P]

        def c_pe(pe, _, n, st):
            m = MC
            g = lambda s: sm["C", s]
            pe.wait_ge(w_loaded["C"], 16)
            pe.wait_ge(ln_T, n + 1)
            for i in range(NI):
                for k in range(KD):
                    last = nc.tensor.matmul(ps[:, 0, i * 80:(i + 1) * 80], xnT[:, k, i * P:(i + 1) * P],
                                            W("C", C_G + 80 * k, 80), start=(k == 0), stop=(k == KD - 1))
            last.then_inc(g("gl_mm"), 1)
            for i in range(NI):
                for k in range(KD):
                    last = nc.tensor.matmul(ps[:, 1 + i, 0:320], xnT[:, k, i * P:(i + 1) * P],
                                            W("C", C_X + 320 * k, 320), start=(k == 0), stop=(k == KD - 1))
                last.then_inc(g("xv_mm"), 1)
            for e in range(8):
                if e >= 3:
                    pe.wait_ge(g("qk_up"), e - 2)
                base = (C_Q if e < 4 else C_K) + (e % 4) * P
                for k in range(KD):
                    last = nc.tensor.matmul(ps[:, 5 + e % 3, :], W("C", base + 512 * k, P), xnT[:, k, :],
                                            start=(k == 0), stop=(k == KD - 1))
                last.then_inc(g("qk_mm"), 1)
            pe.wait_ge(g("qk_up"), 8)
            pe.wait_ge(g("xv_up"), NI)
            pe.wait_ge(g("gl_free"), 1)

            def scores(s):
                h, i = divmod(s, NI)
                if s >= 2:
                    pe.wait_ge(g("exp"), s - 1)
                r = CW * (h % 2)
                nc.tensor.matmul(ps[:, s % 2, :], m["qk"][r:r + CW, h // 2, i * P:(i + 1) * P], m["qk"][r:r + CW, 4 + h // 2, :],
                                 start=True, stop=True).then_inc(g("s_mm"), 1)

            def turn(s):
                pe.wait_ge(g("exp"), s + 1)
                if s >= 2:
                    pe.wait_ge(g("pt_up"), s - 1)
                for j in range(NI):
                    last = nc.tensor.transpose(ps[:, 2 + s % 2, j * P:(j + 1) * P], m["Pr"][:, s % 2, j * P:(j + 1) * P], ident[:, :])
                last.then_inc(g("tr"), 1)

            def weighted(h):
                pe.wait_ge(g("pt_up"), NI * (h + 1))
                pe.wait_ge(g("v_up"), NI)
                if h % 2 == 0 and h >= 4:
                    pe.wait_ge(g("o_up"), h // 2 - 1)
                r = CW * (h % 2)
                for j in range(NI):
                    last = nc.tensor.matmul(ps[r:r + CW, 4 + (h // 2) % 2, :], m["V"][:, j, h * CW:(h + 1) * CW], m["PT"][:, h % 2, j, :],
                                            start=(j == 0), stop=(j == NI - 1), tile_position=(0, r))
                last.then_inc(g("pv"), 1)

            def back(q):
                pe.wait_ge(g("o_up"), q + 1)
                if q >= 2:
                    pe.wait_ge(g("attn"), q - 1)
                for i in range(NI):
                    last = nc.tensor.transpose(ps[:, 6 + q % 2, i * P:(i + 1) * P], m["OT"][:, q % 2, i * P:(i + 1) * P], ident[:, :])
                last.then_inc(g("ob_mm"), 1)

            scores(0)
            scores(1)
            for s in range(CH * NI):
                if s + 2 < CH * NI:
                    scores(s + 2)
                h, i = divmod(s, NI)
                if i == 1 and h:
                    weighted(h - 1)
                if i == 3 and h and h % 2 == 0:
                    back(h // 2 - 1)
                turn(s)
            weighted(CH - 1)
            back(CH // 2 - 1)
            for i in range(NI):
                pe.wait_ge(g("ae_dve"), DVE_E)
                pe.wait_ge(g("ae_pool"), CN * CH // 2 - DVE_E)
                if i >= 2:
                    pe.wait_ge(g("aet_up"), i - 1)
                for t, rows in enumerate(KT_AE):
                    last = nc.tensor.transpose(ps[0:rows, i % 2, t * P:(t + 1) * P], m["ae"][:, i, t * P:t * P + rows], ident[:, :])
                last.then_inc(g("aet_mm"), 1)
            for i in range(NI):
                pe.wait_ge(g("aet_up"), i + 1)
                for t, rows in enumerate(KT_AE):
                    last = nc.tensor.matmul(ps[:, 4 + i, 0:DM], m["aeT"][0:rows, t, i * P:(i + 1) * P],
                                            wbuf[0:rows, slot_of["C"], C_O + t * DM:C_O + (t + 1) * DM],
                                            start=(t == 0), stop=(t == 2))
                last.then_inc(g("y_mm"), 1)

        def c_act(act, _, n, st):
            m = MC
            g = lambda s: sm["C", s]
            act.wait_ge(g("gl_free"), 1)
            nc.scalar.activation(m["sg"][:, :, :], m["gl"][:, :, :].rearrange("p (i a) e -> p i (a e)", i=NI), ACT.Exp, scale=-1.0).then_inc(g("sig"), 1)
            for i in range(NI):
                act.wait_ge(g("xv_mm"), i + 1)
                nc.scalar.activation(m["xv"][:, i, :], ps[:, 1 + i, 0:320], ACT.Copy).then_inc(g("xv_up"), 1)
            for e in range(8):
                act.wait_ge(g("qk_mm"), e + 1)
                nc.scalar.activation(m["qk"][:, e, :], ps[:, 5 + e % 3, :], ACT.Copy).then_inc(g("qk_up"), 1)

            def up(s):
                h, i = divmod(s, NI)
                act.wait_ge(g("tr"), s + 1)
                if h >= 2:
                    act.wait_ge(g("pv"), h - 1)
                nc.scalar.activation(m["PT"][:, h % 2, :, i * P:(i + 1) * P],
                                     ps[:, 2 + s % 2, :].rearrange("p (j q) -> p j q", j=NI), ACT.Copy).then_inc(g("pt_up"), 1)

            for s in range(CH * NI):
                h, i = divmod(s, NI)
                act.wait_ge(g("negm"), s + 1)
                if s >= 2:
                    act.wait_ge(g("tr"), s - 1)
                nc.scalar.activation(m["Pr"][:, s % 2, :], ps[:, s % 2, :], ACT.Exp, bias=m["nm"][:, s:s + 1], scale=CW ** -0.5,
                                     accum_out=m["den"][:, i, h:h + 1]).then_inc(g("exp"), 1)
                if s:
                    up(s - 1)
            up(CH * NI - 1)
            for i in range(NI):
                act.wait_ge(g("aet_mm"), i + 1)
                for t, rows in enumerate(KT_AE):
                    last = nc.scalar.activation(m["aeT"][0:rows, t, i * P:(i + 1) * P], ps[0:rows, i % 2, t * P:(t + 1) * P], ACT.Copy)
                last.then_inc(g("aet_up"), 1)

        POOL_MIX = 2
        DVE_E = 3

        def mix(eng, ch, i):
            m = MC
            k = 1 if eng is nc.gpsimd else 0
            shape = [P, CH, CW]
            dst = m["V"][:, i, :].rearrange("p (h k) -> p h k", h=CH)
            for e in range(CN):
                gate = spread(m["sg"][:, i, 0:CH * CN].rearrange("p (h e) -> p h e", e=CN)[:, :, e], 2, shape)
                val = spread(m["xv"][:, i, e * CW:(e + 1) * CW], 1, shape)
                o = dst if e == 0 else m["tmp"][:, k, :].rearrange("p (h k) -> p h k", h=CH)
                ch.link(eng.tensor_tensor(o, val, gate, ALU.mult))
                if e:
                    add = eng.tensor_tensor(dst, dst, o, ALU.add)
                    if e < CN - 1:
                        ch.link(add)
            add.then_inc(sm["C", "v_up"], 1)

        def add_pair(eng, ch, q, experts, done, n=0):
            m = MC
            k = 1 if eng is nc.gpsimd else 0
            t = m["tmp"][:, k, :].rearrange("p (i h k) -> p i h k", i=NI, h=2)
            for e in experts:
                pick = spread(m["msk"][:, :, :].rearrange("p (i a) e -> p i a e", i=NI)[:, :, CH + 2 * q:CH + 2 * q + 2, e], 3, [P, NI, 2, CW])
                ch.link(eng.tensor_tensor(t, m["at"][:, :, :].rearrange("p i (h k) -> p i h k", h=2), pick, ALU.mult))
                acc = m["ae"][:, :, e * CW:(e + 1) * CW]
                if q:
                    ch.link(eng.tensor_tensor(acc, acc, t[:, :, 0, :], ALU.add))
                eng.tensor_tensor(acc, acc if q else t[:, :, 0, :], t[:, :, 1, :], ALU.add).then_inc(done, 1)
                n += 1
                ch.eng.wait_ge(done, n)
            return n

        def c_pool(pool, ch, n, st):
            g = lambda s: sm["C", s]
            pool.wait_ge(g("gated"), 1)
            pool.wait_ge(g("xv_up"), NI)
            for i in range(NI - POOL_MIX, NI):
                mix(nc.gpsimd, ch, i)
            added = 0
            for q in range(CH // 2):
                pool.wait_ge(g("attn"), q + 1)
                added = add_pair(nc.gpsimd, ch, q, range(CN) if q < CH // 2 - 1 else range(DVE_E, CN), g("ae_pool"), added)

        def c_dve(dve, ch, n, st):
            m = MC
            g = lambda s: sm["C", s]
            dve.wait_ge(g("gl_mm"), 1)
            nc.vector.tensor_copy(m["gl"][:, :, :], ps[:, 0, 0:320].rearrange("p (a e) -> p a e", e=CN)).then_inc(g("gl_free"), 1)
            dve.wait_ge(g("gl_free"), 1)
            top_mask(ch, m["gl"][:, :, :], NI * 2 * CH, CN, 2, m["c1"][:, :, :, :], m["c2"][:, :, :, :], m["msk"][:, :, :])
            dve.wait_ge(g("sig"), 1)
            ch.link(nc.vector.tensor_scalar(m["sg"][:, :, :], m["sg"][:, :, :], 1.0, None, ALU.add))
            ch.link(nc.vector.reciprocal(m["sg"][:, :, :], m["sg"][:, :, :]))
            mk = m["msk"][:, :, :].rearrange("p (i a) e -> p i (a e)", i=NI)
            nc.vector.tensor_tensor(m["sg"][:, :, :], m["sg"][:, :, :], mk, ALU.mult).then_inc(g("gated"), 1)
            dve.wait_ge(g("gated"), 1)

            def maximum(s):
                dve.wait_ge(g("s_mm"), s + 1)
                ch.link(nc.vector.tensor_reduce(m["nm"][:, s:s + 1], ps[:, s % 2, :], AX.X, ALU.max))
                nc.vector.tensor_scalar(m["nm"][:, s:s + 1], m["nm"][:, s:s + 1], -(CW ** -0.5), None, ALU.mult).then_inc(g("negm"), 1)

            def pair(q):
                dve.wait_ge(g("pv"), 2 * q + 2)
                if q >= 2:
                    dve.wait_ge(g("ob_mm"), q - 1)
                nc.vector.tensor_copy(m["OT"][:, q % 2, :], ps[:, 4 + q % 2, :]).then_inc(g("o_up"), 1)
                ch.link(nc.vector.reciprocal(m["rden"][:, :, 2 * q:2 * q + 2], m["den"][:, :, 2 * q:2 * q + 2]))
                dve.wait_ge(g("ob_mm"), q + 1)
                if q:
                    dve.wait_ge(g("ae_pool"), CN * q)
                for i in range(NI):
                    last = nc.vector.tensor_tensor(m["at"][:, i, :].rearrange("p (h k) -> p h k", h=2),
                                                   ps[:, 6 + q % 2, i * P:(i + 1) * P].rearrange("p (h k) -> p h k", h=2),
                                                   spread(m["rden"][:, i, 2 * q:2 * q + 2], 2, [P, 2, CW]), ALU.mult)
                last.then_inc(g("attn"), 1)
            dve.wait_ge(g("xv_up"), NI)
            for s in range(CH * NI):
                h, i = divmod(s, NI)
                maximum(s)
                if s < NI - POOL_MIX:
                    mix(nc.vector, ch, s)
                if i == 3 and h >= 2 and h % 2 == 0:
                    pair(h // 2 - 1)
            pair(CH // 2 - 1)
            dve.wait_ge(g("attn"), CH // 2)
            add_pair(nc.vector, ch, CH // 2 - 1, range(DVE_E), g("ae_dve"))
            for i in range(NI):
                dve.wait_ge(g("y_mm"), i + 1)
                ch.link(nc.vector.tensor_tensor(x[:, i, :], x[:, i, :], ps[:, 4 + i, 0:DM], ALU.add))

        EXTRA["C"] = dict(pe=c_pe, act=c_act, dve=c_dve, pool=c_pool, sp=lambda *a: None)

        named("F", "lg_mm", "lg_exp", "comb", "ct_mm", "ct_up", "gu_mm", "silu", "gu", "down")

        if "F" in STAGES:
            w_in = [sem(f"w_in{k}_F") for k in range(NRING)]

        def f_mem(sb2):
            m = {}
            m["w"] = sb2("f_w", [P, NRING, 3 * DM])
            m["sc"] = sb2("f_sc", [P, NI, NE])
            m["sb"] = sb2("f_sb", [P, NI, NE])
            m["mb"] = sb2("f_mb", [P, NI, NE])
            m["rp"] = sb2("f_rp", [P, NI, NE])
            m["t8"] = sb2("f_t8", [P, NI, 8])
            m["m4"] = sb2("f_m4", [P, NI * 8, 4])
            m["c1"] = sb2("f_c1", [P, NI * 128])
            m["c2"] = sb2("f_c2", [P, NI * 128])
            m["gs"] = sb2("f_gs", [P, NI, 8])
            m["gm"] = sb2("f_gm", [P, NI, 8])
            m["sum"] = sb2("f_sum", [P, NI])
            m["rest"] = sb2("f_rest", [P, NI, NE])
            m["cp"] = sb2("f_cp", [P, NI, 3, NE], BF16)
            m["cT"] = sb2("f_cT", [96, S], BF16)
            m["si"] = sb2("f_si", [P, 2, S])
            m["gu"] = sb2("f_gu", [P, 2, S])
            m["tm"] = sb2("f_tm", [P, S])
            return m

        MF = scope(f_mem)

        ahead = sem("ahead")

        def load_ahead(sp, b, signal):
            sp.dma_start(M1["x"][:, :, :], io["x"][bass.ds(b, 1), :, :].rearrange("o (t p) d -> p (o t) d", p=P)).then_inc(signal, 16)
            sp.dma_start(M1["w"][:, :, :], io["wA"].rearrange("(k p) c -> p k c", p=P)).then_inc(signal, 16)
            sp.dma_start(M1["wo"][:, :, :], io["woA"].rearrange("(k p) c -> p k c", p=P)).then_inc(signal, 16)

        def f_sp(sp, b, *_):
            for e in range(NE + NSH):
                if e >= NRING:
                    sp.wait_ge(sm["F", "down"], e - NRING + 1)
                sp.dma_start(MF["w"][:, e % NRING, :], io["wF"][e]).then_inc(w_in[e % NRING], 16)
                if e == NRING - 1:
                    load_ahead(sp, b + 1, ahead)
            sp.wait_ge(ahead, 3 * 16)

        def f_pe(pe, _, n, st):
            m = MF
            g = lambda s: sm["F", s]
            pe.wait_ge(ln_T, n + 1)
            for i in range(NI):
                for k in range(KD):
                    last = nc.tensor.matmul(ps[:, 4, i * NE:(i + 1) * NE], xnT[:, k, i * P:(i + 1) * P], gateW[:, k, :],
                                            start=(k == 0), stop=(k == KD - 1))
            last.then_inc(g("lg_mm"), 1)

            def up(e):
                pe.wait_ge(w_in[e % NRING], 16 * (e // NRING + 1))
                if e >= 2:
                    pe.wait_ge(g("gu"), e - 1)
                for v in range(2):
                    for k in range(KD):
                        last = nc.tensor.matmul(ps[:, 2 * v + e % 2, :], m["w"][:, e % NRING, (2 * v + k) * P:(2 * v + k + 1) * P],
                                                xnT[:, k, :], start=(k == 0), stop=(k == KD - 1))
                if e == NSH:
                    pe.wait_ge(g("comb"), 1)
                    for i in range(NI):
                        last = nc.tensor.matmul(ps[0:96, 5, i * P:(i + 1) * P], m["cp"][:, i, :, :].rearrange("p a e -> p (a e)"),
                                                identb[:, :], start=True, stop=True)
                    last.then_inc(g("ct_mm"), 1)
                    pe.wait_ge(g("ct_up"), 1)
                if e >= NSH:
                    last = nc.tensor.matmul(ps[:, 4 + e % 2, :], selE[:, e - NSH, :], m["cT"][:, :], start=True, stop=True)
                last.then_inc(g("gu_mm"), 1)

            def down(e):
                pe.wait_ge(g("gu"), e + 1)
                for i in range(NI):
                    last = nc.tensor.matmul(ps[:, 6 + i // 2, (i % 2) * DM:(i % 2 + 1) * DM], m["gu"][:, e % 2, i * P:(i + 1) * P],
                                            m["w"][:, e % NRING, 2 * DM:3 * DM], start=(e == 0 and i % 2 == 0),
                                            stop=(e == NE + NSH - 1), skip_group_check=True)
                last.then_inc(g("down"), 1)

            up(0)
            for e in range(1, NE + NSH):
                up(e)
                down(e - 1)
            down(NE + NSH - 1)

        def f_act(act, _, n, st):
            m = MF
            g = lambda s: sm["F", s]
            act.wait_ge(g("lg_mm"), 1)
            nc.scalar.activation(m["sc"][:, :, :], ps[:, 4, 0:NI * NE].rearrange("p (i e) -> p i e", i=NI), ACT.Exp, scale=-1.0).then_inc(g("lg_exp"), 1)
            for e in range(NE + NSH):
                if e == NSH:
                    act.wait_ge(g("ct_mm"), 1)
                    nc.scalar.activation(m["cT"][:, :], ps[0:96, 5, :], ACT.Copy).then_inc(g("ct_up"), 1)
                act.wait_ge(g("gu_mm"), e + 1)
                if e >= 2:
                    act.wait_ge(g("gu"), e - 1)
                nc.scalar.activation(m["si"][:, e % 2, :], ps[:, e % 2, :], ACT.Silu).then_inc(g("silu"), 1)

        def f_dve(dve, ch, n, st):
            m = MF
            g = lambda s: sm["F", s]

            def gate():
                dve.wait_ge(g("lg_exp"), 1)
                f2 = lambda t: m[t][:, :, :]
                ch.link(nc.vector.tensor_scalar(f2("sc"), f2("sc"), 1.0, None, ALU.add))
                ch.link(nc.vector.reciprocal(f2("sc"), f2("sc")))
                ch.link(nc.vector.tensor_tensor(f2("sb"), f2("sc"), spread(gateB[:, :], 1, [P, NI, NE]), ALU.add))
                by4 = m["sb"][:, :, :].rearrange("p i (g e) -> p (i g) e", e=4)
                c = lambda t, k: m[t][:, 0:NI * 8 * k * k if k == 4 else NI * 64].rearrange("p (a e f) -> p a e f", e=k, f=k)
                top_mask(ch, by4, NI * 8, 4, 2, c("c1", 4), c("c2", 4), m["m4"][:, :, :])
                ch.link(nc.vector.tensor_tensor(m["m4"][:, :, :], m["m4"][:, :, :], by4, ALU.mult))
                ch.link(nc.vector.tensor_reduce(m["gs"][:, :, :].rearrange("p i g -> p (i g)"), m["m4"][:, :, :], AX.X, ALU.add))
                top_mask(ch, m["gs"][:, :, :], NI, 8, 4, c("c1", 8), c("c2", 8), m["gm"][:, :, :])
                ch.link(nc.vector.tensor_tensor(m["mb"][:, :, :].rearrange("p i (g e) -> p (i g) e", e=4), by4,
                                                spread(m["gm"][:, :, :].rearrange("p i g -> p (i g)"), 2, [P, NI * 8, 4]), ALU.mult))
                for i in range(NI):
                    last = nc.vector.max(m["t8"][:, i, :], m["mb"][:, i, :])
                ch.link(last)
                for i in range(NI):
                    last = nc.vector.match_replace(m["rp"][:, i, :], m["t8"][:, i, :], m["mb"][:, i, :], -1e30)
                ch.link(last)
                ch.link(nc.vector.tensor_tensor(f2("rp"), f2("rp"), f2("mb"), ALU.is_lt))
                ch.link(nc.vector.tensor_tensor(f2("mb"), f2("rp"), f2("sc"), ALU.mult))
                ch.link(nc.vector.tensor_reduce(m["sum"][:, :], f2("mb"), AX.X, ALU.add))
                ch.link(nc.vector.tensor_scalar(m["sum"][:, :], m["sum"][:, :], 1e-20, None, ALU.add))
                ch.link(nc.vector.reciprocal(m["sum"][:, :], m["sum"][:, :]))
                ch.link(nc.vector.tensor_tensor(f2("mb"), f2("mb"), spread(m["sum"][:, :], 2, [P, NI, NE]), ALU.mult))
                ch.link(nc.vector.tensor_scalar(f2("mb"), f2("mb"), 2.5, None, ALU.mult))
                ch.link(nc.vector.tensor_copy(m["cp"][:, :, 0, :], f2("mb")))
                ch.link(nc.vector.tensor_tensor(f2("rest"), f2("mb"), m["cp"][:, :, 0, :], ALU.subtract))
                ch.link(nc.vector.tensor_copy(m["cp"][:, :, 1, :], f2("rest")))
                nc.vector.tensor_tensor(m["cp"][:, :, 2, :], f2("rest"), m["cp"][:, :, 1, :], ALU.subtract).then_inc(g("comb"), 1)

            gate()
            for e in range(NE + NSH):
                dve.wait_ge(g("silu"), e + 1)
                if e >= 2:
                    dve.wait_ge(g("down"), e - 1)
                if e < NSH:
                    nc.vector.tensor_tensor(m["gu"][:, e % 2, :], m["si"][:, e % 2, :], ps[:, 2 + e % 2, :], ALU.mult).then_inc(g("gu"), 1)
                else:
                    ch.link(nc.vector.tensor_tensor(m["tm"][:, :], m["si"][:, e % 2, :], ps[:, 2 + e % 2, :], ALU.mult))
                    nc.vector.tensor_tensor(m["gu"][:, e % 2, :], m["tm"][:, :], ps[:, 4 + e % 2, :], ALU.mult).then_inc(g("gu"), 1)
                    dve.wait_ge(g("gu"), e + 1)
            dve.wait_ge(g("down"), NE + NSH)
            for i in range(NI):
                ch.link(nc.vector.tensor_tensor(x[:, i, :], x[:, i, :], ps[:, 6 + i // 2, (i % 2) * DM:(i % 2 + 1) * DM], ALU.add))

        EXTRA["F"] = dict(pe=f_pe, act=f_act, dve=f_dve, pool=lambda *a: None, sp=f_sp)

        AH, AW = 16, 64
        SA_R = [4, 2, 1, 1]
        CH_ROWS = 4
        NCHUNK = NI * 16 // CH_ROWS
        HB = [0, 1, 6]
        BACK = 399
        sk = [nc.dram_tensor(f"scores_kerple{i}", (2 * AH, P, (i + 1) * P), F32, kind="Internal").ap() for i in range(NI)]
        named("A", "rot", "qk_mm", "qk_up", "e_mm", "e_up", "out0", "out1", "out2", "out3", "cmb0", "cmb1", "fin0", "fin1", "fin2", "fin3",
              "w1", "gelu", "w2", "mixed", "negm", "exp", "prob", "tr", "pt_up", "pv", "ot_up", "y_mm", "y_up")
        KT_A = AH * AW // P
        AC = 3 * AH * AW

        TRI_L = [(i + 1) * P for i in range(NI)]

        def a1_mem(sb2):
            m = dict(both)
            m["qk"] = sb2("a_qk", [P, 16, S])
            m["rot"] = sb2("a_rot", [P, 2, S])
            m["w"] = sb2("a_w", [P, KD, AC])
            m["x"] = sb2("a_x", [P, NI, DM])
            m["Ss"] = sb2("a_Ss", [P, 4 * sum(TRI_L)])
            return m

        def a2_mem(sb2):
            m = dict(both)
            m["PT"] = sb2("a_PT", [P, NI, 16, P])
            m["cmb"] = sb2("a_cmb", [P, 2, 2, CH_ROWS * S])
            m["fin"] = sb2("a_fin", [P, 4, CH_ROWS * S])
            hid2 = sb2("a_hid", [P, BANK])
            m["hid"] = [xn[:, 0:2, :].rearrange("p a c -> p (a c)"), xn[:, 2:4, :].rearrange("p a c -> p (a c)"), hid2[:, :]]
            m["OT"] = spare[:, KT_A * DM:KT_A * (DM + P)].rearrange("p (t c) -> p t c", t=KT_A)
            m["nm"] = sb2("a_nm", [P, 4, CH_ROWS])
            m["den"] = sb2("a_den", [P, 4, CH_ROWS])
            return m

        def a_mem(sb2):
            both.update(V=sb2("a_V", [P, NI, AH * AW]), wo=spare[:, 0:KT_A * DM].rearrange("p (t c) -> p t c", t=KT_A))
            return scope(a1_mem), scope(a2_mem)

        spare = wbuf[:, 1, :]
        both = {}
        M1, M2 = scope(a_mem)

        def chunk(n):
            i, c = divmod(n, 4)
            return i, c, (i + 1) * P

        A_UNITS = [(n, f, q) for n in range(NCHUNK) for q in range(0, CH_ROWS, SA_R[n // 4]) for f in range(2)]
        UNITS_TO = [sum(u[0] < n for u in A_UNITS) for n in range(NCHUNK + 1)]
        TURNS_TO = [sum(chunk(k)[0] + 1 for k in range(n)) for n in range(NCHUNK + 1)]

        def a_sp(sp, _, n, st):
            g = lambda s: sm["A", s]
            for grp in range(16):
                hq, i = divmod(grp, NI)
                L = (i + 1) * P
                sp.wait_ge(g("e_up"), 8 + 4 * (grp + 1))
                sp.dma_start(sk[i][4 * hq:4 * hq + 4].rearrange("h p j -> p h j"),
                             M1["Ss"][:, 4 * sum(TRI_L[:i]):4 * sum(TRI_L[:i + 1])].rearrange("p (h l) -> p h l", h=4)).then_inc(g(f"out{i}"), 16)
            sp.wait_ge(g("out0"), 4 * 16)
            for c in range(NCHUNK):
                i, q, L = chunk(c)
                if c == 1:
                    for k in range(1, NI):
                        sp.wait_ge(g(f"out{k}"), 4 * 16)
                    st.end()
                if c >= 2:
                    sp.wait_ge(g("w1"), UNITS_TO[c - 1])
                rows = sk[i].rearrange("r (f g q) j -> g r f (q j)", f=2, g=4)
                part = slice(CH_ROWS * q * L, CH_ROWS * (q + 1) * L)
                for u in range(4):
                    sp.dma_start(M2["cmb"][32 * u:32 * u + 32, c % 2, :, 0:CH_ROWS * L], rows[u, :, :, part]).then_inc(g(f"cmb{c % 2}"), 16)
                if c >= 4:
                    sp.wait_ge(g("tr"), TURNS_TO[c - 3])
                rows = sk[i][0:AH].rearrange("h (g q) j -> g h (q j)", g=8)
                sp.dma_start(M2["fin"][:, c % 4, 0:CH_ROWS * L], rows[:, :, part]).then_inc(g(f"fin{c % 4}"), 16)

        def a_pe(pe, _, n, st):
            g = lambda s: sm["A", s]
            m = M1
            pe.wait_ge(ln_T, n + 1)
            HW = AH * AW
            for e in range(16):
                if e >= 4:
                    pe.wait_ge(g("qk_up"), e - 3)
                t, kind = divmod(e, 2)
                col = kind * HW + t * P
                for k in range(KD):
                    last = nc.tensor.matmul(ps[:, e % 4, :], m["w"][:, k, col:col + P], xnT[:, k, :],
                                            start=(k == 0), stop=(k == KD - 1))
                last.then_inc(g("qk_mm"), 1)
            for e in range(8):
                i, f = divmod(e, 2)
                if e >= 4:
                    pe.wait_ge(g("e_up"), e - 3)
                for k in range(KD):
                    last = nc.tensor.matmul(ps[:, 4 + e % 4, :], xnT[:, k, i * P:(i + 1) * P],
                                            m["w"][:, k, 2 * HW + f * BANK:2 * HW + (f + 1) * BANK], start=(k == 0), stop=(k == KD - 1))
                last.then_inc(g("e_mm"), 1)
            for s in range(64):
                e = 8 + s
                grp, hh = divmod(s, 4)
                hq, i = divmod(grp, NI)
                h = 4 * hq + hh
                pe.wait_ge(g("e_up"), e - 3)
                if i == 0:
                    pe.wait_ge(g("qk_up"), 2 * (h // 2 + 1))
                r = AW * (h % 2)
                nc.tensor.matmul(ps[:, 4 + e % 4, 0:(i + 1) * P], m["qk"][r:r + AW, 2 * (h // 2), i * P:(i + 1) * P],
                                 m["qk"][r:r + AW, 2 * (h // 2) + 1, 0:(i + 1) * P], start=True, stop=True).then_inc(g("e_mm"), 1)
            st.end()
            m = M2

            def up(k):
                c, f, q = A_UNITS[k]
                i, _, L = chunk(c)
                if k == UNITS_TO[c]:
                    pe.wait_ge(g(f"cmb{c % 2}"), 16 * 4 * (c // 2 + 1))
                if k >= 3:
                    pe.wait_ge(g("gelu"), k - 2)
                R = SA_R[i]
                nc.tensor.matmul(ps[:, HB[k % 3], 0:R * L], w1A[:, :], m["cmb"][:, c % 2, f, q * L:(q + R) * L],
                                 start=True, stop=True).then_inc(g("w1"), 1)

            def down(k):
                c, f, q = A_UNITS[k]
                i, _, L = chunk(c)
                w = k // 2
                pe.wait_ge(g("gelu"), k + 1)
                if w >= 2:
                    pe.wait_ge(g("mixed"), w - 1)
                nc.tensor.matmul(ps[64 * f:64 * f + 64, 2 + w % 2, 0:SA_R[i] * L], w2A[:, :], m["hid"][k % 3][:, 0:SA_R[i] * L],
                                 start=True, stop=True, tile_position=(0, 64 * f)).then_inc(g("w2"), 1)

            def turn(c, j):
                t = TURNS_TO[c] + j
                L = chunk(c)[2]
                if j == 0:
                    pe.wait_ge(g("prob"), c + 1)
                if t >= 2:
                    pe.wait_ge(g("pt_up"), t - 1)
                if j == 0 and c >= 4:
                    pe.wait_ge(g("ot_up"), c // 4)
                for q in range(CH_ROWS):
                    last = nc.tensor.transpose(ps[:, 4 + t % 2, q * P:(q + 1) * P], m["fin"][:, c % 4, q * L + j * P:q * L + (j + 1) * P], ident[:, :])
                last.then_inc(g("tr"), 1)

            def weighted(i):
                pe.wait_ge(g("pt_up"), TURNS_TO[4 * (i + 1)])
                for h in range(AH):
                    r, t = AW * (h % 2), h // 2
                    for j in range(i + 1):
                        rhs = m["PT"][:, j, :, :].rearrange("p q (g h) -> p h g q", h=AH)[:, h]
                        o = ps[r:r + AW, 4 + t // 4, (t % 4) * P:(t % 4 + 1) * P].rearrange("p (g q) -> p g q", g=8)
                        last = nc.tensor.matmul(o, m["V"][:, j, h * AW:(h + 1) * AW], rhs, start=(j == 0), stop=(j == i), tile_position=(0, r))
                last.then_inc(g("pv"), 1)

            def project(i):
                pe.wait_ge(g("ot_up"), i + 1)
                if i:
                    pe.wait_ge(g("y_up"), i)
                for t in range(KT_A):
                    last = nc.tensor.matmul(ps[:, 7, 0:DM], m["OT"][:, t, :], m["wo"][:, t, :], start=(t == 0), stop=(t == KT_A - 1))
                last.then_inc(g("y_mm"), 1)

            up(0)
            up(1)
            for s in range(NCHUNK + 3):
                c = s - 2
                if s < NCHUNK:
                    for k in range(UNITS_TO[s], UNITS_TO[s + 1]):
                        if k + 2 < len(A_UNITS):
                            up(k + 2)
                        down(k)
                if 0 <= c < NCHUNK:
                    turn(c, 0)
                if s % 4 == 2 and s >= 6:
                    project(s // 4 - 1)
                if 0 <= c < NCHUNK:
                    for j in range(1, chunk(c)[0] + 1):
                        turn(c, j)
                if s % 4 == 1 and s >= 5:
                    weighted(s // 4 - 1)

        def a_act(act, _, n, st):
            g = lambda s: sm["A", s]
            m = M1
            for e in range(16):
                act.wait_ge(g("qk_mm"), e + 1)
                if e >= 2:
                    act.wait_ge(g("qk_up"), e - 1)
                for r in range(0, P, 32):
                    r2 = r ^ 32
                    last = nc.scalar.activation(m["rot"][r:r + 32, e % 2, :], ps[r2:r2 + 32, e % 4, :], ACT.Copy)
                last.then_inc(g("rot"), 1)
            for e in range(8):
                i, f = divmod(e, 2)
                act.wait_ge(g("e_mm"), e + 1)
                nc.scalar.activation(m["V"][:, i, f * BANK:(f + 1) * BANK], ps[:, 4 + e % 4, :], ACT.Copy).then_inc(g("e_up"), 1)
            for s in range(64):
                grp, hh = divmod(s, 4)
                i = grp % NI
                e = 8 + s
                act.wait_ge(g("e_mm"), e + 1)
                if grp >= 4 and hh == 0:
                    act.wait_ge(g(f"out{i}"), 16 * (grp // 4))
                s0 = 4 * sum(TRI_L[:i]) + hh * TRI_L[i]
                nc.scalar.activation(m["Ss"][:, s0:s0 + TRI_L[i]], ps[:, 4 + e % 4, 0:(i + 1) * P], ACT.Copy,
                                     scale=AW ** -0.5).then_inc(g("e_up"), 1)
            st.end()
            m = M2
            for s in range(NCHUNK + 1):
                if s < NCHUNK:
                    for k in range(UNITS_TO[s], UNITS_TO[s + 1]):
                        i, _, L = chunk(s)
                        w = SA_R[i] * L
                        act.wait_ge(g("w1"), k + 1)
                        if k >= 3:
                            act.wait_ge(g("w2"), k - 2)
                        nc.scalar.activation(m["hid"][k % 3][:, 0:w], ps[:, HB[k % 3], 0:w], ACT.Gelu, bias=b1A[:, 0:1]).then_inc(g("gelu"), 1)
                if s:
                    c = s - 1
                    L = chunk(c)[2]
                    act.wait_ge(g("negm"), c + 1)
                    for q in range(CH_ROWS):
                        row = m["fin"][:, c % 4, q * L:(q + 1) * L]
                        nc.scalar.activation(row, row, ACT.Exp, bias=m["nm"][:, c % 4, q:q + 1],
                                             accum_out=m["den"][:, c % 4, q:q + 1]).then_inc(g("exp"), 1)

        def a_dve(dve, ch, n, st):
            g = lambda s: sm["A", s]
            m = M1
            for e in range(16):
                rot = m["rot"][:, e % 2, :]
                dve.wait_ge(g("rot"), e + 1)
                ch.link(nc.vector.tensor_tensor(rot, rot, sinA[:, :], ALU.mult))
                ch.link(nc.vector.tensor_tensor(m["qk"][:, e, :], ps[:, e % 4, :], cosA[:, :], ALU.mult))
                nc.vector.tensor_tensor(m["qk"][:, e, :], m["qk"][:, e, :], rot, ALU.add).then_inc(g("qk_up"), 1)
                dve.wait_ge(g("qk_up"), e + 1)
            st.end()
            m = M2
            for s in range(NCHUNK + 3):
                if s < NCHUNK:
                    i, c4, L = chunk(s)
                    R = SA_R[i]
                    slot = s % 4
                    dve.wait_ge(g(f"fin{slot}"), 16 * (s // 4 + 1))
                    for w in range(UNITS_TO[s] // 2, UNITS_TO[s + 1] // 2):
                        q0 = A_UNITS[2 * w][2]
                        dve.wait_ge(g("w2"), 2 * w + 2)
                        rows = m["fin"][:, slot, q0 * L:(q0 + R) * L]
                        nc.vector.tensor_tensor(rows, rows, ps[:, 2 + w % 2, 0:R * L], ALU.add).then_inc(g("mixed"), 1)
                        dve.wait_ge(g("mixed"), w + 1)
                        for q in range(q0, q0 + R):
                            row = m["fin"][:, slot, q * L:(q + 1) * L]
                            t0 = BACK - i * P - (CH_ROWS * c4 + q)
                            last = nc.vector.tensor_tensor(row, row, biasA[:, t0:t0 + L], ALU.add)
                        ch.link(last)
                    ch.link(nc.vector.tensor_reduce(m["nm"][:, slot, :], m["fin"][:, slot, 0:CH_ROWS * L].rearrange("p (q l) -> p q l", q=CH_ROWS), AX.X, ALU.max))
                    nc.vector.tensor_scalar(m["nm"][:, slot, :], m["nm"][:, slot, :], -1.0, None, ALU.mult).then_inc(g("negm"), 1)
                if 2 <= s < NCHUNK + 2:
                    c = s - 2
                    i, c4, L = chunk(c)
                    for j in range(i + 1):
                        t = TURNS_TO[c] + j
                        dve.wait_ge(g("tr"), t + 1)
                        nc.vector.tensor_copy(m["PT"][:, j, CH_ROWS * c4:CH_ROWS * (c4 + 1), :],
                                              ps[:, 4 + t % 2, :].rearrange("p (q c) -> p q c", q=CH_ROWS)).then_inc(g("pt_up"), 1)
                if 1 <= s <= NCHUNK:
                    c = s - 1
                    slot, L = c % 4, chunk(c)[2]
                    dve.wait_ge(g("exp"), CH_ROWS * (c + 1))
                    ch.link(nc.vector.reciprocal(m["den"][:, slot, :], m["den"][:, slot, :]))
                    for q in range(CH_ROWS):
                        row = m["fin"][:, slot, q * L:(q + 1) * L]
                        last = nc.vector.tensor_scalar(row, row, m["den"][:, slot, q:q + 1], None, ALU.mult)
                    last.then_inc(g("prob"), 1)
                if s % 4 == 1 and s >= 5:
                    dve.wait_ge(g("pv"), s // 4)
                    if s > 5:
                        dve.wait_ge(g("y_mm"), s // 4 - 1)
                    for f in range(2):
                        last = nc.vector.tensor_copy(m["OT"][:, 4 * f:4 * f + 4, :], ps[:, 4 + f, :].rearrange("p (t q) -> p t q", t=4))
                    last.then_inc(g("ot_up"), 1)
                if s % 4 == 2 and s >= 6:
                    i = s // 4 - 1
                    dve.wait_ge(g("y_mm"), i + 1)
                    nc.vector.tensor_tensor(x[:, i, :], x[:, i, :], ps[:, 7, 0:DM], ALU.add).then_inc(g("y_up"), 1)

            dve.wait_ge(g("y_up"), NI)

        EXTRA["A"] = dict(pe=a_pe, act=a_act, dve=a_dve, pool=lambda pool, ch, n, st: st.end(), sp=a_sp)

        def ker_mem(sb2):
            m = dict(pad=sb2("k_pad", [P, 9400]))
            for t in ("lp", "la", "b2", "e", "r"):
                m[t] = sb2("k_" + t, [P, 2])
            m["dist"] = sb2("k_dist", [P, NWIN])
            m["ahead"] = sb2("k_ahead", [P, NWIN])
            m["kt"] = sb2("k_kt", [P, NWIN])
            return m

        MK = scope(ker_mem)
        kt_ready = ctx.enter_context(nc.semaphore("kt_ready"))
        kt_act = ctx.enter_context(nc.semaphore("kt_act"))
        kt_dve = ctx.enter_context(nc.semaphore("kt_dve"))
        kt_out = ctx.enter_context(nc.semaphore("kt_out"))
        N_SETUP = 21

        def more_sp(sp):
            sp.dma_start(gateW[:, :, :], io["gateW"].rearrange("(k p) e -> p k e", p=P)).then_inc(setup_loaded, 16)
            sp.dma_start(gateB[:, :], io["gateB"].partition_broadcast(P)).then_inc(setup_loaded, 16)
            for t, n in ((w1A, "w1A"), (w2A, "w2A"), (b1A, "b1A"), (cosA, "cosA"), (sinA, "sinA"), (MK["lp"][:, 0:1], "lp"),
                         (MK["lp"][:, 1:2], "la"), (MK["b2"][:, 0:1], "b2"), (MK["dist"], "dist"), (MK["ahead"], "ahead")):
                sp.dma_start(t if len(n) == 2 else t[:, :], io[n]).then_inc(setup_loaded, 16)
            if "A" in STAGES:
                sp.wait_ge(kt_ready, 1)
                for i in range(NI):
                    L = (i + 1) * P
                    rows = sk[i][AH:2 * AH].rearrange("h (g q) j -> g h q j", g=8)
                    for q in range(16):
                        t0 = BACK - i * P - q
                        sp.dma_start(rows[:, :, q, :], MK["kt"][:, t0:t0 + L]).then_inc(kt_out, 16)
                sp.wait_ge(kt_out, 16 * 64)

        def more_dve(dve):
            m = MK
            n = [0]

            def link(ins):
                n[0] += 1
                ins.then_inc(kt_dve, 1)
                dve.wait_ge(kt_dve, n[0])

            link(nc.vector.tensor_scalar(m["e"][:, :], m["lp"][:, :], -1.0, None, ALU.mult))
            link(nc.vector.tensor_tensor(m["e"][:, :], m["e"][:, :], m["lp"][:, :], ALU.min))
            dve.wait_ge(kt_act, 2)
            link(nc.vector.tensor_scalar(m["r"][:, :], m["lp"][:, :], 0.0, None, ALU.max))
            link(nc.vector.tensor_tensor(m["r"][:, :], m["r"][:, :], m["la"][:, :], ALU.add))
            link(nc.vector.tensor_scalar(m["e"][:, 0:1], m["r"][:, 0:1], -1.0, None, ALU.mult))
            dve.wait_ge(kt_act, 3)
            nc.vector.tensor_scalar(m["kt"][:, :], m["kt"][:, :], m["e"][:, 0:1], None, ALU.mult).then_inc(kt_ready, 1)
            dve.wait_ge(kt_ready, 1)
            nc.vector.scalar_tensor_tensor(out=biasA[:, :], in0=m["kt"][:, :], scalar=m["b2"][:, 0:1], in1=m["ahead"][:, :],
                                           op0=ALU.add, op1=ALU.add)

        def more_act(act):
            m = MK
            act.wait_ge(kt_dve, 2)
            nc.scalar.activation(m["la"][:, :], m["e"][:, :], ACT.Exp).then_inc(kt_act, 1)
            act.wait_ge(kt_act, 1)
            nc.scalar.activation(m["la"][:, :], m["la"][:, :], ACT.Ln, bias=1.0).then_inc(kt_act, 1)
            act.wait_ge(kt_dve, 4)
            nc.scalar.activation(m["kt"][:, :], m["dist"][:, :], ACT.Ln, bias=1.0, scale=m["r"][:, 1:2]).then_inc(kt_act, 1)

        def more_pool(pool):
            nc.gpsimd.memset(tri[:, :, :], 1.0).then_inc(setup_pool_sem, 1)
            nc.gpsimd.memset(selE[:, :, :], 0.0).then_inc(setup_pool_sem, 1)
            pool.wait_ge(setup_pool_sem, 10)
            nc.gpsimd.affine_select(out=tri[:, :, :], in_=tri[:, :, :], compare_op=ALU.is_ge, fill=0.0,
                                    base=-1, pattern=[[1, 8], [-1, 8]], channel_multiplier=0).then_inc(setup_pool_sem, 1)
            for a in range(3):
                nc.gpsimd.affine_select(out=selE[:, :, :], in_=selE[:, :, :], compare_op=ALU.not_equal, fill=1.0,
                                        base=-NE * a, pattern=[[-1, NE], [0, P]], channel_multiplier=1).then_inc(setup_pool_sem, 1)
                pool.wait_ge(setup_pool_sem, 12 + a)

        SETUP_MORE.update(sp=more_sp, pool=more_pool, dve=more_dve, act=more_act)

        def setup_mem(sb2):
            return dict(mi=sb2("mi", [P, NI, CTX], I32), mt=sb2("mt", [P, CTX // P, S], I32), dg=sb2("dg", [P, S]),
                        ones=sb2("ones", [P, P]), cf=sb2("cf", [P, 2, P]), mm=sb2("mm", [P, NI]))

        SU = scope(setup_mem)

        def setup_sp(sp):
            sp.dma_start(SU["mi"][:, :, :], io["mask"].rearrange("(i p) j -> p i j", p=P)).then_inc(setup_loaded, 16)
            sp.dma_start(SU["mt"][:, :, :], io["maskT"].rearrange("(j p) i -> p j i", p=P)).then_inc(setup_loaded, 16)
            for t, n in ((cosD, "cosD"), (sinD, "sinD"), (bqE, "bqE"), (bkE, "bkE")):
                sp.dma_start(t[:, :], io[n]).then_inc(setup_loaded, 16)
            for t, n in ((boB, "boB"), (bvE, "bvE"), (boE, "boE")):
                sp.dma_start(t[:, :], io[n].partition_broadcast(P)).then_inc(setup_loaded, 16)
            SETUP_MORE["sp"](sp)

        def setup_pool(pool):
            nc.gpsimd.memset(half[:, :], -0.5)
            for t in (ident, selden, SU["cf"][:, 0, :], SU["cf"][:, 1, :]):
                nc.gpsimd.memset(t[:, :] if t is ident or t is selden else t, 0.0).then_inc(setup_pool_sem, 1)
            pool.wait_ge(setup_pool_sem, 4)
            nc.gpsimd.affine_select(out=ident[:, :], in_=ident[:, :], compare_op=ALU.not_equal, fill=1.0,
                                    base=0, pattern=[[-1, P]], channel_multiplier=1).then_inc(setup_pool_sem, 1)
            sv = selden[:, :].rearrange("p (a b) -> p a b", a=4)
            nc.gpsimd.affine_select(out=sv, in_=sv, compare_op=ALU.not_equal, fill=1.0,
                                    base=-HD, pattern=[[-32, 4], [0, 32]], channel_multiplier=1).then_inc(setup_pool_sem, 1)
            nc.gpsimd.affine_select(out=SU["cf"][:, 0, :], in_=SU["cf"][:, 0, :], compare_op=ALU.is_ge, fill=NEG,
                                    base=0, pattern=[[-1, P]], channel_multiplier=1).then_inc(setup_pool_sem, 1)
            nc.gpsimd.affine_select(out=SU["cf"][:, 1, :], in_=SU["cf"][:, 1, :], compare_op=ALU.is_ge, fill=NEG,
                                    base=0, pattern=[[1, P]], channel_multiplier=-1).then_inc(setup_pool_sem, 1)
            SETUP_MORE["pool"](pool)

        def setup_vector(dve):
            nc.vector.memset(SU["ones"][:, :], 1.0)
            dve.wait_ge(setup_pool_sem, 8)
            nc.vector.tensor_copy(identb[:, :], ident[:, :])
            nc.vector.tensor_copy(caus[:, :], SU["cf"][:, 0, :])
            nc.vector.tensor_copy(causT[:, :], SU["cf"][:, 1, :])
            dve.wait_ge(setup_loaded, N_SETUP * 16)
            nc.vector.tensor_scalar(mneg[:, :, :], SU["mi"][:, :, :], 0.0, MASKED, ALU.is_equal, ALU.mult).then_inc(setup_dve, 1)
            nc.vector.tensor_scalar(mnegT[:, :, :], SU["mt"][:, :, :], 0.0, MASKED, ALU.is_equal, ALU.mult).then_inc(setup_dve, 1)
            dve.wait_ge(setup_dve, 2)
            nc.vector.tensor_reduce(SU["mm"][:, :], mneg[:, :, :], AX.X, ALU.max).then_inc(setup_dve, 1)
            dve.wait_ge(setup_dve, 3)
            nc.vector.tensor_scalar(livec[:, :], SU["mm"][:, :], -1.0, None, ALU.is_ge).then_inc(setup_dve, 1)
            dve.wait_ge(setup_dve, 4)
            for i in range(NI):
                nc.vector.tensor_scalar(SU["dg"][:, i * P:(i + 1) * P], ident[:, :], livec[:, i:i + 1], None, ALU.mult).then_inc(setup_dve, 1)
                nc.vector.tensor_scalar(mneg[:, i, :], mneg[:, i, :], livec[:, i:i + 1], None, ALU.mult)
            dve.wait_ge(setup_act, 1)
            for j in range(CTX // P):
                nc.vector.tensor_tensor(mnegT[:, j, :], mnegT[:, j, :], live[:, :], ALU.mult)
            SETUP_MORE["dve"](dve)

        def setup_pe(pe):
            pe.wait_ge(setup_dve, 4 + NI)
            nc.tensor.matmul(ps[:, 0, :], SU["ones"][:, :], SU["dg"][:, :], start=True, stop=True).then_inc(setup_pe_sem, 1)

        def setup_scalar(act):
            act.wait_ge(setup_pe_sem, 1)
            nc.scalar.activation(live[:, :], ps[:, 0, :], ACT.Copy).then_inc(setup_act, 1)
            SETUP_MORE["act"](act)

        block = ctx.enter_context(nc.Block())
        SETUP_PHASES = 3

        def load_weights(sp, s):
            sp.dma_start(W(s, 0, WIDTH[s]), io["w" + s]).then_inc(w_loaded[s], 16)

        @block.sync
        def _(sp):
            st = Steps(sp, bars, True)
            setup_sp(sp)
            st.end()
            load_ahead(sp, 0, setup_loaded)
            sp.wait_ge(setup_loaded, 16 * (N_SETUP + 3))
            for _ in range(1, SETUP_PHASES):
                st.end()
            with sp.Fori(0, rounds) as b:
                if ORDER:
                    load_weights(sp, ORDER[0])
                sp.dma_start(ctxT[:, :, :], io["ctxT"][bass.ds(b, 1), :, :].rearrange("o (k p) j -> p (o k) j", p=P)).then_inc(ctx_loaded, 16)
                for n, s in enumerate(STAGES):
                    if s in ORDER and ORDER.index(s) + 1 < len(ORDER):
                        load_weights(sp, ORDER[ORDER.index(s) + 1])
                    if s in CFG:
                        a16_sp(sp, CFG[s])
                    else:
                        EXTRA[s]["sp"](sp, b, n, st)
                    st.end()
                    if s == "B":
                        for (stage, _), sem_b in sm.items():
                            if stage == "B":
                                sp.sem_clear(sem_b)
                sp.dma_start(out[bass.ds(b, 1), :, :].rearrange("o (t p) d -> p (o t) d", p=P), x[:, :, :]).then_inc(x_stored, 16)
                sp.wait_ge(x_stored, 16)
                st.end_round(counting)

        @block.gpsimd
        def _(pool):
            st = Steps(pool, bars, False)
            setup_pool(pool)
            for _ in range(SETUP_PHASES):
                st.end()
            with pool.Fori(0, rounds) as b:
                ch = Chain(pool, pool_chain)
                for n, s in enumerate(STAGES):
                    ln_pool(pool, n)
                    if s in CFG:
                        a16_pool(pool, ch, CFG[s])
                    else:
                        EXTRA[s]["pool"](pool, ch, n, st)
                    st.end()
                st.end_round()

        @block.scalar
        def _(act):
            st = Steps(act, bars, False)
            setup_scalar(act)
            for _ in range(SETUP_PHASES):
                st.end()
            with act.Fori(0, rounds) as b:
                for n, s in enumerate(STAGES):
                    ln_act(act, n)
                    if s in CFG:
                        a16_act(act, CFG[s])
                    else:
                        EXTRA[s]["act"](act, None, n, st)
                    st.end()
                st.end_round()

        @block.vector
        def _(dve):
            st = Steps(dve, bars, False)
            setup_vector(dve)
            for _ in range(SETUP_PHASES):
                st.end()
            with dve.Fori(0, rounds) as b:
                ch = Chain(dve, dve_chain)
                ch.link(nc.vector.tensor_copy(x[:, :, :], M1["x"][:, :, :]))
                for n, s in enumerate(STAGES):
                    ln_dve(dve, ch, n)
                    if s in CFG:
                        a16_dve(dve, ch, CFG[s])
                    else:
                        EXTRA[s]["dve"](dve, ch, n, st)
                    st.end()
                st.end_round()

        @block.tensor
        def _(pe):
            st = Steps(pe, bars, False)
            setup_pe(pe)
            for _ in range(SETUP_PHASES):
                st.end()
            with pe.Fori(0, rounds) as b:
                for n, s in enumerate(STAGES):
                    ln_pe(pe, n)
                    if s in CFG:
                        a16_pe(pe, CFG[s], n)
                    else:
                        EXTRA[s]["pe"](pe, None, n, st)
                    st.end()
                st.end_round()


def lay_out_more(d, a, ktiles):
    import numpy as np

    wo = a["L0_ffn_Wo"].reshape(320, DM)
    wop = np.zeros((3 * P, DM), wo.dtype)
    wop[:320] = wo
    d["wC"] = np.concatenate([ktiles(w) for w in (a["L0_ffn_Wq"], a["L0_ffn_Wk"],
                                                  np.concatenate([a["L0_ffn_Ws"], a["L0_ffn_Wd"]], 1),
                                                  a["L0_ffn_Wv"].transpose(1, 0, 2).reshape(DM, 320), wop)], 1)
    gate = np.concatenate([a["L1_ffn_sh_gate"].reshape(2, P, DM), a["L1_ffn_w_gate"]])
    up = np.concatenate([a["L1_ffn_sh_up"].reshape(2, P, DM), a["L1_ffn_w_up"]])
    down = np.concatenate([a["L1_ffn_sh_down"].reshape(DM, 2, P).transpose(1, 0, 2), a["L1_ffn_w_down"]])

    def feature_rows(w):
        return w.transpose(0, 2, 1).reshape(-1, KD, P, P).transpose(0, 2, 1, 3).reshape(-1, P, DM)

    d["wF"] = np.concatenate([feature_rows(gate), feature_rows(up), down.transpose(0, 2, 1)], 2)
    d["gateW"] = a["L1_ffn_gate_w"].T
    d["gateB"] = a["L1_ffn_gate_bias"]

    d["wA"] = a["L0_attn_w_qkv"]
    d["woA"] = a["L0_attn_w_o"]
    w1, w2 = np.zeros((4, 32, 4, 32), np.float32), np.zeros((4, 32, 4, 16), np.float32)
    for g in range(4):
        w1[g, :, g], w2[g, :, g] = a["L0_attn_w1"], a["L0_attn_w2"]
    d["w1A"], d["w2A"] = w1.reshape(P, P), w2.reshape(P, 64)
    d["b1A"] = np.tile(a["L0_attn_b1"], 4).reshape(P, 1)
    d["lp"], d["la"], d["b2"] = (np.tile(a["L0_attn_" + n].reshape(-1), 8).reshape(P, 1) for n in ("log_p", "log_a", "b2"))
    d["cosA"], d["sinA"] = rope_half_tables()
    off = 399 + 16 * (np.arange(P)[:, None] // 16) - np.arange(528)[None, :]
    d["dist"] = np.abs(off).astype(np.float32)
    d["ahead"] = np.where(off < 0, np.float32(NEG), np.float32(0))


def lay_out(i):
    import numpy as np

    def ktiles(w):
        k = w.shape[0] // P
        return w.reshape(k, P, w.shape[1]).transpose(1, 0, 2).reshape(P, -1)

    def padded_out(w):
        q = np.zeros((NH, 32, w.shape[1]), w.dtype)
        q[:, :HD, :] = w.reshape(NH, HD, -1)
        return ktiles(q.reshape(NH * 32, -1))

    a = {k: np.asarray(v) for k, v in i.items()}
    swap = np.arange(DM) ^ 1
    d = {}
    d["x"] = np.concatenate([a["x"], a["x"][:1]])
    d["ctxT"] = a["ctx_1024"].transpose(0, 2, 1)
    mask = a["mask_1x1xSxS2_ik0"][0, 0]
    d["mask"], d["maskT"] = mask, mask.T
    d["cosD"], d["sinD"] = rope_pair_tables()
    d["wB"] = np.concatenate([ktiles(a["L0_xattn_" + n].T) for n in ("Wq", "Wk", "Wv")] + [padded_out(a["L0_xattn_Wo"].T)], 1)
    d["boB"] = a["L0_xattn_bo"]
    wd = a["L1_attn_W_qkv"]
    q, k, v = wd[:DM], wd[DM:2 * DM], wd[2 * DM:]
    d["wD"] = np.concatenate([ktiles(w.T) for w in (q, q[swap], k, k[swap], v)] + [padded_out(a["L1_attn_W_o"].T)], 1)
    d["wE"] = np.concatenate([ktiles(a["L1_xattn_" + n].T) for n in ("w_q", "w_k", "w_v")] + [padded_out(a["L1_xattn_w_o"].T)], 1)
    d["bqE"] = a["L1_xattn_b_q"].reshape(2, P).T
    d["bkE"] = a["L1_xattn_b_k"].reshape(2, P).T
    d["bvE"], d["boE"] = a["L1_xattn_b_v"], a["L1_xattn_b_o"]
    lay_out_more(d, a, ktiles)
    return {n: np.ascontiguousarray(v) for n, v in d.items()}


def kernel(**inputs):
    import concourse.bacc as _bacc
    from concourse import mybir as _mybir
    from concourse.bass_utils import run_bass_kernel_spmd as _run

    nc = _bacc.Bacc("TRN2", target_bir_lowering=False, num_devices=1)
    arrays, io = {}, {}
    for name, a in lay_out(inputs).items():
        arrays[f"in_{name}"] = a
        io[name] = nc.dram_tensor(f"in_{name}", a.shape, _mybir.dt.from_np(a.dtype), kind="ExternalInput").ap()
    out = nc.dram_tensor("out_0", (B, S, DM), _mybir.dt.float32, kind="ExternalOutput").ap()
    decoder(nc, io, out, 4)
    r = _run(nc, [arrays], core_ids=[0])
    return r.results[0]["out_0"]
```

```python
import numpy as np
import concourse.bass as bass
from concourse import mybir
from contextlib import ExitStack

F32 = mybir.dt.float32
BF16 = mybir.dt.bfloat16
I32 = mybir.dt.int32
ALU = mybir.AluOpType
ACT = mybir.ActivationFunctionType
AX = mybir.AxisListType

P = 128
B, S, DM = 4, 512, 256
NI = S // P
KD = DM // P
CTX = 1024
BANK = 512
NEG = -1e30
MASKED = -float(2 ** 30)
STAGES = "ABCDEF"


def rope_half_tables():
    d = 64
    inv = (1.0 / 10000.0 ** (np.arange(0, d, 2, dtype=np.float32) / np.float32(d))).astype(np.float32)
    ang = np.outer(np.arange(S, dtype=np.float32), inv).astype(np.float32)
    ang = np.concatenate([ang, ang], -1).T
    cos, sin = np.cos(ang.astype(np.float64)), np.sin(ang.astype(np.float64))
    sin[: d // 2] = -sin[: d // 2]
    return np.tile(cos, (2, 1)).astype(np.float32), np.tile(sin, (2, 1)).astype(np.float32)


def rope_pair_tables():
    d = 16
    inv = (np.float32(10000.0) ** (np.arange(0, d, 2, dtype=np.float32) / np.float32(d))).astype(np.float32)
    ang = (np.arange(S, dtype=np.float32)[:, None] / inv[None, :]).astype(np.float32)
    ang = np.repeat(ang, 2, axis=1).T
    cos, sin = np.cos(ang.astype(np.float64)), np.sin(ang.astype(np.float64))
    sin[0::2] = -sin[0::2]
    return np.tile(cos, (8, 1)).astype(np.float32), np.tile(sin, (8, 1)).astype(np.float32)


class Chain:

    def __init__(self, eng, sem):
        self.eng, self.sem, self.n = eng, sem, 0

    def link(self, ins):
        self.n += 1
        ins.then_inc(self.sem, 1)
        self.eng.wait_ge(self.sem, self.n)


class Steps:

    def __init__(self, eng, bars, clears):
        self.eng, self.bars, self.clears, self.k = eng, bars, clears, 0

    def end(self):
        k = self.k % 3
        self.k += 1
        self.eng.drain().then_inc(self.bars[k], 1)
        self.eng.wait_ge(self.bars[k], 5)
        if self.clears:
            self.eng.sem_clear(self.bars[(k - 1) % 3])

    def end_round(self, sems=()):
        self.end()
        if self.clears:
            for s in sems:
                self.eng.sem_clear(s)
        self.end()
        while self.k % 3:
            self.end()


class Attn16:

    def __init__(self, name, nk, causal, masked, rope, cross):
        self.name, self.nk, self.causal, self.masked, self.rope, self.cross = name, nk, causal, masked, rope, cross
        self.nj = nk // P
        self.halves = nk // BANK
        if cross:
            self.tiles = [("k", t, f) for t in range(2) for f in range(self.halves)] + [("q", 0, 0), ("q", 1, 0)]
            self.moves = [("out", "k", 0), ("in", "k", 0), ("out", "k", 1), ("out", "q", 0), ("in", "q", 0), ("in", "k", 1),
                          ("out", "q", 1), ("in", "q", 1)]
        else:
            self.tiles = [(kind, t, 0) for t in range(2) for kind in "kq"]
            self.moves = [(way, kind, t) for t in range(2) for way in ("out", "in") for kind in "kq"]
        self.step = 2 if rope else 1
        self.s_banks = [0, 1]
        self.banks_deep = 4 if cross else 6 // self.step
        if causal:
            self.s_tiles = [(i, 0, (i + 1) * P) for i in range(NI)]
            self.units = [[j] for j in range(self.nj)]
        else:
            self.s_tiles = [(i, f * BANK, BANK) for i in range(NI) for f in range(self.halves)]
            self.units = [[2 * u, 2 * u + 1] for u in range(self.nj // 2)]


    def bank(self, e):
        return 2 + e % 4 if self.cross else self.step * e % 6


NH = 16
HD = 16
NE, NSH = 32, 2
WARM_LN, WARM_T, WARM_STACK = 22, 6, 22
NRING = 6
CB = Attn16("B", CTX, False, False, False, True)
CD = Attn16("D", S, True, False, True, False)
CE = Attn16("E", CTX, False, True, False, True)
CFG = {"B": CB, "D": CD, "E": CE}
QPART = [0, 0, 1, 0, 1, 2]
KPART = [0, 1, 0, 2, 1, 0]
KR = 6 * HD
KST = KR + 3
Y_BANKS = [0, 1, 4, 5]


def decoder(nc, io, out, rounds=B):
    ctx = ExitStack()
    with ctx:
        def sb(name, shape, dt=F32):
            return ctx.enter_context(nc.sbuf_tensor(name, shape, dt))

        def sem(name):
            s = ctx.enter_context(nc.semaphore(name))
            counting.append(s)
            return s

        counting = []

        x = sb("x", [P, NI, DM])
        xn = sb("xn", [P, NI, DM])
        xnT = sb("xnT", [P, KD, S])
        ctxT = sb("ctxT", [P, KD, CTX])
        ident = sb("ident", [P, P])
        identb = sb("identb", [P, P], BF16)
        caus = sb("caus", [P, P], BF16)
        causT = sb("causT", [P, P], BF16)
        selden = sb("selden", [P, P])
        mneg = sb("mneg", [P, NI, CTX], BF16)
        mnegT = sb("mnegT", [P, CTX // P, S], BF16)
        live = sb("live", [P, S])
        livec = sb("livec", [P, NI])
        half = sb("half", [P, NI])
        st6 = sb("st6", [P, NI, 6])
        mv = sb("mv", [P, NI, 2])
        rstd = sb("rstd", [P, NI])
        rt = sb("rt", [P, NI])
        cosD = sb("cosD", [P, S])
        sinD = sb("sinD", [P, S])
        boB = sb("boB", [P, DM])
        bvE = sb("bvE", [P, DM])
        boE = sb("boE", [P, DM])
        ones = sb("ones_row", [1, P])
        bqE = sb("bqE", [P, 2])
        bkE = sb("bkE", [P, 2])
        tri = sb("tri", [P, 8, 8])
        selE = sb("selE", [96, NE, P], BF16)
        gateW = sb("gateW", [P, KD, NE])
        gateB = sb("gateB", [P, NE])
        NWIN = 528
        biasA = sb("biasA", [P, NWIN])
        w1A = sb("w1A", [P, P])
        w2A = sb("w2A", [P, 64])
        b1A = sb("b1A", [P, 1])
        cosA = sb("cosA", [P, S])
        sinA = sb("sinA", [P, S])
        WCOLS = 3712
        wbuf = sb("wbuf", [P, 2, WCOLS])
        ps = ctx.enter_context(nc.psum_tensor("ps", [P, 8, BANK], F32))

        bars = [ctx.enter_context(nc.semaphore(f"phase{k}")) for k in range(3)]
        setup_loaded = ctx.enter_context(nc.semaphore("setup_loaded"))
        setup_dve = ctx.enter_context(nc.semaphore("setup_dve"))
        setup_pool_sem = ctx.enter_context(nc.semaphore("setup_pool"))
        setup_pe_sem = ctx.enter_context(nc.semaphore("setup_pe"))
        setup_act = ctx.enter_context(nc.semaphore("setup_act"))
        ctx_loaded = sem("ctx_loaded")
        x_stored = sem("x_stored")
        dve_chain = sem("dve_chain")
        pool_chain = sem("pool_chain")
        ln_var = sem("ln_var")
        ln_pow = sem("ln_pow")
        ln_xn = sem("ln_xn")
        ln_tr = sem("ln_tr")
        ln_T = sem("ln_T")
        w_loaded = {s: sem(f"w_loaded_{s}") for s in "BCDE"}
        sm = {}
        for c in CFG:
            if c in STAGES:
                for n in ("proj", "val", "split", "v_mm", "v_up", "v_zero", "k_ones", "part_out", "stack_in0", "stack_in1", "s_mm", "s_max",
                          "m_parts", "m_mm", "m_row", "st_mm", "exp", "pv", "o_up", "den_mm", "den_up", "recip", "o_norm", "y_mm"):
                    sm[c, n] = sm["B", n] if c == "D" and "B" in STAGES else sem(f"{n}_{c}")

        def scope(fn):
            with ExitStack() as inner:
                return fn(lambda name, shape, dt=F32: inner.enter_context(nc.sbuf_tensor(name, shape, dt)))

        NVAL = 4

        def attn16_mem(sb2):
            m = {}
            m["QS"] = sb2("QS", [P, NH, S], BF16)
            m["KS"] = sb2("KS", [P, NH, CTX], BF16)
            m["VP"] = sb2("VP", [P, CTX // P, NH, 32])
            m["val"] = sb2("val", [P, NVAL, BANK])
            m["rope"] = sb2("rope", [P, BANK])
            m["rest"] = sb2("rest", [P, BANK])
            m["mx"] = sb2("mx", [P, 2, NI, 2])
            m["nm"] = sb2("nm", [P, NI])
            m["nr"] = sb2("nr", [P, NI])
            m["nmp"] = sb2("nmp", [P, 2, NI, 3], BF16)
            m["PT"] = sb2("PT", [P, 2, 2, BANK])
            m["OT"] = sb2("OT", [P, 4, S])
            m["rec"] = sb2("rec", [P, BANK])
            m["den"] = m["rope"]
            m.update(scope(lambda sb3: dict(QP=sb3("QP", [P, 3, 2, S], BF16), KP=sb3("KP", [P, 3, 2, CTX], BF16))))
            m["ON"] = sb2("ON", [P, 4, S])
            return m

        M16 = scope(attn16_mem)
        qd = nc.dram_tensor("qparts", (3, 2, P, S), BF16, kind="Internal").ap()
        kd = nc.dram_tensor("kparts", (3, 2, P, CTX), BF16, kind="Internal").ap()

        WIDTH = {"B": 2560, "D": 3584, "E": 2560, "C": 3616}
        ORDER = [s for s in "BCDE" if s in STAGES]
        slot_of = {s: n % 2 for n, s in enumerate(ORDER)}

        def W(stage, first, cols):
            return wbuf[:, slot_of[stage], first:first + cols]

        def ln_dve(dve, ch, n):
            for i in range(NI):
                last = nc.vector.bn_stats(out=st6[:, i, :], in_=x[:, i, :])
            ch.link(last)
            for i in range(NI):
                last = nc.vector.bn_aggr(out=mv[:, i, :], in_=st6[:, i, :])
            ch.link(last)
            nc.vector.tensor_scalar(mv[:, :, 1], mv[:, :, 1], 1e-5, None, ALU.add).then_inc(ln_var, 1)
            dve.wait_ge(ln_pow, n + 1)
            ch.link(nc.vector.tensor_tensor(rt[:, :], rstd[:, :], rstd[:, :], ALU.mult))
            ch.link(nc.vector.tensor_tensor(rt[:, :], rt[:, :], mv[:, :, 1], ALU.mult))
            ch.link(nc.vector.tensor_scalar(rt[:, :], rt[:, :], -0.5, 1.5, ALU.mult, ALU.add))
            ch.link(nc.vector.tensor_tensor(rstd[:, :], rstd[:, :], rt[:, :], ALU.mult))
            for i in range(NI):
                nc.vector.tensor_scalar(xn[:, i, :], x[:, i, :], mv[:, i, 0:1], rstd[:, i:i + 1],
                                        ALU.subtract, ALU.mult).then_inc(ln_xn, 1)

        def ln_pool(pool, n):
            pool.wait_ge(ln_var, n + 1)
            nc.gpsimd.tensor_tensor(rstd[:, :], mv[:, :, 1], half[:, :], ALU.pow).then_inc(ln_pow, 1)

        def keep_warm(count, bank=7):
            for _ in range(count):
                nc.tensor.matmul(ps[:, bank, :], identb[:, :], mneg[:, 0, 0:BANK], start=True, stop=True)

        def ln_pe(pe, n):
            for i in range(NI):
                pe.wait_ge(ln_xn, NI * n + i + 1)
                for k in range(KD):
                    last = nc.tensor.transpose(ps[:, k, i * P:(i + 1) * P], xn[:, i, k * P:(k + 1) * P], ident[:, :])
            last.then_inc(ln_tr, 1)

        def ln_act(act, n):
            act.wait_ge(ln_tr, n + 1)
            for k in range(KD):
                last = nc.scalar.activation(xnT[:, k, :], ps[:, k, :], ACT.Copy)
            last.then_inc(ln_T, 1)

        def a16_sp(sp, c):
            m = M16
            g = lambda n: sm[c.name, n]
            outs = 0
            for way, kind, t in c.moves:
                dram, parts, stack = (qd, m["QP"], m["QS"]) if kind == "q" else (kd, m["KP"], m["KS"])
                n = S if kind == "q" else c.nk
                if way == "out":
                    last = max(e for e, tile in enumerate(c.tiles) if tile[:2] == (kind, t))
                    sp.wait_ge(g("split"), last + 1)
                    outs += 1
                    sp.dma_start(dram[:, t, :, 0:n].rearrange("a p n -> p a n"), parts[:, :, t, 0:n]).then_inc(g("part_out"), 16)
                    continue
                sp.wait_ge(g("part_out"), 16 * outs)
                for r in range(6):
                    src = dram[(QPART if kind == "q" else KPART)[r], t, :, 0:n].rearrange("(e d) n -> d e n", d=HD)
                    sp.dma_start(stack[HD * r:HD * r + HD, 8 * t:8 * t + 8, 0:n], src).then_inc(g(f"stack_in{t}"), 16)

        def a16_pool(pool, ch, c):
            m = M16
            ch.link(nc.gpsimd.memset(m["VP"][:, :, :, :], 0.0))
            nc.gpsimd.memset(m["VP"][:, :, :, HD:HD + 1], 1.0).then_inc(sm[c.name, "v_zero"], 1)
            pool.wait_ge(sm[c.name, "v_zero"], 1)
            nc.gpsimd.memset(m["KS"][KR:KST, :, 0:c.nk], 1.0).then_inc(sm[c.name, "k_ones"], 1)
            pool.wait_ge(sm[c.name, "k_ones"], 1)
            for q in range(3):
                pool.wait_ge(sm[c.name, "recip"], NI * (q + 1))
                nc.gpsimd.tensor_tensor(m["ON"][:, q, :], m["OT"][:, q, :], m["rec"][:, :], ALU.mult).then_inc(sm[c.name, "o_norm"], 1)

        def a16_pe(pe, c, n):
            m = M16
            g = lambda s: sm[c.name, s]
            src = ctxT if c.cross else xnT
            nw = 4 if c.rope else 2
            wq, wk = 0, (2 if c.rope else 1) * KD * DM
            wv = nw * KD * DM
            wo = wv + KD * DM
            pe.wait_ge(w_loaded[c.name], 16)
            if c.cross:
                pe.wait_ge(ctx_loaded, 16)
            def project(e):
                kind, t, f = c.tiles[e]
                if e >= c.banks_deep:
                    pe.wait_ge(g("val"), e - c.banks_deep + 1)
                for v in range(c.step):
                    base = (wq if kind == "q" else wk) + v * KD * DM
                    for k in range(KD):
                        rhs = xnT[:, k, :] if kind == "q" else src[:, k, f * BANK:(f + 1) * BANK]
                        last = nc.tensor.matmul(ps[:, c.bank(e) + v, :], W(c.name, base + k * DM + t * P, P), rhs,
                                                start=(k == 0), stop=(k == KD - 1))
                last.then_inc(g("proj"), 1)

            def values(j):
                if j >= 2:
                    pe.wait_ge(g("v_up"), j - 1)
                for e in range(2):
                    jt = 2 * j + e
                    o = ps[:, 6 + j % 2, e * DM:(e + 1) * DM]
                    for k in range(KD):
                        last = nc.tensor.matmul(o, src[:, k, jt * P:(jt + 1) * P],
                                                W(c.name, wv + k * DM, DM), start=(k == 0), stop=(k == KD - 1 and not c.masked))
                    if c.masked:
                        last = nc.tensor.matmul(o, ones[:, :], bvE[0:1, :], start=False, stop=True)
                last.then_inc(g("v_mm"), 1)

            if c.cross:
                for e in range(4):
                    project(e)
                ln_pe(pe, n)
                values(0)
                pe.wait_ge(ln_T, n + 1)
                for e in (4, 5):
                    project(e)
            else:
                keep_warm(WARM_LN)
                ln_pe(pe, n)
                keep_warm(WARM_T)
                pe.wait_ge(ln_T, n + 1)
                for e in range(4):
                    project(e)
                values(0)
            for j in range(1, c.nj // 2):
                values(j)
            pe.wait_ge(g("v_up"), c.nj // 2)
            pe.wait_ge(g("val"), len(c.tiles))
            keep_warm(WARM_STACK)
            ns, nu = len(c.s_tiles), len(c.units)

            def scores(h, tiles):
                if h % 8 == 0 and 0 in tiles:
                    pe.wait_ge(g(f"stack_in{h // 8}"), 12 * 16)
                for e in tiles:
                    s = h * ns + e
                    i, f, w = c.s_tiles[e]
                    n = len(c.s_banks)
                    if s >= n:
                        pe.wait_ge(g("s_max"), s - n + 1)
                    bank = c.s_banks[s % n]
                    o = ps[:, bank, 0:w]
                    plain = not (c.causal or c.masked)
                    last = nc.tensor.matmul(o, m["QS"][0:KR, h, i * P:(i + 1) * P], m["KS"][0:KR, h, f:f + w],
                                            start=True, stop=plain)
                    if c.causal:
                        last = nc.tensor.matmul(ps[:, bank, i * P:(i + 1) * P], identb[:, :], caus[:, :], start=False, stop=True)
                    if c.masked:
                        last = nc.tensor.matmul(o, identb[:, :], mneg[:, i, f:f + w], start=False, stop=True)
                    last.then_inc(g("s_mm"), 1)

            def max_row(h):
                pe.wait_ge(g("m_parts"), h + 1)
                if h:
                    pe.wait_ge(g("m_row"), h)
                if h >= 6 and h % 4 == 2:
                    pe.wait_ge(g("den_up"), (h - 2) // 4)
                for i in range(NI):
                    last = nc.tensor.matmul(ps[KR:KST, 7, i * P:(i + 1) * P], m["nmp"][:, h % 2, i, :], identb[:, :],
                                            start=True, stop=True)
                last.then_inc(g("m_mm"), 1)

            def scores_t(h, u):
                gu = h * nu + u
                if gu == 0:
                    pe.wait_ge(g("k_ones"), 1)
                if u == 0:
                    pe.wait_ge(g("m_row"), h + 1)
                if gu >= 2:
                    pe.wait_ge(g("exp"), gu - 1)
                for e, j in enumerate(c.units[u]):
                    q0 = j * P if c.causal else 0
                    o = ps[:, 2 + 2 * (gu % 2) + e, 0:S - q0]
                    plain = not (c.causal or c.masked)
                    last = nc.tensor.matmul(o, m["KS"][0:KST, h, j * P:(j + 1) * P], m["QS"][0:KST, h, q0:S],
                                            start=True, stop=plain)
                    if c.causal:
                        last = nc.tensor.matmul(o[:, 0:P], identb[:, :], causT[:, :], start=False, stop=True)
                    if c.masked:
                        last = nc.tensor.matmul(o, identb[:, :], mnegT[:, j, :], start=False, stop=True)
                last.then_inc(g("st_mm"), 1)

            def weighted(h, u):
                gu = h * nu + u
                pe.wait_ge(g("exp"), gu + 1)
                if h % 4 == 0 and u == 0 and h:
                    pe.wait_ge(g("o_up"), h // 4)
                for e, j in enumerate(c.units[u]):
                    q0 = j * P if c.causal else 0
                    r = 32 * (h % 4)
                    last = nc.tensor.matmul(ps[r:r + 32, 6, q0:S], m["VP"][:, j, h, :], m["PT"][:, gu % 2, e, 0:S - q0],
                                            start=(j == 0), stop=(j == c.nj - 1), tile_position=(0, r))
                last.then_inc(g("pv"), 1)

            def denominators(q):
                pe.wait_ge(g("o_up"), q + 1)
                nc.tensor.matmul(ps[:, 7, :], selden[:, :], m["OT"][:, q, :], start=True, stop=True).then_inc(g("den_mm"), 1)

            scores(0, range(ns))
            scores(1, range(ns))
            max_row(0)
            before = None
            share = ns // nu
            for h in range(NH):
                for u in range(nu):
                    scores_t(h, u)
                    if u == 0 and h >= 5 and h % 4 == 1:
                        denominators(h // 4 - 1)
                    if u == 1 and h + 1 < NH:
                        max_row(h + 1)
                    if h + 2 < NH:
                        scores(h + 2, range(u * share, (u + 1) * share))
                    if before:
                        weighted(*before)
                    before = (h, u)
            weighted(*before)
            denominators(3)
            for i in range(NI):
                pe.wait_ge(g("o_norm"), 3)
                for q in range(3):
                    nc.tensor.matmul(ps[:, Y_BANKS[i], 0:DM], m["ON"][:, q, i * P:(i + 1) * P],
                                     W(c.name, wo + q * DM, DM), start=(q == 0), stop=False)
            for i in range(NI):
                pe.wait_ge(g("o_norm"), 3 + i + 1)
                nc.tensor.matmul(ps[:, Y_BANKS[i], 0:DM], m["ON"][:, 3, i * P:(i + 1) * P],
                                 W(c.name, wo + 3 * DM, DM), start=False, stop=True).then_inc(g("y_mm"), 1)

        def a16_act(act, c, n):
            m = M16
            g = lambda s: sm[c.name, s]
            def val(e):
                kind, t, f = c.tiles[e]
                act.wait_ge(g("proj"), e + 1)
                if e >= NVAL:
                    act.wait_ge(g("split"), e - NVAL + 1)
                o = m["val"][:, e % NVAL, :]
                if c.masked:
                    nc.scalar.activation(o, ps[:, c.bank(e), :], ACT.Identity, bias=(bqE if kind == "q" else bkE)[:, t:t + 1]).then_inc(g("val"), 1)
                else:
                    nc.scalar.activation(o, ps[:, c.bank(e), :], ACT.Copy).then_inc(g("val"), 1)

            def values(j):
                act.wait_ge(g("v_mm"), j + 1)
                nc.scalar.activation(m["VP"][:, 2 * j:2 * j + 2, :, 0:HD],
                                     ps[:, 6 + j % 2, :].rearrange("p (j h d) -> p j h d", j=2, d=HD), ACT.Copy).then_inc(g("v_up"), 1)

            if c.cross:
                for e in range(4):
                    val(e)
            ln_act(act, n)
            act.wait_ge(g("v_zero"), 1)
            values(0)
            if c.cross:
                for e in (4, 5):
                    val(e)
            for j in range(1, c.nj // 2):
                values(j)
            nu = len(c.units)

            def row(h):
                act.wait_ge(g("m_mm"), h + 1)
                nc.scalar.activation(m["QS"][KR:KST, h, :], ps[KR:KST, 7, :], ACT.Copy).then_inc(g("m_row"), 1)

            def denominators(q):
                act.wait_ge(g("den_mm"), q + 1)
                if q:
                    act.wait_ge(g("recip"), NI * q)
                nc.scalar.activation(m["den"][:, :], ps[:, 7, :], ACT.Copy).then_inc(g("den_up"), 1)

            row(0)
            for h in range(NH):
                for u in range(nu):
                    gu = h * nu + u
                    act.wait_ge(g("st_mm"), gu + 1)
                    if gu >= 2:
                        act.wait_ge(g("pv"), gu - 1)
                    n = len(c.units[u])
                    w = S - c.units[u][0] * P if c.causal else S
                    b0 = 2 + 2 * (gu % 2)
                    nc.scalar.activation(m["PT"][:, gu % 2, 0:n, 0:w], ps[:, b0:b0 + n, 0:w], ACT.Exp,
                                         scale=HD ** -0.5).then_inc(g("exp"), 1)
                    if u == 0 and h >= 5 and h % 4 == 1:
                        denominators(h // 4 - 1)
                    if u == 1 and h + 1 < NH:
                        row(h + 1)
            denominators(3)

        def a16_dve(dve, ch, c):
            m = M16
            g = lambda s: sm[c.name, s]

            def parts(dst, src, rest, last_sem):
                ch.link(nc.vector.tensor_copy(dst(0), src))
                ch.link(nc.vector.tensor_tensor(rest, src, dst(0), ALU.subtract))
                ch.link(nc.vector.tensor_copy(dst(1), rest))
                nc.vector.tensor_tensor(dst(2), rest, dst(1), ALU.subtract).then_inc(last_sem, 1)

            for e, (kind, t, f) in enumerate(c.tiles):
                if c.rope:
                    dve.wait_ge(g("proj"), e + 1)
                    b0 = c.bank(e)
                    if e >= 1:
                        dve.wait_ge(g("split"), e)
                    ch.link(nc.vector.tensor_tensor(m["rope"][:, :], ps[:, b0 + 1, :], sinD[:, :], ALU.mult))
                    ch.link(nc.vector.tensor_tensor(m["val"][:, e % NVAL, :], ps[:, b0, :], cosD[:, :], ALU.mult))
                    nc.vector.tensor_tensor(m["val"][:, e % NVAL, :], m["val"][:, e % NVAL, :], m["rope"][:, :], ALU.add).then_inc(g("val"), 1)
                dve.wait_ge(g("val"), e + 1)
                if c.masked and kind == "q":
                    ch.link(nc.vector.tensor_tensor(m["val"][:, e % NVAL, :], m["val"][:, e % NVAL, :], live[:, :], ALU.mult))
                if e >= 1:
                    dve.wait_ge(g("split"), e)
                dst = (lambda a: m["QP"][:, a, t, :]) if kind == "q" else (lambda a: m["KP"][:, a, t, f * BANK:(f + 1) * BANK])
                parts(dst, m["val"][:, e % NVAL, :], m["rest"][:, :], g("split"))
            ns, nu = len(c.s_tiles), len(c.units)

            def recip(q, i):
                if i == 0:
                    dve.wait_ge(g("den_up"), q + 1)
                    if q:
                        dve.wait_ge(g("o_norm"), q)
                t = slice(i * P, (i + 1) * P)
                nc.vector.reciprocal(m["rec"][:, t], m["den"][:, t]).then_inc(g("recip"), 1)

            def maxima(h, q=None):
                for e, (i, f, w) in enumerate(c.s_tiles):
                    s = h * ns + e
                    dve.wait_ge(g("s_mm"), s + 1)
                    nc.vector.tensor_reduce(m["mx"][:, h % 2, i, f // BANK:f // BANK + 1], ps[:, c.s_banks[s % len(c.s_banks)], 0:w], AX.X, ALU.max).then_inc(g("s_max"), 1)
                    if q is not None and e < NI:
                        recip(q, e)
                dve.wait_ge(g("s_max"), (h + 1) * ns)
                if c.halves == 2:
                    ch.link(nc.vector.tensor_tensor(m["nm"][:, :], m["mx"][:, h % 2, :, 0], m["mx"][:, h % 2, :, 1], ALU.max))
                    ch.link(nc.vector.tensor_scalar(m["nm"][:, :], m["nm"][:, :], -1.0, None, ALU.mult))
                else:
                    ch.link(nc.vector.tensor_scalar(m["nm"][:, :], m["mx"][:, h % 2, :, 0], -1.0, None, ALU.mult))
                if h >= 2:
                    dve.wait_ge(g("m_mm"), h - 1)
                parts(lambda a: m["nmp"][:, h % 2, :, a], m["nm"][:, :], m["nr"][:, :], g("m_parts"))
                dve.wait_ge(g("m_parts"), h + 1)

            maxima(0)
            maxima(1)
            for h in range(NH):
                q = h // 4 - 1 if h % 4 == 2 and h > 4 else None
                if h + 2 < NH:
                    maxima(h + 2, q)
                elif q is not None:
                    for i in range(NI):
                        recip(q, i)
                if h % 4 == 3:
                    dve.wait_ge(g("pv"), (h + 1) * nu)
                    nc.vector.tensor_copy(m["OT"][:, h // 4, :], ps[:, 6, :]).then_inc(g("o_up"), 1)
            for i in range(NI):
                recip(3, i)
                dve.wait_ge(g("recip"), 3 * NI + i + 1)
                t = slice(i * P, (i + 1) * P)
                nc.vector.tensor_tensor(m["ON"][:, 3, t], m["OT"][:, 3, t], m["rec"][:, t], ALU.mult).then_inc(g("o_norm"), 1)
            for i in range(NI):
                dve.wait_ge(g("y_mm"), i + 1)
                ch.link(nc.vector.tensor_tensor(x[:, i, :], x[:, i, :], ps[:, Y_BANKS[i], 0:DM], ALU.add))
                bo = {"B": boB, "E": boE}.get(c.name)
                if bo is not None:
                    ch.link(nc.vector.tensor_tensor(x[:, i, :], x[:, i, :], bo[:, :], ALU.add))
        EXTRA = {}
        SETUP_MORE = {}

        def named(prefix, *names):
            if prefix in STAGES:
                for n in names:
                    sm[prefix, n] = sem(f"{n}_{prefix}")


        def spread(ap, axis, shape):
            return ap.unsqueeze(axis).broadcast_to(shape)

        def top_mask(ch, v, groups, n, keep, c1, c2, mask):
            shape = [P, groups, n, n]
            other, own = spread(v, 2, shape), spread(v, 3, shape)
            earlier = spread(tri[:, 0:n, 0:n], 1, shape)
            ch.link(nc.vector.tensor_tensor(c1, other, own, ALU.is_gt))
            ch.link(nc.vector.tensor_tensor(c2, other, own, ALU.is_equal))
            ch.link(nc.vector.tensor_tensor(c2, c2, earlier, ALU.mult))
            ch.link(nc.vector.tensor_tensor(c1, c1, c2, ALU.add))
            ch.link(nc.vector.tensor_reduce(mask, c1, AX.X, ALU.add))
            ch.link(nc.vector.tensor_scalar(mask, mask, keep - 0.5, None, ALU.is_lt))

        CH, CW, CN = 8, 64, 5
        named("C", "gated", "gl_mm", "sig", "gl_free", "xv_mm", "xv_up", "qk_mm", "qk_up", "s_mm", "negm", "exp", "tr", "pt_up", "v_up", "pv",
              "o_up", "ob_mm", "attn", "ae_pool", "ae_dve", "aet_mm", "aet_up", "y_mm")

        def c_mem(sb2):
            m = {}
            m["qk"] = sb2("c_qk", [P, 8, S])
            m["gl"] = sb2("c_gl", [P, NI * 2 * CH, CN])
            m["msk"] = sb2("c_msk", [P, NI * 2 * CH, CN])
            m["c1"] = sb2("c_c1", [P, NI * 2 * CH, CN, CN])
            m["c2"] = sb2("c_c2", [P, NI * 2 * CH, CN, CN])
            m["sg"] = sb2("c_sg", [P, NI, 2 * CH * CN])
            m["xv"] = sb2("c_xv", [P, NI, CN * CW])
            m["V"] = sb2("c_V", [P, NI, CH * CW])
            m["tmp"] = sb2("c_tmp", [P, 2, CH * CW])
            m["Pr"] = sb2("c_P", [P, 2, S])
            m["PT"] = sb2("c_PT", [P, 2, NI, S])
            m["nm"] = sb2("c_nm", [P, CH * NI])
            m["den"] = sb2("c_den", [P, NI, CH])
            m["rden"] = sb2("c_rden", [P, NI, CH])
            m["OT"] = sb2("c_OT", [P, 2, S])
            m["at"] = sb2("c_at", [P, NI, P])
            m["ae"] = sb2("c_ae", [P, NI, CN * CW])
            m["aeT"] = sb2("c_aeT", [P, 3, S])
            return m

        MC = scope(c_mem)
        C_Q, C_K, C_G, C_X, C_O = 0, 1024, 2048, 2208, 2848
        KT_AE = [P, P, CN * CW - 2 * P]

        def c_pe(pe, _, n, st):
            m = MC
            g = lambda s: sm["C", s]
            pe.wait_ge(w_loaded["C"], 16)
            pe.wait_ge(ln_T, n + 1)
            for i in range(NI):
                for k in range(KD):
                    last = nc.tensor.matmul(ps[:, 0, i * 80:(i + 1) * 80], xnT[:, k, i * P:(i + 1) * P],
                                            W("C", C_G + 80 * k, 80), start=(k == 0), stop=(k == KD - 1))
            last.then_inc(g("gl_mm"), 1)
            for i in range(NI):
                for k in range(KD):
                    last = nc.tensor.matmul(ps[:, 1 + i, 0:320], xnT[:, k, i * P:(i + 1) * P],
                                            W("C", C_X + 320 * k, 320), start=(k == 0), stop=(k == KD - 1))
                last.then_inc(g("xv_mm"), 1)
            for e in range(8):
                if e >= 3:
                    pe.wait_ge(g("qk_up"), e - 2)
                base = (C_Q if e < 4 else C_K) + (e % 4) * P
                for k in range(KD):
                    last = nc.tensor.matmul(ps[:, 5 + e % 3, :], W("C", base + 512 * k, P), xnT[:, k, :],
                                            start=(k == 0), stop=(k == KD - 1))
                last.then_inc(g("qk_mm"), 1)
            pe.wait_ge(g("qk_up"), 8)
            pe.wait_ge(g("xv_up"), NI)
            pe.wait_ge(g("gl_free"), 1)

            def scores(s):
                h, i = divmod(s, NI)
                if s >= 2:
                    pe.wait_ge(g("exp"), s - 1)
                r = CW * (h % 2)
                nc.tensor.matmul(ps[:, s % 2, :], m["qk"][r:r + CW, h // 2, i * P:(i + 1) * P], m["qk"][r:r + CW, 4 + h // 2, :],
                                 start=True, stop=True).then_inc(g("s_mm"), 1)

            def turn(s):
                pe.wait_ge(g("exp"), s + 1)
                if s >= 2:
                    pe.wait_ge(g("pt_up"), s - 1)
                for j in range(NI):
                    last = nc.tensor.transpose(ps[:, 2 + s % 2, j * P:(j + 1) * P], m["Pr"][:, s % 2, j * P:(j + 1) * P], ident[:, :])
                last.then_inc(g("tr"), 1)

            def weighted(h):
                pe.wait_ge(g("pt_up"), NI * (h + 1))
                pe.wait_ge(g("v_up"), NI)
                if h % 2 == 0 and h >= 4:
                    pe.wait_ge(g("o_up"), h // 2 - 1)
                r = CW * (h % 2)
                for j in range(NI):
                    last = nc.tensor.matmul(ps[r:r + CW, 4 + (h // 2) % 2, :], m["V"][:, j, h * CW:(h + 1) * CW], m["PT"][:, h % 2, j, :],
                                            start=(j == 0), stop=(j == NI - 1), tile_position=(0, r))
                last.then_inc(g("pv"), 1)

            def back(q):
                pe.wait_ge(g("o_up"), q + 1)
                if q >= 2:
                    pe.wait_ge(g("attn"), q - 1)
                for i in range(NI):
                    last = nc.tensor.transpose(ps[:, 6 + q % 2, i * P:(i + 1) * P], m["OT"][:, q % 2, i * P:(i + 1) * P], ident[:, :])
                last.then_inc(g("ob_mm"), 1)

            scores(0)
            scores(1)
            for s in range(CH * NI):
                if s + 2 < CH * NI:
                    scores(s + 2)
                h, i = divmod(s, NI)
                if i == 1 and h:
                    weighted(h - 1)
                if i == 3 and h and h % 2 == 0:
                    back(h // 2 - 1)
                turn(s)
            weighted(CH - 1)
            back(CH // 2 - 1)
            keep_warm(WARM_LN, bank=2)
            for i in range(NI):
                pe.wait_ge(g("ae_dve"), DVE_E)
                pe.wait_ge(g("ae_pool"), CN * CH // 2 - DVE_E)
                if i >= 2:
                    pe.wait_ge(g("aet_up"), i - 1)
                for t, rows in enumerate(KT_AE):
                    last = nc.tensor.transpose(ps[0:rows, i % 2, t * P:(t + 1) * P], m["ae"][:, i, t * P:t * P + rows], ident[:, :])
                last.then_inc(g("aet_mm"), 1)
            for i in range(NI):
                pe.wait_ge(g("aet_up"), i + 1)
                for t, rows in enumerate(KT_AE):
                    last = nc.tensor.matmul(ps[:, 4 + i, 0:DM], m["aeT"][0:rows, t, i * P:(i + 1) * P],
                                            wbuf[0:rows, slot_of["C"], C_O + t * DM:C_O + (t + 1) * DM],
                                            start=(t == 0), stop=(t == 2))
                last.then_inc(g("y_mm"), 1)

        def c_act(act, _, n, st):
            m = MC
            g = lambda s: sm["C", s]
            act.wait_ge(g("gl_free"), 1)
            nc.scalar.activation(m["sg"][:, :, :], m["gl"][:, :, :].rearrange("p (i a) e -> p i (a e)", i=NI), ACT.Exp, scale=-1.0).then_inc(g("sig"), 1)
            for i in range(NI):
                act.wait_ge(g("xv_mm"), i + 1)
                nc.scalar.activation(m["xv"][:, i, :], ps[:, 1 + i, 0:320], ACT.Copy).then_inc(g("xv_up"), 1)
            for e in range(8):
                act.wait_ge(g("qk_mm"), e + 1)
                nc.scalar.activation(m["qk"][:, e, :], ps[:, 5 + e % 3, :], ACT.Copy).then_inc(g("qk_up"), 1)

            def up(s):
                h, i = divmod(s, NI)
                act.wait_ge(g("tr"), s + 1)
                if h >= 2:
                    act.wait_ge(g("pv"), h - 1)
                nc.scalar.activation(m["PT"][:, h % 2, :, i * P:(i + 1) * P],
                                     ps[:, 2 + s % 2, :].rearrange("p (j q) -> p j q", j=NI), ACT.Copy).then_inc(g("pt_up"), 1)

            for s in range(CH * NI):
                h, i = divmod(s, NI)
                act.wait_ge(g("negm"), s + 1)
                if s >= 2:
                    act.wait_ge(g("tr"), s - 1)
                nc.scalar.activation(m["Pr"][:, s % 2, :], ps[:, s % 2, :], ACT.Exp, bias=m["nm"][:, s:s + 1], scale=CW ** -0.5,
                                     accum_out=m["den"][:, i, h:h + 1]).then_inc(g("exp"), 1)
                if s:
                    up(s - 1)
            up(CH * NI - 1)
            for i in range(NI):
                act.wait_ge(g("aet_mm"), i + 1)
                for t, rows in enumerate(KT_AE):
                    last = nc.scalar.activation(m["aeT"][0:rows, t, i * P:(i + 1) * P], ps[0:rows, i % 2, t * P:(t + 1) * P], ACT.Copy)
                last.then_inc(g("aet_up"), 1)

        POOL_MIX = 2
        DVE_E = 3

        def mix(eng, ch, i):
            m = MC
            k = 1 if eng is nc.gpsimd else 0
            shape = [P, CH, CW]
            dst = m["V"][:, i, :].rearrange("p (h k) -> p h k", h=CH)
            for e in range(CN):
                gate = spread(m["sg"][:, i, 0:CH * CN].rearrange("p (h e) -> p h e", e=CN)[:, :, e], 2, shape)
                val = spread(m["xv"][:, i, e * CW:(e + 1) * CW], 1, shape)
                o = dst if e == 0 else m["tmp"][:, k, :].rearrange("p (h k) -> p h k", h=CH)
                ch.link(eng.tensor_tensor(o, val, gate, ALU.mult))
                if e:
                    add = eng.tensor_tensor(dst, dst, o, ALU.add)
                    if e < CN - 1:
                        ch.link(add)
            add.then_inc(sm["C", "v_up"], 1)

        def add_pair(eng, ch, q, experts, done, n=0):
            m = MC
            k = 1 if eng is nc.gpsimd else 0
            t = m["tmp"][:, k, :].rearrange("p (i h k) -> p i h k", i=NI, h=2)
            for e in experts:
                pick = spread(m["msk"][:, :, :].rearrange("p (i a) e -> p i a e", i=NI)[:, :, CH + 2 * q:CH + 2 * q + 2, e], 3, [P, NI, 2, CW])
                ch.link(eng.tensor_tensor(t, m["at"][:, :, :].rearrange("p i (h k) -> p i h k", h=2), pick, ALU.mult))
                acc = m["ae"][:, :, e * CW:(e + 1) * CW]
                if q:
                    ch.link(eng.tensor_tensor(acc, acc, t[:, :, 0, :], ALU.add))
                eng.tensor_tensor(acc, acc if q else t[:, :, 0, :], t[:, :, 1, :], ALU.add).then_inc(done, 1)
                n += 1
                ch.eng.wait_ge(done, n)
            return n

        def c_pool(pool, ch, n, st):
            g = lambda s: sm["C", s]
            pool.wait_ge(g("gated"), 1)
            pool.wait_ge(g("xv_up"), NI)
            for i in range(NI - POOL_MIX, NI):
                mix(nc.gpsimd, ch, i)
            added = 0
            for q in range(CH // 2):
                pool.wait_ge(g("attn"), q + 1)
                added = add_pair(nc.gpsimd, ch, q, range(CN) if q < CH // 2 - 1 else range(DVE_E, CN), g("ae_pool"), added)

        def c_dve(dve, ch, n, st):
            m = MC
            g = lambda s: sm["C", s]
            dve.wait_ge(g("gl_mm"), 1)
            nc.vector.tensor_copy(m["gl"][:, :, :], ps[:, 0, 0:320].rearrange("p (a e) -> p a e", e=CN)).then_inc(g("gl_free"), 1)
            dve.wait_ge(g("gl_free"), 1)
            top_mask(ch, m["gl"][:, :, :], NI * 2 * CH, CN, 2, m["c1"][:, :, :, :], m["c2"][:, :, :, :], m["msk"][:, :, :])
            dve.wait_ge(g("sig"), 1)
            ch.link(nc.vector.tensor_scalar(m["sg"][:, :, :], m["sg"][:, :, :], 1.0, None, ALU.add))
            ch.link(nc.vector.reciprocal(m["sg"][:, :, :], m["sg"][:, :, :]))
            mk = m["msk"][:, :, :].rearrange("p (i a) e -> p i (a e)", i=NI)
            nc.vector.tensor_tensor(m["sg"][:, :, :], m["sg"][:, :, :], mk, ALU.mult).then_inc(g("gated"), 1)
            dve.wait_ge(g("gated"), 1)

            def maximum(s):
                dve.wait_ge(g("s_mm"), s + 1)
                ch.link(nc.vector.tensor_reduce(m["nm"][:, s:s + 1], ps[:, s % 2, :], AX.X, ALU.max))
                nc.vector.tensor_scalar(m["nm"][:, s:s + 1], m["nm"][:, s:s + 1], -(CW ** -0.5), None, ALU.mult).then_inc(g("negm"), 1)

            def pair(q):
                dve.wait_ge(g("pv"), 2 * q + 2)
                if q >= 2:
                    dve.wait_ge(g("ob_mm"), q - 1)
                nc.vector.tensor_copy(m["OT"][:, q % 2, :], ps[:, 4 + q % 2, :]).then_inc(g("o_up"), 1)
                ch.link(nc.vector.reciprocal(m["rden"][:, :, 2 * q:2 * q + 2], m["den"][:, :, 2 * q:2 * q + 2]))
                dve.wait_ge(g("ob_mm"), q + 1)
                if q:
                    dve.wait_ge(g("ae_pool"), CN * q)
                for i in range(NI):
                    last = nc.vector.tensor_tensor(m["at"][:, i, :].rearrange("p (h k) -> p h k", h=2),
                                                   ps[:, 6 + q % 2, i * P:(i + 1) * P].rearrange("p (h k) -> p h k", h=2),
                                                   spread(m["rden"][:, i, 2 * q:2 * q + 2], 2, [P, 2, CW]), ALU.mult)
                last.then_inc(g("attn"), 1)
            dve.wait_ge(g("xv_up"), NI)
            for i in range(NI - POOL_MIX):
                mix(nc.vector, ch, i)
            for s in range(CH * NI):
                h, i = divmod(s, NI)
                maximum(s)
                if i == 3 and h >= 2 and h % 2 == 0:
                    pair(h // 2 - 1)
            pair(CH // 2 - 1)
            dve.wait_ge(g("attn"), CH // 2)
            add_pair(nc.vector, ch, CH // 2 - 1, range(DVE_E), g("ae_dve"))
            for i in range(NI):
                dve.wait_ge(g("y_mm"), i + 1)
                ch.link(nc.vector.tensor_tensor(x[:, i, :], x[:, i, :], ps[:, 4 + i, 0:DM], ALU.add))

        EXTRA["C"] = dict(pe=c_pe, act=c_act, dve=c_dve, pool=c_pool, sp=lambda *a: None)

        named("F", "lg_mm", "lg_exp", "comb", "ct_mm", "ct_up", "gu_mm", "silu", "gu", "down")

        if "F" in STAGES:
            w_in = [sem(f"w_in{k}_F") for k in range(NRING)]

        def f_mem(sb2):
            m = {}
            m["w"] = sb2("f_w", [P, NRING, 3 * DM])
            m["sc"] = sb2("f_sc", [P, NI, NE])
            m["sb"] = sb2("f_sb", [P, NI, NE])
            m["mb"] = sb2("f_mb", [P, NI, NE])
            m["rp"] = sb2("f_rp", [P, NI, NE])
            m["t8"] = sb2("f_t8", [P, NI, 8])
            m["m4"] = sb2("f_m4", [P, NI * 8, 4])
            m["c1"] = sb2("f_c1", [P, NI * 128])
            m["c2"] = sb2("f_c2", [P, NI * 128])
            m["gs"] = sb2("f_gs", [P, NI, 8])
            m["gm"] = sb2("f_gm", [P, NI, 8])
            m["sum"] = sb2("f_sum", [P, NI])
            m["rest"] = sb2("f_rest", [P, NI, NE])
            m["cp"] = sb2("f_cp", [P, NI, 3, NE], BF16)
            m["cT"] = sb2("f_cT", [96, S], BF16)
            m["si"] = sb2("f_si", [P, 2, S])
            m["gu"] = sb2("f_gu", [P, 2, S])
            m["tm"] = sb2("f_tm", [P, S])
            return m

        MF = scope(f_mem)

        ahead = sem("ahead")

        def load_ahead(sp, b, signal):
            sp.dma_start(M1["x"][:, :, :], io["x"][bass.ds(b, 1), :, :].rearrange("o (t p) d -> p (o t) d", p=P)).then_inc(signal, 16)
            sp.dma_start(M1["w"][:, :, :], io["wA"].rearrange("(k p) c -> p k c", p=P)).then_inc(signal, 16)
            sp.dma_start(M1["wo"][:, :, :], io["woA"].rearrange("(k p) c -> p k c", p=P)).then_inc(signal, 16)

        def f_sp(sp, b, *_):
            for e in range(NE + NSH):
                if e >= NRING:
                    sp.wait_ge(sm["F", "down"], e - NRING + 1)
                sp.dma_start(MF["w"][:, e % NRING, :], io["wF"][e]).then_inc(w_in[e % NRING], 16)
                if e == NRING - 1:
                    load_ahead(sp, b + 1, ahead)
            sp.wait_ge(ahead, 3 * 16)

        def f_pe(pe, _, n, st):
            m = MF
            g = lambda s: sm["F", s]
            pe.wait_ge(ln_T, n + 1)
            for i in range(NI):
                for k in range(KD):
                    last = nc.tensor.matmul(ps[:, 4, i * NE:(i + 1) * NE], xnT[:, k, i * P:(i + 1) * P], gateW[:, k, :],
                                            start=(k == 0), stop=(k == KD - 1))
            last.then_inc(g("lg_mm"), 1)

            def up(e):
                pe.wait_ge(w_in[e % NRING], 16 * (e // NRING + 1))
                if e >= 2:
                    pe.wait_ge(g("gu"), e - 1)
                for v in range(2):
                    for k in range(KD):
                        last = nc.tensor.matmul(ps[:, 2 * v + e % 2, :], m["w"][:, e % NRING, (2 * v + k) * P:(2 * v + k + 1) * P],
                                                xnT[:, k, :], start=(k == 0), stop=(k == KD - 1))
                if e < NSH:
                    last.then_inc(g("gu_mm"), 1)

            def routed(e):
                if e == NSH:
                    pe.wait_ge(g("comb"), 1)
                    for i in range(NI):
                        last = nc.tensor.matmul(ps[0:96, 5, i * P:(i + 1) * P], m["cp"][:, i, :, :].rearrange("p a e -> p (a e)"),
                                                identb[:, :], start=True, stop=True)
                    last.then_inc(g("ct_mm"), 1)
                    pe.wait_ge(g("ct_up"), 1)
                nc.tensor.matmul(ps[:, 4 + e % 2, :], selE[:, e - NSH, :], m["cT"][:, :], start=True, stop=True).then_inc(g("gu_mm"), 1)

            def down(e):
                pe.wait_ge(g("gu"), e + 1)
                for i in range(NI):
                    last = nc.tensor.matmul(ps[:, 6 + i // 2, (i % 2) * DM:(i % 2 + 1) * DM], m["gu"][:, e % 2, i * P:(i + 1) * P],
                                            m["w"][:, e % NRING, 2 * DM:3 * DM], start=(e == 0 and i % 2 == 0),
                                            stop=(e == NE + NSH - 1), skip_group_check=True)
                last.then_inc(g("down"), 1)

            up(0)
            up(1)
            down(0)
            up(NSH)
            down(1)
            up(NSH + 1)
            routed(NSH)
            routed(NSH + 1)
            down(NSH)
            for e in range(NSH + 2, NE + NSH):
                up(e)
                routed(e)
                down(e - 1)
            down(NE + NSH - 1)

        def f_act(act, _, n, st):
            m = MF
            g = lambda s: sm["F", s]
            act.wait_ge(g("lg_mm"), 1)
            nc.scalar.activation(m["sc"][:, :, :], ps[:, 4, 0:NI * NE].rearrange("p (i e) -> p i e", i=NI), ACT.Exp, scale=-1.0).then_inc(g("lg_exp"), 1)
            for e in range(NE + NSH):
                if e == NSH:
                    act.wait_ge(g("ct_mm"), 1)
                    nc.scalar.activation(m["cT"][:, :], ps[0:96, 5, :], ACT.Copy).then_inc(g("ct_up"), 1)
                act.wait_ge(g("gu_mm"), e + 1)
                if e >= 2:
                    act.wait_ge(g("gu"), e - 1)
                nc.scalar.activation(m["si"][:, e % 2, :], ps[:, e % 2, :], ACT.Silu).then_inc(g("silu"), 1)

        def f_dve(dve, ch, n, st):
            m = MF
            g = lambda s: sm["F", s]

            def gate():
                dve.wait_ge(g("lg_exp"), 1)
                f2 = lambda t: m[t][:, :, :]
                ch.link(nc.vector.tensor_scalar(f2("sc"), f2("sc"), 1.0, None, ALU.add))
                ch.link(nc.vector.reciprocal(f2("sc"), f2("sc")))
                ch.link(nc.vector.tensor_tensor(f2("sb"), f2("sc"), spread(gateB[:, :], 1, [P, NI, NE]), ALU.add))
                by4 = m["sb"][:, :, :].rearrange("p i (g e) -> p (i g) e", e=4)
                c = lambda t, k: m[t][:, 0:NI * 8 * k * k if k == 4 else NI * 64].rearrange("p (a e f) -> p a e f", e=k, f=k)
                top_mask(ch, by4, NI * 8, 4, 2, c("c1", 4), c("c2", 4), m["m4"][:, :, :])
                product(0)
                ch.link(nc.vector.tensor_tensor(m["m4"][:, :, :], m["m4"][:, :, :], by4, ALU.mult))
                ch.link(nc.vector.tensor_reduce(m["gs"][:, :, :].rearrange("p i g -> p (i g)"), m["m4"][:, :, :], AX.X, ALU.add))
                top_mask(ch, m["gs"][:, :, :], NI, 8, 4, c("c1", 8), c("c2", 8), m["gm"][:, :, :])
                product(1)
                ch.link(nc.vector.tensor_tensor(m["mb"][:, :, :].rearrange("p i (g e) -> p (i g) e", e=4), by4,
                                                spread(m["gm"][:, :, :].rearrange("p i g -> p (i g)"), 2, [P, NI * 8, 4]), ALU.mult))
                for i in range(NI):
                    last = nc.vector.max(m["t8"][:, i, :], m["mb"][:, i, :])
                ch.link(last)
                for i in range(NI):
                    last = nc.vector.match_replace(m["rp"][:, i, :], m["t8"][:, i, :], m["mb"][:, i, :], -1e30)
                ch.link(last)
                ch.link(nc.vector.tensor_tensor(f2("rp"), f2("rp"), f2("mb"), ALU.is_lt))
                ch.link(nc.vector.tensor_tensor(f2("mb"), f2("rp"), f2("sc"), ALU.mult))
                ch.link(nc.vector.tensor_reduce(m["sum"][:, :], f2("mb"), AX.X, ALU.add))
                ch.link(nc.vector.tensor_scalar(m["sum"][:, :], m["sum"][:, :], 1e-20, None, ALU.add))
                ch.link(nc.vector.reciprocal(m["sum"][:, :], m["sum"][:, :]))
                ch.link(nc.vector.tensor_tensor(f2("mb"), f2("mb"), spread(m["sum"][:, :], 2, [P, NI, NE]), ALU.mult))
                ch.link(nc.vector.tensor_scalar(f2("mb"), f2("mb"), 2.5, None, ALU.mult))
                ch.link(nc.vector.tensor_copy(m["cp"][:, :, 0, :], f2("mb")))
                ch.link(nc.vector.tensor_tensor(f2("rest"), f2("mb"), m["cp"][:, :, 0, :], ALU.subtract))
                ch.link(nc.vector.tensor_copy(m["cp"][:, :, 1, :], f2("rest")))
                nc.vector.tensor_tensor(m["cp"][:, :, 2, :], f2("rest"), m["cp"][:, :, 1, :], ALU.subtract).then_inc(g("comb"), 1)

            def product(e):
                dve.wait_ge(g("silu"), e + 1)
                if e >= 2:
                    dve.wait_ge(g("down"), e - 1)
                if e < NSH:
                    nc.vector.tensor_tensor(m["gu"][:, e % 2, :], m["si"][:, e % 2, :], ps[:, 2 + e % 2, :], ALU.mult).then_inc(g("gu"), 1)
                else:
                    ch.link(nc.vector.tensor_tensor(m["tm"][:, :], m["si"][:, e % 2, :], ps[:, 2 + e % 2, :], ALU.mult))
                    nc.vector.tensor_tensor(m["gu"][:, e % 2, :], m["tm"][:, :], ps[:, 4 + e % 2, :], ALU.mult).then_inc(g("gu"), 1)
                    dve.wait_ge(g("gu"), e + 1)

            gate()
            for e in range(NSH, NE + NSH):
                product(e)
            dve.wait_ge(g("down"), NE + NSH)
            for i in range(NI):
                ch.link(nc.vector.tensor_tensor(x[:, i, :], x[:, i, :], ps[:, 6 + i // 2, (i % 2) * DM:(i % 2 + 1) * DM], ALU.add))

        EXTRA["F"] = dict(pe=f_pe, act=f_act, dve=f_dve, pool=lambda *a: None, sp=f_sp)

        AH, AW = 16, 64
        SA_R = [4, 2, 1, 1]
        CH_R = [4, 4, 4, 4]
        CHUNKS = [(i, r) for i in range(NI) for r in range(0, 16, CH_R[i])]
        NCHUNK = len(CHUNKS)
        CH_MAX = max(CH_R[i] * (i + 1) * P for i in range(NI))
        HB = [0, 1, 6]
        BACK = 399
        sk = [nc.dram_tensor(f"scores_kerple{i}", (2 * AH, P, (i + 1) * P), F32, kind="Internal").ap() for i in range(NI)]
        named("A", "rot", "qk_mm", "qk_up", "e_mm", "e_up", "out0", "out1", "out2", "out3", "cmb0", "cmb1", "fin0", "fin1", "fin2", "fin3",
              "w1", "gelu", "w2", "mixed", "negm", "exp", "prob", "tr", "pt_up", "pv", "ot_up", "y_mm", "y_up")
        KT_A = AH * AW // P
        AC = 3 * AH * AW

        TRI_L = [(i + 1) * P for i in range(NI)]

        def a1_mem(sb2):
            m = dict(both)
            m["qk"] = sb2("a_qk", [P, 16, S])
            m["rot"] = sb2("a_rot", [P, 2, S])
            m["w"] = sb2("a_w", [P, KD, AC])
            m["x"] = sb2("a_x", [P, NI, DM])
            sb2("a_apart", [P, CH_MAX * 3 // 2])
            m["Ss"] = sb2("a_Ss", [P, 4 * sum(TRI_L)])
            return m

        def a2_mem(sb2):
            m = dict(both)
            m["PT"] = sb2("a_PT", [P, NI, 16, P])
            m["cmb"] = sb2("a_cmb", [P, 2, 2, CH_MAX])
            m["fin"] = sb2("a_fin", [P, 4, CH_MAX])
            hid2 = sb2("a_hid", [P, BANK])
            m["hid"] = [xn[:, 0:2, :].rearrange("p a c -> p (a c)"), xn[:, 2:4, :].rearrange("p a c -> p (a c)"), hid2[:, :]]
            m["OT"] = spare[:, KT_A * DM:KT_A * (DM + P)].rearrange("p (t c) -> p t c", t=KT_A)
            m["nm"] = sb2("a_nm", [P, 4, 16])
            m["den"] = sb2("a_den", [P, 4, 16])
            return m

        def a_mem(sb2):
            both.update(V=sb2("a_V", [P, NI, AH * AW]), wo=spare[:, 0:KT_A * DM].rearrange("p (t c) -> p t c", t=KT_A))
            return scope(a1_mem), scope(a2_mem)

        spare = wbuf[:, 1, :]
        both = {}
        M1, M2 = scope(a_mem)

        def chunk(n):
            i, r = CHUNKS[n]
            return i, r, CH_R[i], (i + 1) * P

        A_UNITS = [(n, f, q) for n, (i, _) in enumerate(CHUNKS) for q in range(0, CH_R[i], SA_R[i]) for f in range(2)]
        A_TURNS = [[(q, j) for q in range(0, CH_R[i], 4) for j in range(i + 1)] for i, _ in CHUNKS]
        UNITS_TO = [sum(u[0] < n for u in A_UNITS) for n in range(NCHUNK + 1)]
        TURNS_TO = [sum(len(t) for t in A_TURNS[:n]) for n in range(NCHUNK + 1)]
        ROWS_TO = [sum(CH_R[i] for i, _ in CHUNKS[:n]) for n in range(NCHUNK + 1)]
        TILE_END = [max(n for n in range(NCHUNK) if CHUNKS[n][0] == i) for i in range(NI)]

        kt_ready = ctx.enter_context(nc.semaphore("kt_ready"))
        kt_act = ctx.enter_context(nc.semaphore("kt_act"))
        kt_dve = ctx.enter_context(nc.semaphore("kt_dve"))
        kt_out = ctx.enter_context(nc.semaphore("kt_out"))
        first_loaded = ctx.enter_context(nc.semaphore("first_loaded"))

        def a_sp(sp, _, n, st):
            g = lambda s: sm["A", s]

            def load(c):
                i, r, R, L = chunk(c)
                rows = sk[i].rearrange("r (f g q) j -> g r f (q j)", f=2, g=4)
                part = slice(r * L, (r + R) * L)
                for u in range(4):
                    sp.dma_start(M2["cmb"][32 * u:32 * u + 32, c % 2, 
                                 :, 0:R * L], rows[u, :, :, part]).then_inc(g(f"cmb{c % 2}"), 16)
                if c >= 4:
                    sp.wait_ge(g("tr"), TURNS_TO[c - 3])
                rows = sk[i][0:AH].rearrange("h (g q) j -> g h (q j)", g=8)
                sp.dma_start(M2["fin"][:, c % 4, 0:R * L], rows[:, :, part]).then_inc(g(f"fin{c % 4}"), 16)

            for grp in range(16):
                hq, i = divmod(grp, NI)
                L = (i + 1) * P
                if grp == 15:
                    sp.wait_ge(g("out0"), 4 * 16)
                    sp.wait_ge(kt_out, 16 * 16 * NI)
                    load(0)
                sp.wait_ge(g("e_up"), 8 + 4 * (grp + 1))
                sp.dma_start(sk[i][4 * hq:4 * hq + 4].rearrange("h p j -> p h j"),
                             M1["Ss"][:, 4 * sum(TRI_L[:i]):4 * sum(TRI_L[:i + 1])].rearrange("p (h l) -> p h l", h=4)).then_inc(g(f"out{i}"), 16)
            for c in range(1, NCHUNK):
                if CHUNKS[c][1] == 0:
                    sp.wait_ge(g(f"out{CHUNKS[c][0]}"), 4 * 16)
                if c >= 2:
                    sp.wait_ge(g("w1"), UNITS_TO[c - 1])
                load(c)
                if c == 1:
                    st.end()

        def a_pe(pe, _, n, st):
            g = lambda s: sm["A", s]
            m = M1
            pe.wait_ge(ln_T, n + 1)
            HW = AH * AW
            for e in range(16):
                if e >= 4:
                    pe.wait_ge(g("qk_up"), e - 3)
                t, kind = divmod(e, 2)
                col = kind * HW + t * P
                for k in range(KD):
                    last = nc.tensor.matmul(ps[:, e % 4, :], m["w"][:, k, col:col + P], xnT[:, k, :],
                                            start=(k == 0), stop=(k == KD - 1))
                last.then_inc(g("qk_mm"), 1)
            for e in range(8):
                i, f = divmod(e, 2)
                if e >= 4:
                    pe.wait_ge(g("e_up"), e - 3)
                for k in range(KD):
                    last = nc.tensor.matmul(ps[:, 4 + e % 4, :], xnT[:, k, i * P:(i + 1) * P],
                                            m["w"][:, k, 2 * HW + f * BANK:2 * HW + (f + 1) * BANK], start=(k == 0), stop=(k == KD - 1))
                last.then_inc(g("e_mm"), 1)
            for s in range(64):
                e = 8 + s
                grp, hh = divmod(s, 4)
                hq, i = divmod(grp, NI)
                h = 4 * hq + hh
                pe.wait_ge(g("e_up"), e - 3)
                if i == 0:
                    pe.wait_ge(g("qk_up"), 2 * (h // 2 + 1))
                r = AW * (h % 2)
                nc.tensor.matmul(ps[:, 4 + e % 4, 0:(i + 1) * P], m["qk"][r:r + AW, 2 * (h // 2), i * P:(i + 1) * P],
                                 m["qk"][r:r + AW, 2 * (h // 2) + 1, 0:(i + 1) * P], start=True, stop=True).then_inc(g("e_mm"), 1)
            st.end()
            m = M2

            def up(k):
                c, f, q = A_UNITS[k]
                i, _, _, L = chunk(c)
                if k == UNITS_TO[c]:
                    pe.wait_ge(g(f"cmb{c % 2}"), 16 * 4 * (c // 2 + 1))
                if k >= 3:
                    pe.wait_ge(g("gelu"), k - 2)
                R = SA_R[i]
                nc.tensor.matmul(ps[:, HB[k % 3], 0:R * L], w1A[:, :], m["cmb"][:, c % 2, f, q * L:(q + R) * L],
                                 start=True, stop=True).then_inc(g("w1"), 1)

            def down(k):
                c, f, q = A_UNITS[k]
                i, _, _, L = chunk(c)
                w = k // 2
                pe.wait_ge(g("gelu"), k + 1)
                if w >= 2:
                    pe.wait_ge(g("mixed"), w - 1)
                nc.tensor.matmul(ps[64 * f:64 * f + 64, 2 + w % 2, 0:SA_R[i] * L], w2A[:, :], m["hid"][k % 3][:, 0:SA_R[i] * L],
                                 start=True, stop=True, tile_position=(0, 64 * f)).then_inc(g("w2"), 1)

            def turn(c, k):
                t = TURNS_TO[c] + k
                i, r, _, L = chunk(c)
                q0, j = A_TURNS[c][k]
                if k == 0:
                    pe.wait_ge(g("prob"), c + 1)
                if t >= 2:
                    pe.wait_ge(g("pt_up"), t - 1)
                if k == 0 and i and r == 0:
                    pe.wait_ge(g("ot_up"), i)
                for q in range(4):
                    last = nc.tensor.transpose(ps[:, 4 + t % 2, q * P:(q + 1) * P],
                                               m["fin"][:, c % 4, (q0 + q) * L + j * P:(q0 + q) * L + (j + 1) * P], ident[:, :])
                last.then_inc(g("tr"), 1)

            def weighted(i):
                pe.wait_ge(g("pt_up"), TURNS_TO[TILE_END[i] + 1])
                for h in range(AH):
                    r, t = AW * (h % 2), h // 2
                    for j in range(i + 1):
                        rhs = m["PT"][:, j, :, :].rearrange("p q (g h) -> p h g q", h=AH)[:, h]
                        o = ps[r:r + AW, 4 + t // 4, (t % 4) * P:(t % 4 + 1) * P].rearrange("p (g q) -> p g q", g=8)
                        last = nc.tensor.matmul(o, m["V"][:, j, h * AW:(h + 1) * AW], rhs, start=(j == 0), stop=(j == i), tile_position=(0, r))
                last.then_inc(g("pv"), 1)

            def project(i):
                pe.wait_ge(g("ot_up"), i + 1)
                if i:
                    pe.wait_ge(g("y_up"), i)
                for t in range(KT_A):
                    last = nc.tensor.matmul(ps[:, 7, 0:DM], m["OT"][:, t, :], m["wo"][:, t, :], start=(t == 0), stop=(t == KT_A - 1))
                last.then_inc(g("y_mm"), 1)

            keep_warm(WARM_STACK)
            up(0)
            up(1)
            for s in range(NCHUNK + 3):
                c = s - 2
                if s < NCHUNK:
                    for k in range(UNITS_TO[s], UNITS_TO[s + 1]):
                        if k + 2 < len(A_UNITS):
                            up(k + 2)
                        down(k)
                if 0 <= c < NCHUNK:
                    turn(c, 0)
                if s - 3 in TILE_END:
                    project(TILE_END.index(s - 3))
                if 0 <= c < NCHUNK:
                    for k in range(1, len(A_TURNS[c])):
                        turn(c, k)
                if c in TILE_END:
                    weighted(TILE_END.index(c))

        def a_act(act, _, n, st):
            g = lambda s: sm["A", s]
            m = M1
            for e in range(16):
                act.wait_ge(g("qk_mm"), e + 1)
                if e >= 2:
                    act.wait_ge(g("qk_up"), e - 1)
                for r in range(0, P, 32):
                    r2 = r ^ 32
                    last = nc.scalar.activation(m["rot"][r:r + 32, e % 2, :], ps[r2:r2 + 32, e % 4, :], ACT.Copy)
                last.then_inc(g("rot"), 1)
            for e in range(8):
                i, f = divmod(e, 2)
                act.wait_ge(g("e_mm"), e + 1)
                nc.scalar.activation(m["V"][:, i, f * BANK:(f + 1) * BANK], ps[:, 4 + e % 4, :], ACT.Copy).then_inc(g("e_up"), 1)
            for s in range(64):
                grp, hh = divmod(s, 4)
                i = grp % NI
                e = 8 + s
                act.wait_ge(g("e_mm"), e + 1)
                if grp >= 4 and hh == 0:
                    act.wait_ge(g(f"out{i}"), 16 * (grp // 4))
                s0 = 4 * sum(TRI_L[:i]) + hh * TRI_L[i]
                nc.scalar.activation(m["Ss"][:, s0:s0 + TRI_L[i]], ps[:, 4 + e % 4, 0:(i + 1) * P], ACT.Copy,
                                     scale=AW ** -0.5).then_inc(g("e_up"), 1)
            st.end()
            m = M2
            for s in range(NCHUNK + 1):
                if s < NCHUNK:
                    for k in range(UNITS_TO[s], UNITS_TO[s + 1]):
                        i, _, _, L = chunk(s)
                        w = SA_R[i] * L
                        act.wait_ge(g("w1"), k + 1)
                        if k >= 3:
                            act.wait_ge(g("w2"), k - 2)
                        nc.scalar.activation(m["hid"][k % 3][:, 0:w], ps[:, HB[k % 3], 0:w], ACT.Gelu, bias=b1A[:, 0:1]).then_inc(g("gelu"), 1)
                if s:
                    c = s - 1
                    _, _, R, L = chunk(c)
                    act.wait_ge(g("negm"), c + 1)
                    for q in range(R):
                        row = m["fin"][:, c % 4, q * L:(q + 1) * L]
                        nc.scalar.activation(row, row, ACT.Exp, bias=m["nm"][:, c % 4, q:q + 1],
                                             accum_out=m["den"][:, c % 4, q:q + 1]).then_inc(g("exp"), 1)

        def a_dve(dve, ch, n, st):
            g = lambda s: sm["A", s]
            m = M1
            for e in range(16):
                rot = m["rot"][:, e % 2, :]
                dve.wait_ge(g("rot"), e + 1)
                ch.link(nc.vector.tensor_tensor(rot, rot, sinA[:, :], ALU.mult))
                ch.link(nc.vector.tensor_tensor(m["qk"][:, e, :], ps[:, e % 4, :], cosA[:, :], ALU.mult))
                nc.vector.tensor_tensor(m["qk"][:, e, :], m["qk"][:, e, :], rot, ALU.add).then_inc(g("qk_up"), 1)
                dve.wait_ge(g("qk_up"), e + 1)
            st.end()
            m = M2

            def turned(c, first, end=None):
                r = chunk(c)[1]
                for k in range(len(A_TURNS[c]))[first:end]:
                    t = TURNS_TO[c] + k
                    q, j = A_TURNS[c][k]
                    dve.wait_ge(g("tr"), t + 1)
                    nc.vector.tensor_copy(m["PT"][:, j, r + q:r + q + 4, :],
                                          ps[:, 4 + t % 2, :].rearrange("p (q c) -> p q c", q=4)).then_inc(g("pt_up"), 1)

            for s in range(NCHUNK + 3):
                if s < NCHUNK:
                    i, r, CR, L = chunk(s)
                    R = SA_R[i]
                    slot = s % 4
                    dve.wait_ge(g(f"fin{slot}"), 16 * (s // 4 + 1))
                    groups = range(UNITS_TO[s] // 2, UNITS_TO[s + 1] // 2)
                    for w in groups:
                        if w == groups[-1] and s >= 2:
                            turned(s - 2, 0, 1)
                        q0 = A_UNITS[2 * w][2]
                        dve.wait_ge(g("w2"), 2 * w + 2)
                        rows = m["fin"][:, slot, q0 * L:(q0 + R) * L]
                        nc.vector.tensor_tensor(rows, rows, ps[:, 2 + w % 2, 0:R * L], ALU.add).then_inc(g("mixed"), 1)
                        dve.wait_ge(g("mixed"), w + 1)
                        for q in range(q0, q0 + R):
                            row = m["fin"][:, slot, q * L:(q + 1) * L]
                            t0 = BACK - i * P - (r + q)
                            last = nc.vector.tensor_tensor(row, row, biasA[:, t0:t0 + L], ALU.add)
                        ch.link(last)
                    if s >= 2:
                        turned(s - 2, 1)
                    nm = m["nm"][:, slot, 0:CR]
                    ch.link(nc.vector.tensor_reduce(nm, m["fin"][:, slot, 0:CR * L].rearrange("p (q l) -> p q l", q=CR), AX.X, ALU.max))
                    nc.vector.tensor_scalar(nm, nm, -1.0, None, ALU.mult).then_inc(g("negm"), 1)
                if NCHUNK <= s < NCHUNK + 2:
                    turned(s - 2, 0)
                if 1 <= s <= NCHUNK:
                    c = s - 1
                    slot = c % 4
                    _, _, CR, L = chunk(c)
                    dve.wait_ge(g("exp"), ROWS_TO[c + 1])
                    ch.link(nc.vector.reciprocal(m["den"][:, slot, 0:CR], m["den"][:, slot, 0:CR]))
                    for q in range(CR):
                        row = m["fin"][:, slot, q * L:(q + 1) * L]
                        last = nc.vector.tensor_scalar(row, row, m["den"][:, slot, q:q + 1], None, ALU.mult)
                    last.then_inc(g("prob"), 1)
                if s - 2 in TILE_END:
                    i = TILE_END.index(s - 2)
                    dve.wait_ge(g("pv"), i + 1)
                    if i:
                        dve.wait_ge(g("y_mm"), i)
                    for f in range(2):
                        last = nc.vector.tensor_copy(m["OT"][:, 4 * f:4 * f + 4, :], ps[:, 4 + f, :].rearrange("p (t q) -> p t q", t=4))
                    last.then_inc(g("ot_up"), 1)
                if s - 3 in TILE_END:
                    i = TILE_END.index(s - 3)
                    dve.wait_ge(g("y_mm"), i + 1)
                    nc.vector.tensor_tensor(x[:, i, :], x[:, i, :], ps[:, 7, 0:DM], ALU.add).then_inc(g("y_up"), 1)

            dve.wait_ge(g("y_up"), NI)

        EXTRA["A"] = dict(pe=a_pe, act=a_act, dve=a_dve, pool=lambda pool, ch, n, st: st.end(), sp=a_sp)

        def ker_mem(sb2):
            m = dict(above=sb2("k_above", [P, 20500]))
            for t in ("lp", "la", "b2", "e", "r"):
                m[t] = sb2("k_" + t, [P, 2])
            m["dist"] = sb2("k_dist", [P, NWIN])
            m["ahead"] = sb2("k_ahead", [P, NWIN])
            m["kt"] = sb2("k_kt", [P, NWIN])
            return m

        MK = scope(ker_mem)
        N_SETUP = 21

        def more_sp(sp):
            sp.dma_start(gateW[:, :, :], io["gateW"].rearrange("(k p) e -> p k e", p=P)).then_inc(setup_loaded, 16)
            sp.dma_start(gateB[:, :], io["gateB"].partition_broadcast(P)).then_inc(setup_loaded, 16)
            for t, n in ((w1A, "w1A"), (w2A, "w2A"), (b1A, "b1A"), (cosA, "cosA"), (sinA, "sinA"), (MK["lp"][:, 0:1], "lp"),
                         (MK["lp"][:, 1:2], "la"), (MK["b2"][:, 0:1], "b2"), (MK["dist"], "dist"), (MK["ahead"], "ahead")):
                sp.dma_start(t if len(n) == 2 else t[:, :], io[n]).then_inc(setup_loaded, 16)

        def kerple_out(sp):
            sp.wait_ge(kt_ready, 1)
            for i in range(NI):
                L = (i + 1) * P
                rows = sk[i][AH:2 * AH].rearrange("h (g q) j -> g h q j", g=8)
                for q in range(16):
                    t0 = BACK - i * P - q
                    sp.dma_start(rows[:, :, q, :], MK["kt"][:, t0:t0 + L]).then_inc(kt_out, 16)

        def more_dve(dve):
            m = MK
            n = [0]

            def link(ins):
                n[0] += 1
                ins.then_inc(kt_dve, 1)
                dve.wait_ge(kt_dve, n[0])

            link(nc.vector.tensor_scalar(m["e"][:, :], m["lp"][:, :], -1.0, None, ALU.mult))
            link(nc.vector.tensor_tensor(m["e"][:, :], m["e"][:, :], m["lp"][:, :], ALU.min))
            dve.wait_ge(kt_act, 2)
            link(nc.vector.tensor_scalar(m["r"][:, :], m["lp"][:, :], 0.0, None, ALU.max))
            link(nc.vector.tensor_tensor(m["r"][:, :], m["r"][:, :], m["la"][:, :], ALU.add))
            link(nc.vector.tensor_scalar(m["e"][:, 0:1], m["r"][:, 0:1], -1.0, None, ALU.mult))
            dve.wait_ge(kt_act, 3)
            nc.vector.tensor_scalar(m["kt"][:, :], m["kt"][:, :], m["e"][:, 0:1], None, ALU.mult).then_inc(kt_ready, 1)
            dve.wait_ge(kt_ready, 1)
            nc.vector.scalar_tensor_tensor(out=biasA[:, :], in0=m["kt"][:, :], scalar=m["b2"][:, 0:1], in1=m["ahead"][:, :],
                                           op0=ALU.add, op1=ALU.add)

        def more_act(act):
            m = MK
            act.wait_ge(kt_dve, 2)
            nc.scalar.activation(m["la"][:, :], m["e"][:, :], ACT.Exp).then_inc(kt_act, 1)
            act.wait_ge(kt_act, 1)
            nc.scalar.activation(m["la"][:, :], m["la"][:, :], ACT.Ln, bias=1.0).then_inc(kt_act, 1)
            act.wait_ge(kt_dve, 4)
            nc.scalar.activation(m["kt"][:, :], m["dist"][:, :], ACT.Ln, bias=1.0, scale=m["r"][:, 1:2]).then_inc(kt_act, 1)

        def more_pool(pool):
            nc.gpsimd.memset(tri[:, :, :], 1.0).then_inc(setup_pool_sem, 1)
            nc.gpsimd.memset(selE[:, :, :], 0.0).then_inc(setup_pool_sem, 1)
            pool.wait_ge(setup_pool_sem, 10)
            nc.gpsimd.affine_select(out=tri[:, :, :], in_=tri[:, :, :], compare_op=ALU.is_ge, fill=0.0,
                                    base=-1, pattern=[[1, 8], [-1, 8]], channel_multiplier=0).then_inc(setup_pool_sem, 1)
            for a in range(3):
                nc.gpsimd.affine_select(out=selE[:, :, :], in_=selE[:, :, :], compare_op=ALU.not_equal, fill=1.0,
                                        base=-NE * a, pattern=[[-1, NE], [0, P]], channel_multiplier=1).then_inc(setup_pool_sem, 1)
                pool.wait_ge(setup_pool_sem, 12 + a)

        SETUP_MORE.update(sp=more_sp, pool=more_pool, dve=more_dve, act=more_act)

        def setup_mem(sb2):
            return dict(mi=sb2("mi", [P, NI, CTX], I32), mt=sb2("mt", [P, CTX // P, S], I32), dg=sb2("dg", [P, S]),
                        ones=sb2("ones", [P, P]), cf=sb2("cf", [P, 2, P]), mm=sb2("mm", [P, NI]))

        SU = scope(setup_mem)

        def setup_sp(sp):
            sp.dma_start(SU["mi"][:, :, :], io["mask"].rearrange("(i p) j -> p i j", p=P)).then_inc(setup_loaded, 16)
            sp.dma_start(SU["mt"][:, :, :], io["maskT"].rearrange("(j p) i -> p j i", p=P)).then_inc(setup_loaded, 16)
            for t, n in ((cosD, "cosD"), (sinD, "sinD"), (bqE, "bqE"), (bkE, "bkE")):
                sp.dma_start(t[:, :], io[n]).then_inc(setup_loaded, 16)
            for t, n in ((boB, "boB"), (bvE, "bvE"), (boE, "boE")):
                sp.dma_start(t[:, :], io[n].partition_broadcast(P)).then_inc(setup_loaded, 16)
            SETUP_MORE["sp"](sp)

        def setup_pool(pool):
            nc.gpsimd.memset(half[:, :], -0.5)
            for t in (ident, selden, SU["cf"][:, 0, :], SU["cf"][:, 1, :]):
                nc.gpsimd.memset(t[:, :] if t is ident or t is selden else t, 0.0).then_inc(setup_pool_sem, 1)
            pool.wait_ge(setup_pool_sem, 4)
            nc.gpsimd.affine_select(out=ident[:, :], in_=ident[:, :], compare_op=ALU.not_equal, fill=1.0,
                                    base=0, pattern=[[-1, P]], channel_multiplier=1).then_inc(setup_pool_sem, 1)
            sv = selden[:, :].rearrange("p (a b) -> p a b", a=4)
            nc.gpsimd.affine_select(out=sv, in_=sv, compare_op=ALU.not_equal, fill=1.0,
                                    base=-HD, pattern=[[-32, 4], [0, 32]], channel_multiplier=1).then_inc(setup_pool_sem, 1)
            nc.gpsimd.affine_select(out=SU["cf"][:, 0, :], in_=SU["cf"][:, 0, :], compare_op=ALU.is_ge, fill=NEG,
                                    base=0, pattern=[[-1, P]], channel_multiplier=1).then_inc(setup_pool_sem, 1)
            nc.gpsimd.affine_select(out=SU["cf"][:, 1, :], in_=SU["cf"][:, 1, :], compare_op=ALU.is_ge, fill=NEG,
                                    base=0, pattern=[[1, P]], channel_multiplier=-1).then_inc(setup_pool_sem, 1)
            SETUP_MORE["pool"](pool)

        def setup_vector(dve):
            nc.vector.memset(ones[:, :], 1.0)
            nc.vector.memset(SU["ones"][:, :], 1.0)
            dve.wait_ge(setup_pool_sem, 8)
            nc.vector.tensor_copy(identb[:, :], ident[:, :])
            nc.vector.tensor_copy(caus[:, :], SU["cf"][:, 0, :])
            nc.vector.tensor_copy(causT[:, :], SU["cf"][:, 1, :])
            dve.wait_ge(setup_loaded, N_SETUP * 16)
            nc.vector.tensor_scalar(mneg[:, :, :], SU["mi"][:, :, :], 0.0, MASKED, ALU.is_equal, ALU.mult).then_inc(setup_dve, 1)
            nc.vector.tensor_scalar(mnegT[:, :, :], SU["mt"][:, :, :], 0.0, MASKED, ALU.is_equal, ALU.mult).then_inc(setup_dve, 1)
            dve.wait_ge(setup_dve, 2)
            nc.vector.tensor_reduce(SU["mm"][:, :], mneg[:, :, :], AX.X, ALU.max).then_inc(setup_dve, 1)
            dve.wait_ge(setup_dve, 3)
            nc.vector.tensor_scalar(livec[:, :], SU["mm"][:, :], -1.0, None, ALU.is_ge).then_inc(setup_dve, 1)
            dve.wait_ge(setup_dve, 4)
            for i in range(NI):
                nc.vector.tensor_scalar(SU["dg"][:, i * P:(i + 1) * P], ident[:, :], livec[:, i:i + 1], None, ALU.mult).then_inc(setup_dve, 1)
                nc.vector.tensor_scalar(mneg[:, i, :], mneg[:, i, :], livec[:, i:i + 1], None, ALU.mult)
            dve.wait_ge(setup_act, 1)
            for j in range(CTX // P):
                nc.vector.tensor_tensor(mnegT[:, j, :], mnegT[:, j, :], live[:, :], ALU.mult)
            SETUP_MORE["dve"](dve)

        def setup_pe(pe):
            pe.wait_ge(setup_dve, 4 + NI)
            nc.tensor.matmul(ps[:, 0, :], SU["ones"][:, :], SU["dg"][:, :], start=True, stop=True).then_inc(setup_pe_sem, 1)

        def setup_scalar(act):
            act.wait_ge(setup_pe_sem, 1)
            nc.scalar.activation(live[:, :], ps[:, 0, :], ACT.Copy).then_inc(setup_act, 1)
            SETUP_MORE["act"](act)

        block = ctx.enter_context(nc.Block())
        SETUP_PHASES = 3

        def load_weights(sp, s):
            sp.dma_start(W(s, 0, WIDTH[s]), io["w" + s]).then_inc(w_loaded[s], 16)

        @block.sync
        def _(sp):
            st = Steps(sp, bars, True)
            setup_sp(sp)
            load_ahead(sp, 0, first_loaded)
            sp.wait_ge(first_loaded, 3 * 16)
            for _ in range(SETUP_PHASES):
                st.end()
            if "A" in STAGES:
                kerple_out(sp)
            with sp.Fori(0, rounds) as b:
                if ORDER:
                    load_weights(sp, ORDER[0])
                sp.dma_start(ctxT[:, :, :], io["ctxT"][bass.ds(b, 1), :, :].rearrange("o (k p) j -> p (o k) j", p=P)).then_inc(ctx_loaded, 16)
                for n, s in enumerate(STAGES):
                    if s in ORDER and ORDER.index(s) + 1 < len(ORDER):
                        load_weights(sp, ORDER[ORDER.index(s) + 1])
                    if s in CFG:
                        a16_sp(sp, CFG[s])
                    else:
                        EXTRA[s]["sp"](sp, b, n, st)
                    st.end()
                    if s == "B":
                        for (stage, _), sem_b in sm.items():
                            if stage == "B":
                                sp.sem_clear(sem_b)
                sp.dma_start(out[bass.ds(b, 1), :, :].rearrange("o (t p) d -> p (o t) d", p=P), x[:, :, :]).then_inc(x_stored, 16)
                sp.wait_ge(x_stored, 16)
                st.end_round(counting)

        @block.gpsimd
        def _(pool):
            st = Steps(pool, bars, False)
            setup_pool(pool)
            for _ in range(SETUP_PHASES):
                st.end()
            with pool.Fori(0, rounds) as b:
                ch = Chain(pool, pool_chain)
                for n, s in enumerate(STAGES):
                    ln_pool(pool, n)
                    if s in CFG:
                        a16_pool(pool, ch, CFG[s])
                    else:
                        EXTRA[s]["pool"](pool, ch, n, st)
                    st.end()
                st.end_round()

        @block.scalar
        def _(act):
            st = Steps(act, bars, False)
            setup_scalar(act)
            for _ in range(SETUP_PHASES):
                st.end()
            with act.Fori(0, rounds) as b:
                for n, s in enumerate(STAGES):
                    if s in CFG:
                        a16_act(act, CFG[s], n)
                    else:
                        ln_act(act, n)
                        EXTRA[s]["act"](act, None, n, st)
                    st.end()
                st.end_round()

        @block.vector
        def _(dve):
            st = Steps(dve, bars, False)
            setup_vector(dve)
            for _ in range(SETUP_PHASES):
                st.end()
            with dve.Fori(0, rounds) as b:
                ch = Chain(dve, dve_chain)
                ch.link(nc.vector.tensor_copy(x[:, :, :], M1["x"][:, :, :]))
                for n, s in enumerate(STAGES):
                    ln_dve(dve, ch, n)
                    if s in CFG:
                        a16_dve(dve, ch, CFG[s])
                    else:
                        EXTRA[s]["dve"](dve, ch, n, st)
                    st.end()
                st.end_round()

        @block.tensor
        def _(pe):
            st = Steps(pe, bars, False)
            setup_pe(pe)
            for _ in range(SETUP_PHASES):
                st.end()
            with pe.Fori(0, rounds) as b:
                for n, s in enumerate(STAGES):
                    if s in CFG:
                        a16_pe(pe, CFG[s], n)
                    else:
                        keep_warm(WARM_LN)
                        ln_pe(pe, n)
                        keep_warm(WARM_T)
                        EXTRA[s]["pe"](pe, None, n, st)
                    st.end()
                st.end_round()


def lay_out_more(d, a, ktiles):
    import numpy as np

    wo = a["L0_ffn_Wo"].reshape(320, DM)
    wop = np.zeros((3 * P, DM), wo.dtype)
    wop[:320] = wo
    d["wC"] = np.concatenate([ktiles(w) for w in (a["L0_ffn_Wq"], a["L0_ffn_Wk"],
                                                  np.concatenate([a["L0_ffn_Ws"], a["L0_ffn_Wd"]], 1),
                                                  a["L0_ffn_Wv"].transpose(1, 0, 2).reshape(DM, 320), wop)], 1)
    gate = np.concatenate([a["L1_ffn_sh_gate"].reshape(2, P, DM), a["L1_ffn_w_gate"]])
    up = np.concatenate([a["L1_ffn_sh_up"].reshape(2, P, DM), a["L1_ffn_w_up"]])
    down = np.concatenate([a["L1_ffn_sh_down"].reshape(DM, 2, P).transpose(1, 0, 2), a["L1_ffn_w_down"]])

    def feature_rows(w):
        return w.transpose(0, 2, 1).reshape(-1, KD, P, P).transpose(0, 2, 1, 3).reshape(-1, P, DM)

    d["wF"] = np.concatenate([feature_rows(gate), feature_rows(up), down.transpose(0, 2, 1)], 2)
    d["gateW"] = a["L1_ffn_gate_w"].T
    d["gateB"] = a["L1_ffn_gate_bias"]

    d["wA"] = a["L0_attn_w_qkv"]
    d["woA"] = a["L0_attn_w_o"]
    w1, w2 = np.zeros((4, 32, 4, 32), np.float32), np.zeros((4, 32, 4, 16), np.float32)
    for g in range(4):
        w1[g, :, g], w2[g, :, g] = a["L0_attn_w1"], a["L0_attn_w2"]
    d["w1A"], d["w2A"] = w1.reshape(P, P), w2.reshape(P, 64)
    d["b1A"] = np.tile(a["L0_attn_b1"], 4).reshape(P, 1)
    d["lp"], d["la"], d["b2"] = (np.tile(a["L0_attn_" + n].reshape(-1), 8).reshape(P, 1) for n in ("log_p", "log_a", "b2"))
    d["cosA"], d["sinA"] = rope_half_tables()
    off = 399 + 16 * (np.arange(P)[:, None] // 16) - np.arange(528)[None, :]
    d["dist"] = np.abs(off).astype(np.float32)
    d["ahead"] = np.where(off < 0, np.float32(NEG), np.float32(0))


def lay_out(i):
    import numpy as np

    def ktiles(w):
        k = w.shape[0] // P
        return w.reshape(k, P, w.shape[1]).transpose(1, 0, 2).reshape(P, -1)

    def padded_out(w):
        q = np.zeros((NH, 32, w.shape[1]), w.dtype)
        q[:, :HD, :] = w.reshape(NH, HD, -1)
        return ktiles(q.reshape(NH * 32, -1))

    a = {k: np.asarray(v) for k, v in i.items()}
    swap = np.arange(DM) ^ 1
    d = {}
    d["x"] = np.concatenate([a["x"], a["x"][:1]])
    d["ctxT"] = a["ctx_1024"].transpose(0, 2, 1)
    mask = a["mask_1x1xSxS2_ik0"][0, 0]
    d["mask"], d["maskT"] = mask, mask.T
    d["cosD"], d["sinD"] = rope_pair_tables()
    d["wB"] = np.concatenate([ktiles(a["L0_xattn_" + n].T) for n in ("Wq", "Wk", "Wv")] + [padded_out(a["L0_xattn_Wo"].T)], 1)
    d["boB"] = a["L0_xattn_bo"]
    wd = a["L1_attn_W_qkv"]
    q, k, v = wd[:DM], wd[DM:2 * DM], wd[2 * DM:]
    d["wD"] = np.concatenate([ktiles(w.T) for w in (q, q[swap], k, k[swap], v)] + [padded_out(a["L1_attn_W_o"].T)], 1)
    d["wE"] = np.concatenate([ktiles(a["L1_xattn_" + n].T) for n in ("w_q", "w_k", "w_v")] + [padded_out(a["L1_xattn_w_o"].T)], 1)
    d["bqE"] = a["L1_xattn_b_q"].reshape(2, P).T
    d["bkE"] = a["L1_xattn_b_k"].reshape(2, P).T
    d["bvE"], d["boE"] = a["L1_xattn_b_v"], a["L1_xattn_b_o"]
    lay_out_more(d, a, ktiles)
    return {n: np.ascontiguousarray(v) for n, v in d.items()}


def kernel(**inputs):
    import concourse.bacc as _bacc
    from concourse import mybir as _mybir
    from concourse.bass_utils import run_bass_kernel_spmd as _run

    nc = _bacc.Bacc("TRN2", target_bir_lowering=False, num_devices=1)
    arrays, io = {}, {}
    for name, a in lay_out(inputs).items():
        arrays[f"in_{name}"] = a
        io[name] = nc.dram_tensor(f"in_{name}", a.shape, _mybir.dt.from_np(a.dtype), kind="ExternalInput").ap()
    out = nc.dram_tensor("out_0", (B, S, DM), _mybir.dt.float32, kind="ExternalOutput").ap()
    decoder(nc, io, out, B)
    r = _run(nc, [arrays], core_ids=[0])
    return r.results[0]["out_0"]
```
